# Optimizing a Trainium2 kernel written in Bass

```python
import numpy as np
import jax
import jax.numpy as jnp

def _softmax(x, axis=-1):
    return jax.nn.softmax(x, axis=axis)

def _gelu(x):
    return jax.nn.gelu(x, approximate=True)

def _silu(x):
    return jax.nn.silu(x)

def _sigmoid(x):
    return jax.nn.sigmoid(x)

def _layernorm(x, axis=-1, eps=1e-05):
    m = jnp.mean(x, axis=axis, keepdims=True)
    v = jnp.var(x, axis=axis, keepdims=True)
    return (x - m) / jnp.sqrt(v + eps)

def _scatter_add(tgt, idx, src, axis=0):
    return tgt.at[idx].add(src)

def _segment_sum(src, seg, n):
    return jax.ops.segment_sum(src, seg, n)
kernel_name = 'mk_perceiver_d2_seqx_r8_9d4441'

def setup_inputs(seed: int=0):
    np.random.seed(seed)
    _w = jnp.asarray

    def _rec_inputs():
        import jax
        import jax.numpy as jnp
        _rk = jax.random.key(seed)
        x = 0.0002417 + 0.9998 * jax.random.normal(jax.random.fold_in(_rk, 1), (128, 32, 128), jnp.float32)
        _lenS = 32 - jax.random.randint(jax.random.fold_in(_rk, 7), (128,), 0, max(1, 32 // 4) + 1, jnp.int32)
        _lenS2 = 257 - jax.random.randint(jax.random.fold_in(_rk, 8), (128,), 0, max(1, 257 // 4) + 1, jnp.int32)
        _ctx_1024P = jax.random.normal(jax.random.fold_in(_rk, 11), (128, 16, 128), jnp.float32)
        _ctx_1024c = jax.random.dirichlet(jax.random.fold_in(_rk, 511), 0.3 * jnp.ones((16,), jnp.float32), (128, 257))
        _ctx_1024t = jnp.einsum('bsk,bkd->bsd', _ctx_1024c, _ctx_1024P)
        _ctx_1024t = _ctx_1024t * jax.lax.rsqrt(jnp.mean(jnp.square(_ctx_1024t)) + 1e-12) * 0.953939
        ctx_1024 = 7.22013e-05 + 1.00017 * (_ctx_1024t + 0.3 * jax.random.normal(jax.random.fold_in(_rk, 611), (128, 257, 128), jnp.float32))
        return (x, ctx_1024)
    x, ctx_1024 = _rec_inputs()

    def _L0_xattn_setup():
        import jax, jax.numpy as jnp
        import numpy as np
        D_MODEL = 128
        B, S = (4, 256)
        key = jax.random.key(seed)
        ks = jax.random.split(key, 10)
        s = 1.0 / np.sqrt(D_MODEL)
        return {'k': jax.random.normal(ks[0], (B, S, D_MODEL), jnp.float32), 'v': jax.random.normal(ks[1], (B, S, D_MODEL), jnp.float32), 'q': jax.random.normal(ks[2], (B, S, D_MODEL), jnp.float32), 'Wk': jax.random.normal(ks[3], (D_MODEL, D_MODEL), jnp.float32) * s, 'Wv': jax.random.normal(ks[4], (D_MODEL, D_MODEL), jnp.float32) * s, 'bv': jnp.zeros((D_MODEL,), jnp.float32), 'Wq': jax.random.normal(ks[5], (D_MODEL, D_MODEL), jnp.float32) * s, 'bq': jnp.zeros((D_MODEL,), jnp.float32), 'Wo': jax.random.normal(ks[6], (D_MODEL, D_MODEL), jnp.float32) * s, 'bo': jnp.zeros((D_MODEL,), jnp.float32)}
    _L0_xattn_all = _L0_xattn_setup()
    _L0_xattn_in = {k: v for k, v in _L0_xattn_all.items() if k in ('Wk', 'Wv', 'bv', 'Wq', 'bq', 'Wo', 'bo')}
    del _L0_xattn_all

    def _L0_attn_setup():
        import math
        import jax, jax.numpy as jnp
        import numpy as np
        B, S, D, H = (4, 128, 128, 16)
        HD = D // H
        EPS = 1e-05

        def _sinusoidal_encodings(length, d):
            pos = jnp.arange(length, dtype=jnp.float32)
            inv_freq = 1.0 / 10000.0 ** (jnp.arange(0.0, d, 2.0) / d)
            angles = pos[:, None] * inv_freq[None, :]
            enc = jnp.zeros((length, d), dtype=jnp.float32)
            enc = enc.at[:, 0::2].set(jnp.sin(angles))
            enc = enc.at[:, 1::2].set(jnp.cos(angles))
            return enc

        def _relative_shift(emb):
            b, h, l1, l2 = emb.shape
            padded = jnp.concatenate([jnp.zeros((b, h, l1, 1), emb.dtype), emb], axis=-1)
            padded = padded.reshape(b, h, l2 + 1, l1)
            return padded[:, :, 1:, :].reshape(b, h, l1, l2)
        key = jax.random.key(seed)
        ks = jax.random.split(key, 12)
        s = 0.02
        inp = {'x': jax.random.normal(ks[0], (B, S, D), dtype=jnp.float32), 'Wq': jax.random.normal(ks[1], (D, D), dtype=jnp.float32) * s, 'bq': jnp.zeros((D,), jnp.float32), 'Wk': jax.random.normal(ks[2], (D, D), dtype=jnp.float32) * s, 'bk': jnp.zeros((D,), jnp.float32), 'Wv': jax.random.normal(ks[3], (D, D), dtype=jnp.float32) * s, 'bv': jnp.zeros((D,), jnp.float32), 'Wpos': jax.random.normal(ks[4], (D, D), dtype=jnp.float32) * s, 'Wf': jax.random.normal(ks[5], (D, D), dtype=jnp.float32) * s, 'bf': jnp.zeros((D,), jnp.float32), 'u': jax.random.normal(ks[6], (H, HD), dtype=jnp.float32) * s, 'v': jax.random.normal(ks[7], (H, HD), dtype=jnp.float32) * s, 'gamma': jnp.ones((D,), jnp.float32), 'beta': jnp.zeros((D,), jnp.float32)}
        return inp
    _L0_attn_all = _L0_attn_setup()
    _L0_attn_in = {k: v for k, v in _L0_attn_all.items() if k in ('Wq', 'bq', 'Wk', 'bk', 'Wv', 'bv', 'Wpos', 'Wf', 'bf', 'u', 'v', 'gamma', 'beta')}
    del _L0_attn_all

    def _L0_ffn_setup():
        import jax, jax.numpy as jnp
        import numpy as np
        TOP_K = 2
        LN_EPS = 1e-05
        B, S, H, E, F = (2, 256, 128, 8, 512)

        def _layernorm(x, w, b):
            mu = jnp.mean(x, axis=-1, keepdims=True)
            var = jnp.mean(jnp.square(x - mu), axis=-1, keepdims=True)
            return (x - mu) * jax.lax.rsqrt(var + LN_EPS) * w + b
        key = jax.random.key(seed)
        ks = jax.random.split(key, 6)
        x = jax.random.normal(ks[0], (B, S, H), dtype=jnp.float32)
        Wg = jax.random.normal(ks[1], (H, E), dtype=jnp.float32) * 0.02
        alpha = jax.random.normal(ks[2], (E,), dtype=jnp.float32)
        ln_w = jnp.ones((E, H), dtype=jnp.float32)
        ln_b = jnp.zeros((E, H), dtype=jnp.float32)
        fc1_w = jax.random.normal(ks[3], (E, H, F), dtype=jnp.float32) * 0.02
        fc1_b = jnp.zeros((E, F), dtype=jnp.float32)
        fc2_w = jax.random.normal(ks[4], (E, F, H), dtype=jnp.float32) * 0.02
        fc2_b = jnp.zeros((E, H), dtype=jnp.float32)
        return {'x': x, 'Wg': Wg, 'alpha': alpha, 'ln_w': ln_w, 'ln_b': ln_b, 'fc1_w': fc1_w, 'fc1_b': fc1_b, 'fc2_w': fc2_w, 'fc2_b': fc2_b}
    _L0_ffn_all = _L0_ffn_setup()
    _L0_ffn_in = {k: v for k, v in _L0_ffn_all.items() if k in ('Wg', 'alpha', 'ln_w', 'ln_b', 'fc1_w', 'fc1_b', 'fc2_w', 'fc2_b')}
    del _L0_ffn_all

    def _L1_xattn_setup():
        import jax, jax.numpy as jnp
        import numpy as np
        K_DIM = 128
        HEADS = 16
        key = jax.random.key(seed)
        ks = jax.random.split(key, 8)
        b, t, tc, k = (2, 256, 256, K_DIM)
        scale = 1.0 / np.sqrt(k)
        x = jax.random.normal(ks[0], (b, t, k), dtype=jnp.float32)
        context = jax.random.normal(ks[1], (b, tc, k), dtype=jnp.float32)
        Wq = jax.random.normal(ks[2], (k, k), dtype=jnp.float32) * scale
        Wk = jax.random.normal(ks[3], (k, k), dtype=jnp.float32) * scale
        Wv = jax.random.normal(ks[4], (k, k), dtype=jnp.float32) * scale
        Wo = jax.random.normal(ks[5], (k, k), dtype=jnp.float32) * scale
        bo = jax.random.normal(ks[6], (k,), dtype=jnp.float32) * 0.01
        return {'x': x, 'context': context, 'Wq': Wq, 'Wk': Wk, 'Wv': Wv, 'Wo': Wo, 'bo': bo}
    _L1_xattn_all = _L1_xattn_setup()
    _L1_xattn_in = {k: v for k, v in _L1_xattn_all.items() if k in ('Wq', 'Wk', 'Wv', 'Wo', 'bo')}
    del _L1_xattn_all

    def _L1_attn_setup():
        import jax, jax.numpy as jnp
        import numpy as np
        D_MODEL = 128
        N_HEADS = 16
        KV_HEADS = 4
        D_HEAD = D_MODEL // N_HEADS
        EPS = 1.1920929e-07

        def _rope_factor(n, d_head):
            i = jnp.arange(d_head)
            theta = jnp.power(10000.0, -2.0 * (i // 2).astype(jnp.float32) / d_head)
            pos = jnp.arange(n, dtype=jnp.float32)
            ang = pos[:, None] * theta[None, :]
            cos = jnp.cos(ang)
            sin = jnp.sin(ang) * jnp.where(jnp.arange(n) % 2 == 0, -1.0, 1.0)[:, None]
            return cos + sin
        key = jax.random.key(seed)
        ks = jax.random.split(key, 6)
        b, n = (2, 256)
        s = 1.0 / np.sqrt(D_MODEL)
        return {'x': jax.random.normal(ks[0], (b, n, D_MODEL), dtype=jnp.float32), 'w_q': jax.random.normal(ks[1], (D_MODEL, D_MODEL), dtype=jnp.float32) * s, 'w_k': jax.random.normal(ks[2], (D_MODEL, KV_HEADS * D_HEAD), dtype=jnp.float32) * s, 'w_v': jax.random.normal(ks[3], (D_MODEL, KV_HEADS * D_HEAD), dtype=jnp.float32) * s, 'w_o': jax.random.normal(ks[4], (D_MODEL, D_MODEL), dtype=jnp.float32) * s, 'norm_w': jnp.ones((D_MODEL,), dtype=jnp.float32)}
    _L1_attn_all = _L1_attn_setup()
    _L1_attn_in = {k: v for k, v in _L1_attn_all.items() if k in ('w_q', 'w_k', 'w_v', 'w_o', 'norm_w')}
    del _L1_attn_all

    def _L1_ffn_setup():
        import jax, jax.numpy as jnp
        import numpy as np
        N_EXPERTS = 8
        TOP_K = 2
        key = jax.random.key(seed)
        k1, k2, k3, k4 = jax.random.split(key, 4)
        B, T, C, H, E = (2, 256, 128, 512, N_EXPERTS)
        x = jax.random.normal(k1, (B, T, C), dtype=jnp.float32)
        router_w = jax.random.normal(k2, (E, C), dtype=jnp.float32) * 0.02
        w1 = jax.random.normal(k3, (E, C, H), dtype=jnp.float32) * (1.0 / np.sqrt(C))
        w2 = jax.random.normal(k4, (E, H, C), dtype=jnp.float32) * (1.0 / np.sqrt(H))
        return {'x': x, 'router_w': router_w, 'w1': w1, 'w2': w2}
    _L1_ffn_all = _L1_ffn_setup()
    _L1_ffn_in = {k: v for k, v in _L1_ffn_all.items() if k in ('router_w', 'w1', 'w2')}
    del _L1_ffn_all
    return {'x': x, 'ctx_1024': ctx_1024, 'L0_xattn_Wk': _L0_xattn_in['Wk'], 'L0_xattn_Wv': _L0_xattn_in['Wv'], 'L0_xattn_bv': _L0_xattn_in['bv'], 'L0_xattn_Wq': _L0_xattn_in['Wq'], 'L0_xattn_bq': _L0_xattn_in['bq'], 'L0_xattn_Wo': _L0_xattn_in['Wo'], 'L0_xattn_bo': _L0_xattn_in['bo'], 'L0_attn_Wq': _L0_attn_in['Wq'], 'L0_attn_bq': _L0_attn_in['bq'], 'L0_attn_Wk': _L0_attn_in['Wk'], 'L0_attn_bk': _L0_attn_in['bk'], 'L0_attn_Wv': _L0_attn_in['Wv'], 'L0_attn_bv': _L0_attn_in['bv'], 'L0_attn_Wpos': _L0_attn_in['Wpos'], 'L0_attn_Wf': _L0_attn_in['Wf'], 'L0_attn_bf': _L0_attn_in['bf'], 'L0_attn_u': _L0_attn_in['u'], 'L0_attn_v': _L0_attn_in['v'], 'L0_attn_gamma': _L0_attn_in['gamma'], 'L0_attn_beta': _L0_attn_in['beta'], 'L0_ffn_Wg': _L0_ffn_in['Wg'], 'L0_ffn_alpha': _L0_ffn_in['alpha'], 'L0_ffn_ln_w': _L0_ffn_in['ln_w'], 'L0_ffn_ln_b': _L0_ffn_in['ln_b'], 'L0_ffn_fc1_w': _L0_ffn_in['fc1_w'], 'L0_ffn_fc1_b': _L0_ffn_in['fc1_b'], 'L0_ffn_fc2_w': _L0_ffn_in['fc2_w'], 'L0_ffn_fc2_b': _L0_ffn_in['fc2_b'], 'L1_xattn_Wq': _L1_xattn_in['Wq'], 'L1_xattn_Wk': _L1_xattn_in['Wk'], 'L1_xattn_Wv': _L1_xattn_in['Wv'], 'L1_xattn_Wo': _L1_xattn_in['Wo'], 'L1_xattn_bo': _L1_xattn_in['bo'], 'L1_attn_w_q': _L1_attn_in['w_q'], 'L1_attn_w_k': _L1_attn_in['w_k'], 'L1_attn_w_v': _L1_attn_in['w_v'], 'L1_attn_w_o': _L1_attn_in['w_o'], 'L1_attn_norm_w': _L1_attn_in['norm_w'], 'L1_ffn_router_w': _L1_ffn_in['router_w'], 'L1_ffn_w1': _L1_ffn_in['w1'], 'L1_ffn_w2': _L1_ffn_in['w2']}

def reference(x, ctx_1024, L0_xattn_Wk, L0_xattn_Wv, L0_xattn_bv, L0_xattn_Wq, L0_xattn_bq, L0_xattn_Wo, L0_xattn_bo, L0_attn_Wq, L0_attn_bq, L0_attn_Wk, L0_attn_bk, L0_attn_Wv, L0_attn_bv, L0_attn_Wpos, L0_attn_Wf, L0_attn_bf, L0_attn_u, L0_attn_v, L0_attn_gamma, L0_attn_beta, L0_ffn_Wg, L0_ffn_alpha, L0_ffn_ln_w, L0_ffn_ln_b, L0_ffn_fc1_w, L0_ffn_fc1_b, L0_ffn_fc2_w, L0_ffn_fc2_b, L1_xattn_Wq, L1_xattn_Wk, L1_xattn_Wv, L1_xattn_Wo, L1_xattn_bo, L1_attn_w_q, L1_attn_w_k, L1_attn_w_v, L1_attn_w_o, L1_attn_norm_w, L1_ffn_router_w, L1_ffn_w1, L1_ffn_w2):
    import jax
    import jax.numpy as jnp

    def _L0_xattn_ref(k, v, q, Wk, Wv, bv, Wq, bq, Wo, bo):
        import jax, jax.numpy as jnp
        import numpy as np
        D_MODEL = 128
        B, S = (4, 256)
        kp = jnp.einsum('bsd,ed->bse', k, Wk)
        vp = jnp.einsum('bsd,ed->bse', v, Wv) + bv
        qp = jnp.einsum('bsd,ed->bse', q, Wq) + bq
        scale = 1.0 / jnp.sqrt(jnp.float32(kp.shape[-1]))
        scores = jnp.einsum('bqd,bkd->bqk', qp, kp) * scale
        probs = jax.nn.softmax(scores, axis=-1)
        ctx = jnp.einsum('bqk,bkd->bqd', probs, vp)
        return jnp.einsum('bqd,ed->bqe', ctx, Wo) + bo

    def _L0_attn_ref(x, Wq, bq, Wk, bk, Wv, bv, Wpos, Wf, bf, u, v, gamma, beta):
        import math
        import jax, jax.numpy as jnp
        import numpy as np
        B, S, D, H = (4, 128, 128, 16)
        HD = D // H
        EPS = 1e-05

        def _sinusoidal_encodings(length, d):
            pos = jnp.arange(length, dtype=jnp.float32)
            inv_freq = 1.0 / 10000.0 ** (jnp.arange(0.0, d, 2.0) / d)
            angles = pos[:, None] * inv_freq[None, :]
            enc = jnp.zeros((length, d), dtype=jnp.float32)
            enc = enc.at[:, 0::2].set(jnp.sin(angles))
            enc = enc.at[:, 1::2].set(jnp.cos(angles))
            return enc

        def _relative_shift(emb):
            b, h, l1, l2 = emb.shape
            padded = jnp.concatenate([jnp.zeros((b, h, l1, 1), emb.dtype), emb], axis=-1)
            padded = padded.reshape(b, h, l2 + 1, l1)
            return padded[:, :, 1:, :].reshape(b, h, l1, l2)
        b, s, d = x.shape
        mu = jnp.mean(x, axis=-1, keepdims=True)
        var = jnp.mean((x - mu) ** 2, axis=-1, keepdims=True)
        xn = (x - mu) * jax.lax.rsqrt(var + EPS) * gamma + beta
        pe = _sinusoidal_encodings(s, d)
        q = (xn @ Wq + bq).reshape(b, s, H, HD)
        k = (xn @ Wk + bk).reshape(b, s, H, HD)
        val = (xn @ Wv + bv).reshape(b, s, H, HD)
        p = (pe @ Wpos).reshape(s, H, HD)
        AC = jnp.einsum('bihd,bjhd->bhij', q + u, k)
        BD = jnp.einsum('bihd,jhd->bhij', q + v, p)
        BD = _relative_shift(BD)
        attn = jax.nn.softmax((AC + BD) / math.sqrt(d), axis=-1)
        out = jnp.einsum('bhij,bjhd->bihd', attn, val).reshape(b, s, d)
        out = out @ Wf + bf
        return out

    def _L0_ffn_ref(x, Wg, alpha, ln_w, ln_b, fc1_w, fc1_b, fc2_w, fc2_b):
        import jax, jax.numpy as jnp
        import numpy as np
        TOP_K = 2
        LN_EPS = 1e-05
        B, S, H, E, F = (2, 256, 128, 8, 512)

        def _layernorm(x, w, b):
            mu = jnp.mean(x, axis=-1, keepdims=True)
            var = jnp.mean(jnp.square(x - mu), axis=-1, keepdims=True)
            return (x - mu) * jax.lax.rsqrt(var + LN_EPS) * w + b
        b, s, h = x.shape
        xf = x.reshape(-1, h)
        logits = xf @ Wg
        top_vals, top_idx = jax.lax.top_k(logits, TOP_K)
        gate_score = jax.nn.softmax(top_vals, axis=-1)
        one_hot = jax.nn.one_hot(top_idx, Wg.shape[1], dtype=xf.dtype)
        comb = jnp.einsum('tke,tk->te', one_hot, gate_score) * alpha
        out = jnp.zeros_like(xf)
        for e in range(Wg.shape[1]):
            hdn = _layernorm(xf, ln_w[e], ln_b[e])
            a = jax.nn.gelu(hdn @ fc1_w[e] + fc1_b[e], approximate=True)
            y = a @ fc2_w[e] + fc2_b[e]
            out = out + y * comb[:, e:e + 1]
        return out.reshape(b, s, h)

    def _L1_xattn_ref(x, context, Wq, Wk, Wv, Wo, bo):
        import jax, jax.numpy as jnp
        import numpy as np
        K_DIM = 128
        HEADS = 16
        b, t, e = x.shape
        tc = context.shape[1]
        h = HEADS
        s = e // h
        q = (x @ Wq.T).reshape(b, t, h, s)
        k_ = (context @ Wk.T).reshape(b, tc, h, s)
        v = (context @ Wv.T).reshape(b, tc, h, s)
        inv4 = e ** (-0.25)
        q = q * inv4
        k_ = k_ * inv4
        dot = jnp.einsum('bthd,bchd->bhtc', q, k_)
        attn = jax.nn.softmax(dot, axis=-1)
        out = jnp.einsum('bhtc,bchd->bthd', attn, v).reshape(b, t, e)
        return out @ Wo.T + bo

    def _L1_attn_ref(x, w_q, w_k, w_v, w_o, norm_w):
        import jax, jax.numpy as jnp
        import numpy as np
        D_MODEL = 128
        N_HEADS = 16
        KV_HEADS = 4
        D_HEAD = D_MODEL // N_HEADS
        EPS = 1.1920929e-07

        def _rope_factor(n, d_head):
            i = jnp.arange(d_head)
            theta = jnp.power(10000.0, -2.0 * (i // 2).astype(jnp.float32) / d_head)
            pos = jnp.arange(n, dtype=jnp.float32)
            ang = pos[:, None] * theta[None, :]
            cos = jnp.cos(ang)
            sin = jnp.sin(ang) * jnp.where(jnp.arange(n) % 2 == 0, -1.0, 1.0)[:, None]
            return cos + sin
        b, n, d = x.shape
        reps = N_HEADS // KV_HEADS
        scale = jnp.float32(np.sqrt(D_HEAD))
        xn = x * jax.lax.rsqrt(jnp.mean(x * x, axis=-1, keepdims=True) + EPS) * norm_w
        q = (xn @ w_q).reshape(b, n, N_HEADS, D_HEAD).transpose(0, 2, 1, 3)
        k = (xn @ w_k).reshape(b, n, KV_HEADS, D_HEAD).transpose(0, 2, 1, 3)
        v = (xn @ w_v).reshape(b, n, KV_HEADS, D_HEAD).transpose(0, 2, 1, 3)
        rf = _rope_factor(n, D_HEAD)
        q = q * rf
        k = k * rf
        q5 = q.reshape(b, reps, KV_HEADS, n, D_HEAD)
        scores = jnp.einsum('brknd,bkmd->brknm', q5, k) / scale
        causal = jnp.tril(jnp.ones((n, n), dtype=bool))
        scores = jnp.where(causal, scores, jnp.float32(-jnp.inf))
        p = jax.nn.softmax(scores, axis=-1)
        s = jnp.einsum('brknm,bkmd->brknd', p, v)
        s = s.reshape(b, N_HEADS, n, D_HEAD).transpose(0, 2, 1, 3).reshape(b, n, d)
        return x + s @ w_o

    def _L1_ffn_ref(x, router_w, w1, w2):
        import jax, jax.numpy as jnp
        import numpy as np
        N_EXPERTS = 8
        TOP_K = 2
        B, T, C = x.shape
        E = N_EXPERTS
        xf = x.reshape(-1, C)
        logits = jnp.einsum('nc,ec->ne', xf, router_w)
        probs = jax.nn.softmax(logits, axis=-1)
        top_w, top_i = jax.lax.top_k(probs, TOP_K)
        top_w = top_w / jnp.sum(top_w, axis=-1, keepdims=True)
        comb = jnp.einsum('nk,nke->ne', top_w, jax.nn.one_hot(top_i, E, dtype=xf.dtype))
        h = jax.nn.gelu(jnp.einsum('nc,ech->enh', xf, w1), approximate=False)
        y = jnp.einsum('enh,ehc->enc', h, w2)
        out = jnp.einsum('ne,enc->nc', comb, y)
        return out.reshape(B, T, C)
    x = x + _L0_xattn_ref(ctx_1024, ctx_1024, _layernorm(x, axis=-1), L0_xattn_Wk, L0_xattn_Wv, L0_xattn_bv, L0_xattn_Wq, L0_xattn_bq, L0_xattn_Wo, L0_xattn_bo)
    x = x + _L0_attn_ref(_layernorm(x, axis=-1), L0_attn_Wq, L0_attn_bq, L0_attn_Wk, L0_attn_bk, L0_attn_Wv, L0_attn_bv, L0_attn_Wpos, L0_attn_Wf, L0_attn_bf, L0_attn_u, L0_attn_v, L0_attn_gamma, L0_attn_beta)
    x = x + _L0_ffn_ref(_layernorm(x, axis=-1), L0_ffn_Wg, L0_ffn_alpha, L0_ffn_ln_w, L0_ffn_ln_b, L0_ffn_fc1_w, L0_ffn_fc1_b, L0_ffn_fc2_w, L0_ffn_fc2_b)
    x = x + _L1_xattn_ref(_layernorm(x, axis=-1), ctx_1024, L1_xattn_Wq, L1_xattn_Wk, L1_xattn_Wv, L1_xattn_Wo, L1_xattn_bo)
    x = x + _L1_attn_ref(_layernorm(x, axis=-1), L1_attn_w_q, L1_attn_w_k, L1_attn_w_v, L1_attn_w_o, L1_attn_norm_w)
    x = x + _L1_ffn_ref(_layernorm(x, axis=-1), L1_ffn_router_w, L1_ffn_w1, L1_ffn_w2)
    return x

_drawn_inputs = setup_inputs


def setup_inputs(seed=0):
    import zlib

    import numpy as np

    out = dict(_drawn_inputs(seed))
    spreads = {'L0_xattn_bv': (0.0, 0.1),
     'L0_xattn_bq': (0.0, 0.1),
     'L0_xattn_bo': (0.0, 0.1),
     'L0_attn_bq': (0.0, 2.0),
     'L0_attn_bk': (0.0, 2.0),
     'L0_attn_bv': (0.0, 0.1),
     'L0_attn_bf': (0.0, 0.1),
     'L0_attn_gamma': (1.0, 0.6),
     'L0_attn_beta': (0.0, 0.506),
     'L0_ffn_ln_w': (1.0, 0.6),
     'L0_ffn_ln_b': (0.0, 0.8),
     'L0_ffn_fc1_b': (0.0, 0.349),
     'L0_ffn_fc2_b': (0.0, 0.1),
     'L1_attn_norm_w': (1.0, 0.2)}
    factors = {'L0_attn_Wq': 8.0,
     'L0_attn_Wk': 8.0,
     'L0_attn_Wpos': 8.0,
     'L0_attn_u': 55.317,
     'L0_attn_v': 200.0,
     'L1_xattn_bo': 2.72}
    for name, (base, spread) in spreads.items():
        noise = np.random.default_rng([zlib.crc32(name.encode()), seed]).standard_normal(out[name].shape)
        drawn = base * np.exp(spread * noise) if base else spread * noise
        out[name] = jnp.asarray(drawn.astype(out[name].dtype))
    for name, factor in factors.items():
        out[name] = (out[name] * factor).astype(out[name].dtype)
    return out
```

```python
from contextlib import ExitStack

import numpy as np

import concourse.bass as bass
from concourse import mybir
from concourse.alu_op_type import AluOpType as ALU

F32 = mybir.dt.float32
I32 = mybir.dt.int32
U32 = mybir.dt.uint32
ACT = mybir.ActivationFunctionType
AX = mybir.AxisListType
DS = bass.ds

P = 128
D = 128
SEQS, LEN = 128, 32
CTX = 257
B4 = P // LEN
TILES = SEQS // B4
HALF = TILES // 2
H, HD = 16, 8
G, H4 = 4, 4
KC = 86
CHUNKS = ((0, 86), (86, 86), (172, 85))
E, F, FC = 8, 512, 4
LN_EPS = 1e-5
RMS_EPS = 1.1920929e-07
MASKED = -1.0e30

C_ID, C_M16, C_M4G, C_M4P, C_R4 = 0, 128, 144, 148, 152
C_CAUSAL, C_ROPE, C_PE, C_IOTA = 184, 216, 248, 280
C_TRI, C_ONES = 288, 416
C_TILE = 544
C_POW, C_Z, C_LN, C_RMS = 616, 617, 619, 621
C_ALL = 623


def shape_constants():
    c = np.zeros((P, C_ALL), np.float32)
    p = np.arange(P)
    c[:, C_ID:C_ID + P] = np.eye(P)
    c[p, C_M16 + p // HD] = 1.0
    c[p, C_M4G + (p // HD) % H4] = 1.0
    c[p, C_M4P + p // LEN] = 1.0
    c[p, C_R4 + p % LEN] = 1.0
    i, j = p[:, None] % LEN, np.arange(LEN)[None, :]
    c[:, C_CAUSAL:C_CAUSAL + LEN] = np.where(j <= i, 0.0, MASKED)
    d = np.arange(HD)
    theta = np.power(np.float32(10000.0), (-2.0 * (d // 2) / HD).astype(np.float32)).astype(np.float32)
    ang = np.arange(LEN, dtype=np.float32)[:, None] * theta[None, :]
    sign = np.where(np.arange(LEN) % 2 == 0, -1.0, 1.0)[:, None]
    rope = (np.cos(ang) + np.sin(ang) * sign).astype(np.float32)
    c[:, C_ROPE:C_ROPE + LEN] = rope.T[p % HD]
    inv = (1.0 / 10000.0 ** (np.arange(0.0, D, 2.0) / D)).astype(np.float32)
    pa = np.arange(LEN, dtype=np.float32)[:, None] * inv[None, :]
    pe = np.zeros((LEN, D), np.float32)
    pe[:, 0::2], pe[:, 1::2] = np.sin(pa), np.cos(pa)
    c[:, C_PE:C_PE + LEN] = pe.T
    c[:, C_IOTA:C_IOTA + E] = np.arange(E)
    c[:, C_TRI:C_TRI + P] = (p[:, None] < p[None, :])
    c[:, C_ONES:C_ONES + P] = 1.0
    c[:, C_TILE:C_TILE + 72] = np.arange(72)
    c[:, C_POW] = -0.5
    c[:, C_Z:C_Z + 2] = 1.0, LN_EPS
    c[:, C_LN:C_LN + 2] = 1.0 + LN_EPS, LN_EPS * LN_EPS
    c[:, C_RMS:C_RMS + 2] = 1.0 + RMS_EPS, RMS_EPS * LN_EPS
    return c



class Tile:

    def __init__(self, step, p, stage):
        self.half, self.par = step + (p - stage) // 2, (p - stage) % 2
        self.known = isinstance(step, int)
        self.live = not self.known or 0 <= self.half < HALF

    @property
    def n(self):
        return self.half * 2 + self.par

    def cols(self, width=P):
        return DS(self.n * width, width) if not self.known else slice(self.n * width, (self.n + 1) * width)

    def nth(self, each=1):
        return (self.n + 1) * each

    def nth_of_pair(self, each=1):
        return (self.half + 1) * each

    def past(self, back=1):
        return not self.known or self.n >= back

    def unit(self, u, back=0, each=16):
        return self.n * each + u + 1 - back

    def past_unit(self, u, back, each=16):
        return not self.known or self.n * each + u >= back

    def before(self, back=1, each=1):
        return (self.n + 1 - back) * each


def over_tiles(eng, stages, work):
    first = (stages + 3) // 2
    for step in range(first):
        for p in range(2):
            work(lambda s, a=step, b=p: Tile(a, b, s))
    with eng.Fori(first, HALF) as step:
        for p in range(2):
            work(lambda s, a=step, b=p: Tile(a, b, s))
    for step in range(HALF, HALF + (stages + 1) // 2):
        for p in range(2):
            work(lambda s, a=step, b=p: Tile(a, b, s))



class Tail:

    def __init__(self, m, name, forms):
        self.m, self.forms = m, forms
        self.x_new = m.sem(name + "_x_new")
        self.stats_done = m.sem(name + "_stats_done")
        self.mv_ready = m.sem(name + "_mv_ready")
        self.pool_step = m.sem(name + "_norm_step")
        self.steps = 1 + 3 * len(forms)

    def dve(self, dve, t):
        m, nc = self.m, self.m.nc
        dve.wait_ge(self.x_new, t.nth())
        nc.vector.memset(m.gate[:, 0:1], 0.0)
        nc.vector.bn_stats(m.bnst[:, t.par, :], m.X[:, t.cols()]).then_inc(self.stats_done, 1)
        dve.wait_ge(self.stats_done, t.nth())
        if t.past(2):
            dve.wait_ge(self.pool_step, t.before(2, self.steps))
        nc.vector.memset(m.gate[:, 1:2], 0.0)
        nc.vector.bn_aggr(m.mv[:, t.par, :], m.bnst[:, t.par, :]).then_inc(self.mv_ready, 1)

    def pool(self, pool, t):
        m, nc = self.m, self.m.nc
        pool.wait_ge(self.mv_ready, t.nth())
        step = t.before(1, self.steps)
        if t.past():
            pool.wait_ge(self.pool_step, step)
        mv = m.mv[:, t.par, :]
        for out, a, b in self.forms:
            r = m.rstd[:, 0:1]
            for n, (dst, x, y, op) in enumerate(((r, mv[:, 1:2], a, ALU.mult), (r, r, b, ALU.add),
                                                 (out[:, t.cols(1)], r, C_POW, ALU.pow))):
                nc.gpsimd.tensor_tensor(dst, x, m.const[:, y:y + 1], op).then_inc(self.pool_step, 1)
                step = step + 1
                pool.wait_ge(self.pool_step, step)
        nc.gpsimd.tensor_tensor(m.MEAN[:, t.cols(1)], mv[:, 0:1], m.const[:, C_ONES:C_ONES + 1],
                                ALU.mult).then_inc(self.pool_step, 1)


def normed(m, out, t, factor):
    return m.nc.vector.tensor_scalar(out, m.X[:, t.cols()], m.MEAN[:, t.cols(1)], factor[:, t.cols(1)],
                                     ALU.subtract, ALU.mult)


class Chip:
    pass


def sinks(m, which):
    return {"z": (m.RZ, C_Z, C_Z + 1), "ln": (m.RN, C_LN, C_LN + 1), "rms": (m.RN, C_RMS, C_RMS + 1)}[which]


def setup_pass(m):
    nc = m.nc
    loaded = m.sem("weights_loaded")
    x_in = [m.sem("x_in_a"), m.sem("x_in_b")]
    folded = m.sem("folded")
    evac = m.sem("fold_evacuated")
    zeroed = m.sem("setup_zeroed")
    tail = Tail(m, "setup", [sinks(m, "z")])
    loads = m.setup_loads
    c = m.const
    ones_row = c[0:1, C_ONES:C_ONES + P]
    ws = m.w

    with nc.Block() as block:
        @block.sync
        def _(sp):
            for n in range(2):
                sp.dma_start(m.X[:, n * 2048:(n + 1) * 2048].rearrange("p (t d) -> p t d", d=D),
                             m.x_dram[n * 16:(n + 1) * 16].rearrange("t p d -> p t d")).then_inc(x_in[n], 16)
            for dst, src in loads:
                sp.dma_start(dst, src).then_inc(loaded, 16)

        @block.tensor
        def _(pe):
            pe.wait_ge(loaded, 16 * len(loads))
            mm = nc.tensor.matmul
            one = dict(start=True, stop=True)
            mm(m.ps[0][:, 0:D], ws["Wq0"][:, :], ws["Wk0"][:, :], **one)
            mm(m.ps[0][:, D:D + 1], ws["Wk0"][:, :], m.cols[:, m.c_bq0:m.c_bq0 + 1], **one)
            mm(m.ps[1][:, 0:D], ws["Wv0"][:, :], ws["Wo0T"][:, :], **one).then_inc(folded, 1)
            bias = [("bv0", "Wo0T", 0), ("bv_a", "Wf", 1), (None, None, 2)]
            for n, (vec, wt, row) in enumerate(bias):
                dst = m.ps[2 + n][:, 0:D]
                if vec:
                    k = m.colidx[vec]
                    mm(dst, m.cols[:, k:k + 1].broadcast_to([D, P]), ws[wt][:, :], start=True, stop=False)
                mm(dst, ones_row, m.rows[0:1, row * D:(row + 1) * D], start=not vec, stop=True).then_inc(folded, 1)
            mm(m.ps[5][:, 0:LEN], ws["Wpos"][:, :], c[:, C_PE:C_PE + LEN], **one).then_inc(folded, 1)

        @block.vector
        def _(dve):
            nc.vector.memset(m.ptab[:, :, :], 0.0).then_inc(zeroed, 1)
            for half in range(2):
                dve.wait_ge(x_in[half], 16)
                for n in range(16 * half, 16 * half + 16):
                    t = Tile(n // 2, n % 2, 0)
                    nc.vector.memset(m.gate[:, 2:3], 0.0).then_inc(tail.x_new, 1)
                    tail.dve(dve, t)
            dve.wait_ge(folded, 5)
            dve.wait_ge(zeroed, 1)
            s0 = float(D) ** -0.5
            nc.vector.tensor_scalar(m.M0[:, :], m.ps[0][:, 0:D], 1.0, None, ALU.mult).then_inc(evac, 1)
            nc.vector.tensor_scalar(m.c0[:, :], m.ps[0][:, D:D + 1], s0, None, ALU.mult).then_inc(evac, 1)
            nc.vector.tensor_copy(m.N0[:, :], m.ps[1][:, 0:D]).then_inc(evac, 1)
            for n, dst in enumerate((m.b0, m.bA, m.bX)):
                nc.vector.tensor_copy(dst[:, :], m.ps[2 + n][:, 0:D]).then_inc(evac, 1)
            nc.vector.tensor_tensor(
                m.ptab[:, :, 1:1 + LEN],
                m.ps[5][:, 0:LEN].unsqueeze(1).broadcast_to([P, H, LEN]),
                c[:, C_M16:C_M16 + H].unsqueeze(2).broadcast_to([P, H, LEN]), ALU.mult).then_inc(evac, 1)
            for k, (a, b) in enumerate(((m.colidx["bq_a"], m.colidx["u"]), (m.colidx["bq_a"], m.colidx["v"]))):
                nc.vector.tensor_tensor(m.bqu[:, k:k + 1], m.cols[:, a:a + 1], m.cols[:, b:b + 1],
                                        ALU.add).then_inc(evac, 1)

        @block.gpsimd
        def _(pool):
            pool.wait_ge(loaded, 16 * len(loads))
            for n in range(TILES):
                tail.pool(pool, Tile(n // 2, n % 2, 0))


def cross_one_head(m):
    nc = m.nc
    ctx_in = [m.sem("p1_ctx_in_a"), m.sem("p1_ctx_in_b")]
    rows_in = [m.sem("p1_rows_in_a"), m.sem("p1_rows_in_b")]
    s = {n: m.sem("p1_" + n) for n in (
        "zT_ps", "zT", "q_ps", "q", "scores", "maxed", "probs", "pT_ps", "pT", "o_ps", "o", "oT_ps", "oT", "y_ps",
        "recip", "xb", "z")}
    tail = Tail(m, "p1", [sinks(m, "ln")])
    ident = m.const[:, C_ID:C_ID + P]
    ps = m.ps
    s0 = float(D) ** -0.5
    with ExitStack() as own, nc.Block() as block:
        sb = lambda n, shape: own.enter_context(nc.sbuf_tensor("p1_" + n, shape, F32))
        ctxT = sb("ctxT", [P, 2, B4, CTX])
        ctxN = sb("ctxN", [KC, 2, B4, 3, D])
        z, o, zT, qT, oT = sb("z", [P, 2, D]), sb("o", [P, 2, D]), sb("zT", [P, 2, P]), sb("qT", [P, 2, P]), sb("oT", [P, 2, P])
        prob = sb("prob", [P, 2, CTX])
        pT = sb("pT", [KC, 2, 3, P])
        xb = sb("xb", [P, 2, D])
        nmax, total, recip = sb("nmax", [P, 2]), sb("total", [P, 4]), sb("recip", [P, 2])
        STAGES = 6

        @block.sync
        def _(sp):
            def work(at):
                t = at(2)
                if t.live:
                    if t.past(2):
                        sp.wait_ge(s["o_ps"], t.before(2))
                    sp.dma_start(ctxN[:, t.par], m.ctxN_dram[DS(t.n, 1)].rearrange(
                        "a p (b c d) -> p (a b) c d", b=B4, c=3)).then_inc(rows_in[t.par], 16)
                t = at(0)
                if t.live:
                    if t.past(2):
                        sp.wait_ge(s["scores"], t.before(2))
                    sp.dma_start(ctxT[:, t.par], m.ctxT_dram[:, t.cols(B4 * CTX)].rearrange(
                        "d (b k) -> d b k", k=CTX)).then_inc(ctx_in[t.par], 16)
            over_tiles(sp, 2, work)

        @block.tensor
        def _(pe):
            def work(at):
                t = at(2)
                if t.live:
                    pe.wait_ge(s["q"], t.nth())
                    pe.wait_ge(ctx_in[t.par], t.nth_of_pair(16))
                    if t.past(2):
                        pe.wait_ge(s["probs"], t.before(2))
                    for b in range(B4):
                        last = nc.tensor.matmul(ps[3 + t.par][b * LEN:(b + 1) * LEN, 0:CTX],
                                                qT[:, t.par, b * LEN:(b + 1) * LEN], ctxT[:, t.par, b, :],
                                                start=True, stop=True, tile_position=(0, b * LEN))
                    last.then_inc(s["scores"], 1)
                t = at(3)
                if t.live:
                    pe.wait_ge(s["probs"], t.nth())
                    if t.past():
                        pe.wait_ge(s["pT"], t.before())
                    for c, (k0, rows) in enumerate(CHUNKS):
                        last = nc.tensor.transpose(ps[5][:rows, c * P:(c + 1) * P], prob[:, t.par, k0:k0 + rows], ident)
                    last.then_inc(s["pT_ps"], 1)
                t = at(1)
                if t.live:
                    pe.wait_ge(s["zT"], t.nth())
                    if t.past():
                        pe.wait_ge(s["q"], t.before())
                    nc.tensor.matmul(ps[2][:, 0:P], m.M0[:, :], zT[:, t.par, :], start=True, stop=True).then_inc(s["q_ps"], 1)
                t = at(0)
                if t.live:
                    pe.wait_ge(s["z"], t.nth())
                    if t.past():
                        pe.wait_ge(s["zT"], t.before())
                    nc.tensor.transpose(ps[0][:, 0:P], z[:, t.par, :], ident).then_inc(s["zT_ps"], 1)
                t = at(6)
                if t.live:
                    pe.wait_ge(s["oT"], t.nth())
                    if t.past():
                        pe.wait_ge(tail.x_new, t.before())
                    nc.tensor.matmul(ps[7][:, 0:D], oT[:, t.par, :], m.N0[:, :], start=True, stop=True).then_inc(s["y_ps"], 1)
                t = at(5)
                if t.live:
                    pe.wait_ge(s["o"], t.nth())
                    if t.past():
                        pe.wait_ge(s["oT"], t.before())
                    nc.tensor.transpose(ps[1][:, 0:P], o[:, t.par, :], ident).then_inc(s["oT_ps"], 1)
                t = at(4)
                if t.live:
                    pe.wait_ge(s["pT"], t.nth())
                    pe.wait_ge(rows_in[t.par], t.nth_of_pair(16))
                    if t.past():
                        pe.wait_ge(s["o"], t.before())
                    for c, (_, rows) in enumerate(CHUNKS):
                        for b in range(B4):
                            last = nc.tensor.matmul(ps[6][b * LEN:(b + 1) * LEN, 0:D],
                                                    pT[:rows, t.par, c, b * LEN:(b + 1) * LEN],
                                                    ctxN[:rows, t.par, b, c, :], start=(c == 0), stop=(c == 2),
                                                    tile_position=(0, b * LEN))
                    last.then_inc(s["o_ps"], 1)
            over_tiles(pe, STAGES, work)

        @block.scalar
        def _(act):
            def work(at):
                t = at(2)
                if t.live:
                    act.wait_ge(s["maxed"], t.nth())
                    if t.past(2):
                        act.wait_ge(s["pT_ps"], t.before(2))
                        act.wait_ge(s["recip"], t.before(2))
                    nc.scalar.activation(prob[:, t.par, :], ps[3 + t.par][:, 0:CTX], ACT.Exp,
                                         bias=nmax[:, t.par:t.par + 1],
                                         accum_out=total[:, t.par:t.par + 1]).then_inc(s["probs"], 1)
                t = at(1)
                if t.live:
                    act.wait_ge(s["q_ps"], t.nth())
                    if t.past(2):
                        act.wait_ge(s["scores"], t.before(2))
                    nc.scalar.activation(qT[:, t.par, :], ps[2][:, 0:P], ACT.Identity, scale=s0,
                                         bias=m.c0[:, 0:1]).then_inc(s["q"], 1)
                t = at(0)
                if t.live:
                    act.wait_ge(s["zT_ps"], t.nth())
                    if t.past(2):
                        act.wait_ge(s["q_ps"], t.before(2))
                    nc.scalar.activation(zT[:, t.par, :], ps[0][:, 0:P], ACT.Copy).then_inc(s["zT"], 1)
                t = at(5)
                if t.live:
                    act.wait_ge(s["oT_ps"], t.nth())
                    if t.past(2):
                        act.wait_ge(s["y_ps"], t.before(2))
                    nc.scalar.activation(oT[:, t.par, :], ps[1][:, 0:P], ACT.Copy).then_inc(s["oT"], 1)
                t = at(4)
                if t.live:
                    act.wait_ge(s["o_ps"], t.nth())
                    act.wait_ge(s["recip"], t.nth())
                    if t.past(2):
                        act.wait_ge(s["oT_ps"], t.before(2))
                    nc.scalar.activation(o[:, t.par, :], ps[6][:, 0:D], ACT.Copy,
                                         scale=recip[:, t.par:t.par + 1]).then_inc(s["o"], 1)
            over_tiles(act, STAGES, work)

        @block.vector
        def _(dve):
            def work(at):
                t = at(2)
                if t.live:
                    dve.wait_ge(s["scores"], t.nth())
                    if t.past(2):
                        dve.wait_ge(s["probs"], t.before(2))
                    nc.vector.tensor_reduce(nmax[:, t.par:t.par + 1], ps[3 + t.par][:, 0:CTX], AX.X, ALU.max,
                                            negate=True).then_inc(s["maxed"], 1)
                t = at(3)
                if t.live:
                    dve.wait_ge(s["pT_ps"], t.nth())
                    if t.past(2):
                        dve.wait_ge(s["o_ps"], t.before(2))
                    nc.vector.tensor_copy(pT[:85, t.par, 2, :], ps[5][:85, 2 * P:3 * P])
                    nc.vector.tensor_copy(pT[:KC, t.par, 0:2, :], ps[5][:KC, 0:2 * P]).then_inc(s["pT"], 1)
                    if t.past(2):
                        dve.wait_ge(s["o"], t.before(2))
                    nc.vector.reciprocal(recip[:, t.par:t.par + 1], total[:, t.par:t.par + 1]).then_inc(s["recip"], 1)
                t = at(0)
                if t.live:
                    if t.past(2):
                        dve.wait_ge(s["zT_ps"], t.before(2))
                    normed(m, z[:, t.par, :], t, m.RZ).then_inc(s["z"], 1)
                t = at(6)
                if t.live:
                    dve.wait_ge(s["y_ps"], t.nth())
                    dve.wait_ge(s["xb"], t.nth())
                    nc.vector.tensor_tensor(m.X[:, t.cols()], ps[7][:, 0:D], xb[:, t.par, :],
                                            ALU.add).then_inc(tail.x_new, 1)
                    tail.dve(dve, t)
            over_tiles(dve, STAGES, work)

        @block.gpsimd
        def _(pool):
            def work(at):
                t = at(4)
                if t.live:
                    if t.past(2):
                        pool.wait_ge(tail.x_new, t.before(2))
                    nc.gpsimd.tensor_tensor(xb[:, t.par, :], m.X[:, t.cols()], m.b0[:, :], ALU.add).then_inc(s["xb"], 1)
                t = at(6)
                if t.live:
                    tail.pool(pool, t)
            over_tiles(pool, STAGES, work)


def relative_project(m):
    nc, ps = m.nc, m.ps
    s = {n: m.sem("p2_" + n) for n in ("z", "zT_ps", "zT", "q_ps", "q")}
    ident = m.const[:, C_ID:C_ID + P]
    gamma, beta = m.colidx["gamma"], m.colidx["beta"]
    with ExitStack() as own, nc.Block() as block:
        sb = lambda n, shape: own.enter_context(nc.sbuf_tensor("p2_" + n, shape, F32))
        z, zT = sb("z", [P, 2, D]), sb("zT", [P, 2, P])

        @block.vector
        def _(dve):
            def work(at):
                t = at(0)
                if t.live:
                    if t.past(2):
                        dve.wait_ge(s["zT_ps"], t.before(2))
                    normed(m, z[:, t.par, :], t, m.RN).then_inc(s["z"], 1)
                t = at(2)
                if t.live:
                    dve.wait_ge(s["q_ps"], t.nth())
                    nc.vector.tensor_scalar(m.QV[:, t.cols()], ps[2 + t.par][:, 0:P], m.bqu[:, 1:2], None,
                                            ALU.add).then_inc(s["q"], 1)
            over_tiles(dve, 2, work)

        @block.scalar
        def _(act):
            def work(at):
                t = at(1)
                if t.live:
                    act.wait_ge(s["zT_ps"], t.nth())
                    if t.past(2):
                        act.wait_ge(s["q_ps"], t.before(2))
                    nc.scalar.activation(zT[:, t.par, :], ps[t.par][:, 0:P], ACT.Identity,
                                         scale=m.cols[:, gamma:gamma + 1],
                                         bias=m.cols[:, beta:beta + 1]).then_inc(s["zT"], 1)
            over_tiles(act, 2, work)

        @block.tensor
        def _(pe):
            def work(at):
                t = at(1)
                if t.live:
                    pe.wait_ge(s["z"], t.nth())
                    if t.past(2):
                        pe.wait_ge(s["zT"], t.before(2))
                    nc.tensor.transpose(ps[t.par][:, 0:P], z[:, t.par, :], ident).then_inc(s["zT_ps"], 1)
                t = at(2)
                if t.live:
                    pe.wait_ge(s["zT"], t.nth())
                    if t.past(2):
                        pe.wait_ge(s["q"], t.before(2))
                    nc.tensor.matmul(ps[2 + t.par][:, 0:P], m.w["Wq_a"][:, :], zT[:, t.par, :],
                                     start=True, stop=True).then_inc(s["q_ps"], 1)
            over_tiles(pe, 2, work)


def relative_scores(m):
    nc, ps = m.nc, m.ps
    done, moved, stored = m.sem("p3_done"), m.sem("p3_moved"), [m.sem(f"p3_stored{n}") for n in range(4)]
    moved_a = m.sem("p3_moved_a")
    with ExitStack() as own, nc.Block() as block:
        rows = own.enter_context(nc.sbuf_tensor("p3_rows", [P, 4, H * LEN], F32))

        @block.tensor
        def _(pe):
            for i in range(LEN):
                if i >= 8:
                    pe.wait_ge(moved_a if i % 2 else moved, (i - 8) // 2 + 1)
                bank = ps[i % 8][:, :].rearrange("p (h j) -> p h j", j=LEN)
                last = nc.tensor.matmul(bank[:, :, 0:i + 1], m.QV[:, i::LEN], m.ptab[:, :, LEN - i:LEN + 1],
                                        start=True, stop=(i == LEN - 1))
                if i < LEN - 1:
                    last = nc.tensor.matmul(bank[:, :, i + 1:LEN], m.QV[:, i + 1::LEN], m.ptab[:, :, 0:LEN - 1 - i],
                                            start=False, stop=True)
                last.then_inc(done, 1)

        @block.vector
        def _(dve):
            for i in range(0, LEN, 2):
                dve.wait_ge(done, i + 1)
                if i >= 4:
                    dve.wait_ge(stored[i % 4], 16 * (i // 4))
                nc.vector.tensor_copy(rows[:, i % 4, :], ps[i % 8][:, :]).then_inc(moved, 1)

        @block.scalar
        def _(act):
            for i in range(1, LEN, 2):
                act.wait_ge(done, i + 1)
                if i >= 4:
                    act.wait_ge(stored[i % 4], 16 * (i // 4))
                nc.scalar.activation(rows[:, i % 4, :], ps[i % 8][:, :], ACT.Copy).then_inc(moved_a, 1)

        @block.sync
        def _(sp):
            for i in range(LEN):
                sp.wait_ge(moved_a if i % 2 else moved, i // 2 + 1)
                sp.dma_start(m.bd_dram[:, i, :], rows[:, i % 4, :]).then_inc(stored[i % 4], 16)
            for n in range(4):
                sp.wait_ge(stored[n], 16 * (LEN // 4))


def self_attention(m, name, relative):
    nc, ps, c = m.nc, m.ps, m.const
    s = {n: m.sem(name + "_" + n) for n in (
        "z", "zT_ps", "zT", "qk_ps", "v_ps", "q", "k", "v", "k_dve", "k_pool", "scores", "summed", "maxed",
        "shifted", "probs", "pT_ps", "pT", "o_ps", "recip", "o", "oT_ps", "oT", "y_ps", "xb", "zres", "ones")}
    bd_in = [m.sem(name + "_bd_in_a"), m.sem(name + "_bd_in_b")]
    tail = Tail(m, name, [sinks(m, "z")] + ([sinks(m, "ln")] if relative else []))
    ident = c[:, C_ID:C_ID + P]
    col = lambda n: m.cols[:, m.colidx[n]:m.colidx[n] + 1]
    scale = float(D if relative else HD) ** -0.5
    STAGES = 5
    with ExitStack() as own, nc.Block() as block:
        sb = lambda n, shape: own.enter_context(nc.sbuf_tensor(name + "_" + n, shape, F32))
        z, qT, kT = (sb(n, [P, 2, P]) for n in ("z", "qT", "kT"))
        zT4 = sb("zT4", [P, 2, B4, H4, LEN])
        k_all = sb("k_all", [P, 2, B4, H, LEN])
        v_all = sb("v_all", [P, 2, B4 * G, H4, HD + 1])
        bd = sb("bd", [P, 2, H * LEN])
        score, prob = sb("score", [P, 2, H * LEN]), sb("prob", [P, 2, H * LEN])
        mx, recip = sb("mx", [P, 2, H]), sb("recip", [P, 2, H])
        pT = sb("pT", [P, 2, G, P])
        o, oT, xb, zres = (sb(n, [P, 2, P]) for n in ("o", "oT", "xb", "zres"))
        wq = m.w["Wq_a" if relative else "w_q"][:, :]
        if relative:
            wk, wv = m.w["Wk_a"][:, :], m.w["Wv_a"][:, :]
        else:
            wk, wv = m.w["w_k"][:, :], m.w["w_v"][:, :]
        wo = m.w["Wf" if relative else "w_o"][:, :]
        rope = c[:, C_ROPE:C_ROPE + LEN].unsqueeze(1).broadcast_to([P, B4, LEN])
        by_seq = lambda ap: ap.rearrange("p (b i) -> p b i", i=LEN)
        by_head = lambda ap: ap.rearrange("p (h j) -> p h j", j=LEN)

        @block.sync
        def _(sp):
            def work(at):
                t = at(2)
                if t.live:
                    if t.past(2):
                        sp.wait_ge(s["summed"], t.before(2))
                    sp.dma_start(bd[:, t.par, :], m.bd_dram.rearrange("s i n -> (s i) n")[t.cols(), :]
                                 ).then_inc(bd_in[t.par], 16)
            if relative:
                over_tiles(sp, 2, work)

        @block.tensor
        def _(pe):
            def work(at):
                t = at(3)
                if t.live:
                    pe.wait_ge(s["q"], t.nth())
                    pe.wait_ge(s["k_dve"], t.nth(2))
                    pe.wait_ge(s["k_pool"], t.nth(2))
                    if t.past(2):
                        pe.wait_ge(s["summed"], t.before(2))
                    for b in range(B4):
                        last = nc.tensor.matmul(ps[3 + t.par][b * LEN:(b + 1) * LEN, :],
                                                qT[:, t.par, b * LEN:(b + 1) * LEN], k_all[:, t.par, b],
                                                start=True, stop=True, tile_position=(0, b * LEN))
                    last.then_inc(s["scores"], 1)
                t = at(1)
                if t.live:
                    pe.wait_ge(s["zT"], t.nth())
                    if t.past():
                        pe.wait_ge(s["q"], t.before())
                        pe.wait_ge(s["k"], t.before())
                    nc.tensor.matmul(ps[1][:, 0:P], wq, zT4[:, t.par, :, 0, :], start=True, stop=True)
                    nc.tensor.matmul(ps[1][:, P:2 * P], wk, zT4[:, t.par, :, 0, :], start=True, stop=True).then_inc(s["qk_ps"], 1)
                t = at(4)
                if t.live:
                    pe.wait_ge(s["probs"], t.nth())
                    if t.past():
                        pe.wait_ge(s["pT"], t.before())
                    for g in range(G):
                        last = nc.tensor.transpose(ps[5][:, g * P:(g + 1) * P], prob[:, t.par, g * P:(g + 1) * P], ident)
                    last.then_inc(s["pT_ps"], 1)
                t = at(2)
                if t.live:
                    if t.past():
                        pe.wait_ge(s["v"], t.before())
                    for b in range(B4):
                        last = nc.tensor.matmul(ps[2][:, b * D:(b + 1) * D], zT4[:, t.par, b], wv, start=True, stop=True)
                    last.then_inc(s["v_ps"], 1)
                t = at(5)
                if t.live:
                    pe.wait_ge(s["o"], t.nth())
                    if t.past():
                        pe.wait_ge(tail.x_new, t.before())
                    nc.tensor.transpose(ps[7][:, P:2 * P], o[:, t.par, :], ident).then_inc(s["oT_ps"], 1)
                t = at(4)
                if t.live:
                    pe.wait_ge(s["pT"], t.nth())
                    pe.wait_ge(s["v"], t.nth())
                    if t.past():
                        pe.wait_ge(s["o"], t.before())
                    for b in range(B4):
                        for g in range(G):
                            w = H4 * (HD + 1)
                            last = nc.tensor.matmul(ps[6][b * LEN:(b + 1) * LEN, g * w:(g + 1) * w],
                                                    pT[:, t.par, g, b * LEN:(b + 1) * LEN],
                                                    v_all[:, t.par, b * G + g], start=True, stop=True,
                                                    tile_position=(0, b * LEN))
                    last.then_inc(s["o_ps"], 1)
                t = at(5)
                if t.live:
                    pe.wait_ge(s["oT"], t.nth())
                    nc.tensor.matmul(ps[7][:, 0:D], oT[:, t.par, :], wo, start=True, stop=True).then_inc(s["y_ps"], 1)
                t = at(0)
                if t.live:
                    pe.wait_ge(s["z"], t.nth())
                    if t.past():
                        pe.wait_ge(s["zT"], t.before())
                    nc.tensor.transpose(ps[0][:, 0:P], z[:, t.par, :], ident).then_inc(s["zT_ps"], 1)
            over_tiles(pe, STAGES, work)

        @block.scalar
        def _(act):
            def work(at):
                t = at(1)
                if t.live and relative:
                    act.wait_ge(s["qk_ps"], t.nth())
                    if t.past(2):
                        act.wait_ge(s["scores"], t.before(2))
                    nc.scalar.activation(qT[:, t.par, :], ps[1][:, 0:P], ACT.Identity,
                                         bias=m.bqu[:, 0:1]).then_inc(s["q"], 1)
                    if t.past(2):
                        act.wait_ge(s["k_dve"], t.before(2, 2))
                        act.wait_ge(s["k_pool"], t.before(2, 2))
                    nc.scalar.activation(kT[:, t.par, :], ps[1][:, P:2 * P], ACT.Identity,
                                         bias=col("bk_a")).then_inc(s["k"], 1)
                t = at(4)
                if t.live:
                    act.wait_ge(s["pT_ps"], t.nth())
                    if t.past(2):
                        act.wait_ge(s["o_ps"], t.before(2))
                    nc.scalar.activation(pT[:, t.par], ps[5][:, :].rearrange("p (g n) -> p g n", g=G),
                                         ACT.Copy).then_inc(s["pT"], 1)
                t = at(5)
                if t.live:
                    act.wait_ge(s["oT_ps"], t.nth())
                    if t.past(2):
                        act.wait_ge(s["y_ps"], t.before(2))
                    nc.scalar.activation(oT[:, t.par, :], ps[7][:, P:2 * P], ACT.Copy).then_inc(s["oT"], 1)
                t = at(3)
                if t.live:
                    act.wait_ge(s["shifted"], t.nth())
                    if t.past(2):
                        act.wait_ge(s["pT_ps"], t.before(2))
                    nc.scalar.activation(prob[:, t.par, :], score[:, t.par, :], ACT.Exp, scale=scale).then_inc(s["probs"], 1)
                t = at(0)
                if t.live:
                    act.wait_ge(s["zT_ps"], t.nth())
                    if t.past(2):
                        act.wait_ge(s["v_ps"], t.before(2))
                    four = by_seq(ps[0][:, 0:P]).unsqueeze(2).broadcast_to([P, B4, H4, LEN])
                    if relative:
                        nc.scalar.activation(zT4[:, t.par], four, ACT.Identity, scale=col("gamma"),
                                             bias=col("beta")).then_inc(s["zT"], 1)
                    else:
                        nc.scalar.activation(zT4[:, t.par], four, ACT.Copy,
                                             scale=col("norm_w")).then_inc(s["zT"], 1)
            over_tiles(act, STAGES, work)

        @block.vector
        def _(dve):
            def spread(t, b):
                return nc.vector.tensor_tensor(
                    k_all[:, t.par, b], kT[:, t.par, b * LEN:(b + 1) * LEN].unsqueeze(1).broadcast_to([P, H, LEN]),
                    c[:, C_M16:C_M16 + H].unsqueeze(2).broadcast_to([P, H, LEN]), ALU.mult)

            nc.vector.memset(v_all[:, :, :, :, :], 0.0).then_inc(s["ones"], 1)
            dve.wait_ge(s["ones"], 1)
            for par in range(2):
                nc.vector.tensor_copy(v_all[:, par, :, :, HD], c[:, C_M4P:C_M4P + H4].unsqueeze(1).broadcast_to(
                    [P, B4 * G, H4])).then_inc(s["ones"], 1)

            def work(at):
                t = at(2)
                if t.live:
                    dve.wait_ge(s["k"], t.nth())
                    if t.past(2):
                        dve.wait_ge(s["scores"], t.before(2))
                    for b in (0, 1):
                        spread(t, b).then_inc(s["k_dve"], 1)
                t = at(0)
                if t.live:
                    if t.past(2):
                        dve.wait_ge(s["zT_ps"], t.before(2))
                    normed(m, z[:, t.par, :], t, m.RN).then_inc(s["z"], 1)
                t = at(4)
                if t.live and not relative:
                    if t.past(2):
                        dve.wait_ge(s["xb"], t.before(2))
                    normed(m, zres[:, t.par, :], t, m.RZ).then_inc(s["zres"], 1)
                t = at(3)
                if t.live:
                    dve.wait_ge(s["scores"], t.nth())
                    if t.past(2):
                        dve.wait_ge(s["probs"], t.before(2))
                    if relative:
                        dve.wait_ge(bd_in[t.par], t.nth_of_pair(16))
                        more = by_head(bd[:, t.par, :])
                    else:
                        more = c[:, C_CAUSAL:C_CAUSAL + LEN].unsqueeze(1).broadcast_to([P, H, LEN])
                    nc.vector.tensor_tensor(by_head(score[:, t.par, :]), by_head(ps[3 + t.par][:, :]), more,
                                            ALU.add).then_inc(s["summed"], 1)
                    dve.wait_ge(s["summed"], t.nth())
                    if t.past(2):
                        dve.wait_ge(s["shifted"], t.before(2))
                    nc.vector.tensor_reduce(mx[:, t.par, :], by_head(score[:, t.par, :]), AX.X,
                                            ALU.max).then_inc(s["maxed"], 1)
                t = at(1)
                if t.live and not relative:
                    dve.wait_ge(s["qk_ps"], t.nth())
                    if t.past(2):
                        dve.wait_ge(s["scores"], t.before(2))
                        dve.wait_ge(s["k_pool"], t.before(2, 2))
                    nc.vector.tensor_tensor(by_seq(qT[:, t.par, :]), by_seq(ps[1][:, 0:P]), rope,
                                            ALU.mult).then_inc(s["q"], 1)
                    nc.vector.tensor_tensor(by_seq(kT[:, t.par, :]), by_seq(ps[1][:, P:2 * P]), rope,
                                            ALU.mult).then_inc(s["k"], 1)
                t = at(4)
                if t.live:
                    dve.wait_ge(s["o_ps"], t.nth())
                    if t.past(2):
                        dve.wait_ge(s["oT_ps"], t.before(2))
                    heads = ps[6][:, 0:H * (HD + 1)].rearrange("p (h n) -> p h n", n=HD + 1)
                    nc.vector.reciprocal(recip[:, t.par, :], heads[:, :, HD]).then_inc(s["recip"], 1)
                    dve.wait_ge(s["recip"], t.nth())
                    nc.vector.tensor_tensor(o[:, t.par, :].rearrange("p (h d) -> p h d", d=HD), heads[:, :, 0:HD],
                                            recip[:, t.par, :].unsqueeze(2).broadcast_to([P, H, HD]),
                                            ALU.mult).then_inc(s["o"], 1)
                t = at(2)
                if t.live:
                    dve.wait_ge(s["v_ps"], t.nth())
                    dve.wait_ge(s["ones"], 3)
                    if t.past(2):
                        dve.wait_ge(s["o_ps"], t.before(2))
                    nc.vector.tensor_tensor(v_all[:, t.par, :, :, 0:HD],
                                            ps[2][:, :].rearrange("p (n h d) -> p n h d", h=H4, d=HD),
                                            c[:, C_M4P:C_M4P + H4].unsqueeze(1).unsqueeze(3).broadcast_to(
                                                [P, B4 * G, H4, HD]), ALU.mult).then_inc(s["v"], 1)
                t = at(5)
                if t.live:
                    dve.wait_ge(s["y_ps"], t.nth())
                    dve.wait_ge(s["xb"], t.nth())
                    nc.vector.tensor_tensor(m.X[:, t.cols()], ps[7][:, 0:D], xb[:, t.par, :],
                                            ALU.add).then_inc(tail.x_new, 1)
                    tail.dve(dve, t)
            over_tiles(dve, STAGES, work)

        @block.gpsimd
        def _(pool):
            def work(at):
                t = at(2)
                if t.live:
                    pool.wait_ge(s["k"], t.nth())
                    if t.past(2):
                        pool.wait_ge(s["scores"], t.before(2))
                    for b in (2, 3):
                        nc.gpsimd.tensor_tensor(
                            k_all[:, t.par, b],
                            kT[:, t.par, b * LEN:(b + 1) * LEN].unsqueeze(1).broadcast_to([P, H, LEN]),
                            c[:, C_M16:C_M16 + H].unsqueeze(2).broadcast_to([P, H, LEN]), ALU.mult).then_inc(s["k_pool"], 1)
                t = at(4)
                if t.live:
                    if t.past(2):
                        pool.wait_ge(tail.x_new, t.before(2))
                    if relative:
                        more = m.bA[:, :]
                    else:
                        pool.wait_ge(s["zres"], t.nth())
                        more = zres[:, t.par, :]
                    nc.gpsimd.tensor_tensor(xb[:, t.par, :], m.X[:, t.cols()], more, ALU.add).then_inc(s["xb"], 1)
                t = at(3)
                if t.live:
                    pool.wait_ge(s["maxed"], t.nth())
                    sc = by_head(score[:, t.par, :])
                    nc.gpsimd.tensor_tensor(sc, sc, mx[:, t.par, :].unsqueeze(2).broadcast_to([P, H, LEN]),
                                            ALU.subtract).then_inc(s["shifted"], 1)
                t = at(5)
                if t.live:
                    tail.pool(pool, t)
            over_tiles(pool, STAGES, work)


def relative_attention(m):
    self_attention(m, "p4", True)


def causal_attention(m):
    self_attention(m, "p8", False)


def cross_many_heads(m):
    nc, ps, c = m.nc, m.ps, m.const
    N = B4 * G
    AHEAD = 4
    LAST = 2 * P
    s = {n: m.sem("p6_" + n) for n in (
        "z", "zT_ps", "zT", "q_ps", "q", "k_ps", "k", "v_ps", "v", "v_last", "scores", "maxed", "probs", "recip",
        "normed", "pT_ps", "pT", "last_ps", "last", "o_ps", "masked", "oT", "y_ps", "xb")}
    ctx_in = [m.sem("p6_ctx_in_a"), m.sem("p6_ctx_in_b")]
    tail = Tail(m, "p6", [sinks(m, "z"), sinks(m, "rms")])
    ident = c[:, C_ID:C_ID + P]
    s0 = float(D) ** -0.5
    with ExitStack() as own, nc.Block() as block:
        sb = lambda n, shape: own.enter_context(nc.sbuf_tensor("p6_" + n, shape, F32))
        ctxT = sb("ctxT", [P, 2, B4, CTX])
        z, zT, oT, xb = (sb(n, [P, 2, P]) for n in ("z", "zT", "oT", "xb"))
        q_all = sb("q_all", [P, 2, B4, H4, LEN])
        kT = sb("kT", [P, 2, CTX])
        v, v_last = sb("v", [P, 2, 2, P]), sb("v_last", [G, 2, P])
        prob = sb("prob", [P, 2, G, CTX])
        nmax, total, recip = (sb(n, [P, N]) for n in ("nmax", "total", "recip"))
        pT, p_last = sb("pT", [P, 2, 2, P]), sb("p_last", [G, 2, P])
        masked = sb("masked", [P, H4, LEN])

        @block.sync
        def _(sp):
            def work(at):
                t = at(0)
                if t.live:
                    if t.past(2):
                        sp.wait_ge(s["v_ps"], t.before(2, B4))
                    sp.dma_start(ctxT[:, t.par], m.ctxT_dram[:, t.cols(B4 * CTX)].rearrange(
                        "d (b k) -> d b k", k=CTX)).then_inc(ctx_in[t.par], 16)
            over_tiles(sp, 1, work)

        @block.tensor
        def _(pe):
            def scores(t, u):
                b, g = u // G, u % G
                pe.wait_ge(s["q"], t.nth())
                pe.wait_ge(s["k"], t.unit(b, 0, B4))
                if t.past_unit(u, 2):
                    pe.wait_ge(s["probs"], t.unit(u, 2))
                rows = slice(32 * g, 32 * g + 32)
                nc.tensor.matmul(ps[3 + u % 2][:, 0:CTX], q_all[rows, t.par, b], kT[rows, b % 2, :],
                                 start=True, stop=True, tile_position=(32 * g, 0)).then_inc(s["scores"], 1)

            def keys(t, b):
                pe.wait_ge(ctx_in[t.par], t.nth_of_pair(16))
                if t.past_unit(b, 1, B4):
                    pe.wait_ge(s["k"], t.unit(b, 1, B4))
                nc.tensor.matmul(ps[1][:, 0:CTX], m.w["WkT_x"][:, :], ctxT[:, t.par, b, :],
                                 start=True, stop=True).then_inc(s["k_ps"], 1)

            def values(t, b):
                pe.wait_ge(ctx_in[t.par], t.nth_of_pair(16))
                if t.past_unit(b, 1, B4):
                    pe.wait_ge(s["v"], t.unit(b, 1, B4))
                    pe.wait_ge(s["v_last"], t.unit(b, 1, B4))
                for n in range(2):
                    nc.tensor.matmul(ps[2][:, n * P:(n + 1) * P], ctxT[:, t.par, b, n * P:(n + 1) * P],
                                     m.w["WvT_x"][:, :], start=True, stop=True)
                nc.tensor.matmul(ps[2][0:G, LAST:LAST + P], ctxT[:, t.par, b, LAST:LAST + 1].broadcast_to([P, G]),
                                 m.w["WvT_x"][:, :], start=True, stop=True).then_inc(s["v_ps"], 1)

            def turn(t, u):
                b, g = u // G, u % G
                pe.wait_ge(s["normed"], t.unit(u))
                bank = ps[5 + u % 2]
                if t.past_unit(u, 2):
                    pe.wait_ge(s["pT"], t.unit(u, 2))
                if u % 2 and t.past_unit(b, 1, B4):
                    pe.wait_ge(s["last"], t.unit(b, 1, B4))
                for n in range(2):
                    last = nc.tensor.transpose(bank[:, n * P:(n + 1) * P], prob[:, b % 2, g, n * P:(n + 1) * P], ident)
                last.then_inc(s["pT_ps"], 1)
                if g == G - 1:
                    nc.tensor.transpose(bank[0:G, LAST:LAST + P], prob[:, b % 2, :, LAST], ident).then_inc(s["last_ps"], 1)

            def weigh(t, u):
                b, g = u // G, u % G
                pe.wait_ge(s["pT"], t.unit(u))
                pe.wait_ge(s["v"], t.unit(b, 0, B4))
                if g == 0 and t.past_unit(b, 1, B4):
                    pe.wait_ge(s["masked"], t.unit(b, 1, B4))
                for n in range(2):
                    nc.tensor.matmul(ps[7][32 * g:32 * g + 32, 0:P], v[:, b % 2, n, 32 * g:32 * g + 32],
                                     pT[:, u % 2, n, :], start=(n == 0), stop=(n == 1),
                                     tile_position=(0, 32 * g), skip_group_check=True).then_inc(s["o_ps"], 1)
                if g == G - 1:
                    pe.wait_ge(s["last"], t.unit(b, 0, B4))
                    pe.wait_ge(s["v_last"], t.unit(b, 0, B4))
                    nc.tensor.matmul(ps[7][:, 0:P], v_last[:, b % 2, :], p_last[:, b % 2, :], start=False, stop=True,
                                     skip_group_check=True).then_inc(s["o_ps"], 1)

            def steps(at):
                cur, nxt, prev = at(1), at(0), at(2)
                for n in range(N):
                    t, u = (cur, n + AHEAD) if n + AHEAD < N else (nxt, n + AHEAD - N)
                    if t.live:
                        scores(t, u)
                    t, b = (cur, n // G + 2) if n // G + 2 < B4 else (nxt, n // G + 2 - B4)
                    if n % G == 1 and t.live:
                        keys(t, b)
                    t, b = (cur, n // G + 1) if n // G + 1 < B4 else (nxt, 0)
                    if n % G == 2 and t.live:
                        values(t, b)
                    if cur.live:
                        turn(cur, n)
                    t, u = (cur, n - 1) if n else (prev, N - 1)
                    if t.live:
                        weigh(t, u)
                    if n == 3 and prev.live:
                        pe.wait_ge(s["oT"], prev.nth(B4))
                        nc.tensor.matmul(ps[0][:, 2 * P:3 * P], oT[:, prev.par, :], m.w["WoT_x"][:, :],
                                         start=True, stop=True).then_inc(s["y_ps"], 1)
                    if n == 5 and nxt.live:
                        pe.wait_ge(s["z"], nxt.nth())
                        if nxt.past(2):
                            pe.wait_ge(tail.x_new, nxt.before(2))
                        nc.tensor.transpose(ps[0][:, 0:P], z[:, nxt.par, :], ident).then_inc(s["zT_ps"], 1)
                    if n == 7 and nxt.live:
                        pe.wait_ge(s["zT"], nxt.nth())
                        nc.tensor.matmul(ps[0][:, P:2 * P], m.w["WqT_x"][:, :], zT[:, nxt.par, :],
                                         start=True, stop=True).then_inc(s["q_ps"], 1)
            over_tiles(pe, 2, steps)

        @block.scalar
        def _(act):
            def steps(at):
                cur, nxt = at(1), at(0)
                for n in range(N):
                    t, u = (cur, n + AHEAD) if n + AHEAD < N else (nxt, n + AHEAD - N)
                    if t.live:
                        act.wait_ge(s["maxed"], t.unit(u))
                        if t.past_unit(u, 8):
                            act.wait_ge(s["pT_ps"], t.unit(u, 8))
                        if u % G == 0 and t.past_unit(u // G, 2, B4):
                            act.wait_ge(s["last_ps"], t.unit(u // G, 2, B4))
                        nc.scalar.activation(prob[:, u // G % 2, u % G, :], ps[3 + u % 2][:, 0:CTX], ACT.Exp,
                                             bias=nmax[:, u:u + 1], accum_out=total[:, u:u + 1]).then_inc(s["probs"], 1)
                    t, b = (cur, n // G + 2) if n // G + 2 < B4 else (nxt, n // G + 2 - B4)
                    if n % G == 1 and t.live:
                        act.wait_ge(s["k_ps"], t.unit(b, 0, B4))
                        if t.past_unit(b, 2, B4):
                            act.wait_ge(s["scores"], t.unit(b * G + G - 1, 2 * G))
                        nc.scalar.activation(kT[:, b % 2, :], ps[1][:, 0:CTX], ACT.Copy).then_inc(s["k"], 1)
                    t, b = (cur, n // G + 1) if n // G + 1 < B4 else (nxt, 0)
                    if n % G == 2 and t.live:
                        act.wait_ge(s["v_ps"], t.unit(b, 0, B4))
                        act.wait_ge(s["v_last"], t.unit(b, 0, B4))
                        if t.past_unit(b, 2, B4):
                            act.wait_ge(s["o_ps"], t.unit(b, 2, B4) * 9)
                        nc.scalar.activation(v[:, b % 2], ps[2][:, 0:2 * P].rearrange("p (n d) -> p n d", n=2),
                                             ACT.Copy).then_inc(s["v"], 1)
                    if n % G == 3 and cur.live:
                        b = n // G
                        act.wait_ge(s["last_ps"], cur.unit(b, 0, B4))
                        act.wait_ge(s["pT"], cur.unit(n))
                        if cur.past_unit(b, 2, B4):
                            act.wait_ge(s["o_ps"], cur.unit(b, 2, B4) * 9)
                        nc.scalar.activation(p_last[:, b % 2, :], ps[6][0:G, LAST:LAST + P], ACT.Copy).then_inc(s["last"], 1)
                    if n == 5 and nxt.live:
                        act.wait_ge(s["zT_ps"], nxt.nth())
                        if nxt.past(2):
                            act.wait_ge(s["q_ps"], nxt.before(2))
                        nc.scalar.activation(zT[:, nxt.par, :], ps[0][:, 0:P], ACT.Copy, scale=s0).then_inc(s["zT"], 1)
            over_tiles(act, 2, steps)

        @block.vector
        def _(dve):
            def steps(at):
                cur, nxt, prev = at(1), at(0), at(2)
                for n in range(N):
                    t, u = (cur, n + AHEAD - 1) if n + AHEAD - 1 < N else (nxt, n + AHEAD - 1 - N)
                    if t.live:
                        dve.wait_ge(s["probs"], t.unit(u))
                        if t.past_unit(u, N):
                            dve.wait_ge(s["normed"], t.unit(u, N))
                        nc.vector.reciprocal(recip[:, u:u + 1], total[:, u:u + 1]).then_inc(s["recip"], 1)
                    t, u = (cur, n + AHEAD) if n + AHEAD < N else (nxt, n + AHEAD - N)
                    if t.live:
                        dve.wait_ge(s["scores"], t.unit(u))
                        nc.vector.tensor_reduce(nmax[:, u:u + 1], ps[3 + u % 2][:, 0:CTX], AX.X, ALU.max,
                                                negate=True).then_inc(s["maxed"], 1)
                    t, b = (cur, n // G + 1) if n // G + 1 < B4 else (nxt, 0)
                    if n % G == 2 and t.live:
                        dve.wait_ge(s["v_ps"], t.unit(b, 0, B4))
                        if t.past_unit(b, 2, B4):
                            dve.wait_ge(s["o_ps"], t.unit(b, 2, B4) * 9)
                        nc.vector.tensor_tensor(v_last[:, b % 2, :].rearrange("p (g n) -> p g n", g=G),
                                                ps[2][0:G, LAST:LAST + P].rearrange("p (g n) -> p g n", g=G),
                                                c[0:G, C_ID:C_ID + G].unsqueeze(2).broadcast_to([G, G, 32]),
                                                ALU.mult).then_inc(s["v_last"], 1)
                    if cur.live:
                        dve.wait_ge(s["pT_ps"], cur.unit(n))
                        if n % G == G - 1:
                            dve.wait_ge(s["last_ps"], cur.unit(n // G, 0, B4))
                        if cur.past_unit(n, 2):
                            b2, g2 = (n - 2) // G, (n - 2) % G
                            dve.wait_ge(s["o_ps"], (cur.n * B4 + b2) * 9 + 2 * g2 + 2)
                        nc.vector.tensor_copy(pT[:, n % 2], ps[5 + n % 2][:, 0:2 * P].rearrange(
                            "p (n k) -> p n k", n=2)).then_inc(s["pT"], 1)
                    t, b = (cur, n // G - 1) if n else (prev, B4 - 1)
                    if n % G == 0 and t.live:
                        dve.wait_ge(s["o_ps"], t.unit(b, 0, B4) * 9)
                        if t.past_unit(b, 1, B4):
                            dve.wait_ge(s["oT"], t.unit(b, 1, B4))
                        nc.vector.tensor_tensor(masked[:, :, :], ps[7][:, 0:P].rearrange("p (h i) -> p h i", h=H4),
                                                c[:, C_M4G:C_M4G + H4].unsqueeze(2).broadcast_to([P, H4, LEN]),
                                                ALU.mult).then_inc(s["masked"], 1)
                        dve.wait_ge(s["masked"], t.unit(b, 0, B4))
                        if b == 0 and t.past(2):
                            dve.wait_ge(s["y_ps"], t.before(2))
                        nc.vector.tensor_reduce(oT[:, t.par, b * LEN:(b + 1) * LEN],
                                                masked[:, :, :].rearrange("p h i -> p i h"), AX.X,
                                                ALU.add).then_inc(s["oT"], 1)
                    if n == 3 and nxt.live:
                        if nxt.past(2):
                            dve.wait_ge(s["zT_ps"], nxt.before(2))
                        normed(m, z[:, nxt.par, :], nxt, m.RZ).then_inc(s["z"], 1)
                    if n == 4 and prev.live:
                        dve.wait_ge(s["y_ps"], prev.nth())
                        dve.wait_ge(s["xb"], prev.nth())
                        nc.vector.tensor_tensor(m.X[:, prev.cols()], ps[0][:, 2 * P:3 * P], xb[:, prev.par, :],
                                                ALU.add).then_inc(tail.x_new, 1)
                        tail.dve(dve, prev)
                    if n == 8 and nxt.live:
                        dve.wait_ge(s["q_ps"], nxt.nth())
                        if nxt.past(2):
                            dve.wait_ge(s["scores"], nxt.before(2, N))
                        nc.vector.tensor_tensor(
                            q_all[:, nxt.par],
                            ps[0][:, P:2 * P].rearrange("p (b i) -> p b i", i=LEN).unsqueeze(2).broadcast_to(
                                [P, B4, H4, LEN]),
                            c[:, C_M4G:C_M4G + H4].unsqueeze(1).unsqueeze(3).broadcast_to([P, B4, H4, LEN]),
                            ALU.mult).then_inc(s["q"], 1)
            over_tiles(dve, 2, steps)

        @block.gpsimd
        def _(pool):
            def steps(at):
                cur, nxt, prev = at(1), at(0), at(2)
                for n in range(N):
                    t, u = (cur, n + AHEAD - 1) if n + AHEAD - 1 < N else (nxt, n + AHEAD - 1 - N)
                    if t.live:
                        pool.wait_ge(s["recip"], t.unit(u))
                        p = prob[:, u // G % 2, u % G, :]
                        nc.gpsimd.tensor_tensor(p, p, recip[:, u:u + 1].broadcast_to([P, CTX]),
                                                ALU.mult).then_inc(s["normed"], 1)
                    if n == 2 and prev.live:
                        if prev.past(2):
                            pool.wait_ge(tail.x_new, prev.before(2))
                        nc.gpsimd.tensor_tensor(xb[:, prev.par, :], m.X[:, prev.cols()], m.bX[:, :], ALU.add).then_inc(s["xb"], 1)
                    if n == 5 and prev.live:
                        tail.pool(pool, prev)
            over_tiles(pool, 2, steps)


def lay_out_experts(f):
    def first(w):
        return w.transpose(1, 0, 2).reshape(D, E * F)

    def second(w):
        return w.reshape(E, FC, P, D).transpose(2, 0, 1, 3).reshape(P, E * FC * D)

    return {
        "Wg": f["L0_ffn_Wg"], "router_T": f["L1_ffn_router_w"].T,
        "w1_0": first(f["L0_ffn_fc1_w"]), "w2_0": second(f["L0_ffn_fc2_w"]),
        "w1_1": first(f["L1_ffn_w1"]), "w2_1": second(f["L1_ffn_w2"]),
        "b1_T": f["L0_ffn_fc1_b"].reshape(E, FC, P).transpose(2, 0, 1).reshape(P, E * FC),
        "ln_wT": f["L0_ffn_ln_w"].T, "ln_bT": f["L0_ffn_ln_b"].T,
        "b2": f["L0_ffn_fc2_b"], "alpha": np.tile(f["L0_ffn_alpha"][None], (P, 1)),
    }


def route(m, name, layer):
    nc, ps, c = m.nc, m.ps, m.const
    s = {n: m.sem(name + "_" + n) for n in (
        "z", "x", "zT_ps", "xT_ps", "zT", "xT", "logit_ps", "logits", "best", "step", "exp", "loaded")}
    ident = c[:, C_ID:C_ID + P]
    with ExitStack() as own, nc.Block() as block:
        sb = lambda n, shape, dt=F32: own.enter_context(nc.sbuf_tensor(name + "_" + n, shape, dt))
        z, zT = sb("z", [P, 2, D]), sb("zT", [P, 2, P])
        x2 = sb("x2", [P, 2, D])
        wg = sb("wg", [P, E])
        logits, best = sb("logits", [P, TILES, E]), sb("best", [P, TILES, E])
        which, whichf = sb("which", [P, TILES, E], U32), sb("whichf", [P, TILES, 2])
        gap, ex, g = sb("gap", [P, TILES]), sb("ex", [P, TILES]), sb("g", [P, 2, TILES])
        hot = sb("hot", [P, 2, TILES, E])
        double = layer == 0

        @block.sync
        def _(sp):
            sp.dma_start(wg[:, :], m.a["Wg" if layer == 0 else "router_T"]).then_inc(s["loaded"], 16)

        @block.tensor
        def _(pe):
            pe.wait_ge(s["loaded"], 16)

            def work(at):
                t = at(2)
                if t.live:
                    pe.wait_ge(s["zT"], t.nth())
                    if t.past(2):
                        pe.wait_ge(s["logits"], t.before(2))
                    nc.tensor.matmul(ps[4 + t.par][:, 0:E], zT[:, t.par, :], wg[:, :],
                                     start=True, stop=True).then_inc(s["logit_ps"], 1)
                t = at(1)
                if t.live:
                    pe.wait_ge(s["z"], t.nth())
                    if t.past(2):
                        pe.wait_ge(s["zT"], t.before(2))
                        pe.wait_ge(s["xT"], t.before(2))
                    nc.tensor.transpose(ps[t.par][:, 0:P], z[:, t.par, :], ident).then_inc(s["zT_ps"], 1)
                    if double:
                        pe.wait_ge(s["x"], t.nth())
                        nc.tensor.transpose(ps[2 + t.par][:, 0:P], x2[:, t.par, :], ident).then_inc(s["xT_ps"], 1)
            over_tiles(pe, 2, work)

        @block.scalar
        def _(act):
            def work(at):
                t = at(1)
                if t.live:
                    act.wait_ge(s["zT_ps"], t.nth())
                    if t.past(2):
                        act.wait_ge(s["logit_ps"], t.before(2))
                    nc.scalar.activation(zT[:, t.par, :], ps[t.par][:, 0:P], ACT.Copy).then_inc(s["zT"], 1)
            over_tiles(act, 1, work)
            act.wait_ge(s["step"], 1)
            nc.scalar.activation(ex[:, :], gap[:, :], ACT.Exp).then_inc(s["exp"], 1)

        @block.vector
        def _(dve):
            def work(at):
                t = at(0)
                if t.live:
                    if t.past(2):
                        dve.wait_ge(s["zT_ps"], t.before(2))
                    normed(m, z[:, t.par, :], t, m.RZ).then_inc(s["z"], 1)
                    if double:
                        if t.past(2):
                            dve.wait_ge(s["xT_ps"], t.before(2))
                        normed(m, x2[:, t.par, :], t, m.RN).then_inc(s["x"], 1)
                t = at(1)
                if t.live:
                    if double:
                        dve.wait_ge(s["xT_ps"], t.nth())
                        src = ps[2 + t.par][:, 0:P]
                    else:
                        dve.wait_ge(s["zT"], t.nth())
                        src = zT[:, t.par, :]
                    nc.vector.tensor_scalar(m.QV[:, t.cols()], src, 1.0, None, ALU.mult).then_inc(s["xT"], 1)
                t = at(2)
                if t.live:
                    dve.wait_ge(s["logit_ps"], t.nth())
                    nc.vector.tensor_scalar(logits[:, :, :].rearrange("p t e -> p (t e)")[:, t.cols(E)],
                                            ps[4 + t.par][:, 0:E], 1.0, None, ALU.mult).then_inc(s["logits"], 1)
            over_tiles(dve, 2, work)
            dve.wait_ge(s["logits"], TILES)
            for n in range(TILES):
                nc.vector.max(best[:, n, :], logits[:, n, :]).then_inc(s["best"], 1)
            for n in range(TILES):
                dve.wait_ge(s["best"], n + 1)
                last = nc.vector.max_index(which[:, n, :], best[:, n, :], logits[:, n, :])
                last.then_inc(s["best"], 1)
            dve.wait_ge(s["best"], 2 * TILES)
            nc.vector.tensor_tensor(gap[:, :], best[:, :, 1], best[:, :, 0], ALU.subtract).then_inc(s["step"], 1)
            nc.vector.tensor_copy(whichf[:, :, :], which[:, :, 0:2]).then_inc(s["step"], 1)
            dve.wait_ge(s["exp"], 1)
            nc.vector.tensor_scalar(g[:, 1, :], ex[:, :], 1.0, None, ALU.add).then_inc(s["step"], 1)
            dve.wait_ge(s["step"], 3)
            nc.vector.reciprocal(g[:, 0, :], g[:, 1, :]).then_inc(s["step"], 1)
            dve.wait_ge(s["step"], 4)
            nc.vector.tensor_tensor(g[:, 1, :], ex[:, :], g[:, 0, :], ALU.mult).then_inc(s["step"], 1)
            iota = c[:, C_IOTA:C_IOTA + E].unsqueeze(1).broadcast_to([P, TILES, E])
            for k in range(2):
                nc.vector.tensor_tensor(hot[:, k], iota, whichf[:, :, k:k + 1].broadcast_to([P, TILES, E]),
                                        ALU.is_equal).then_inc(s["step"], 1)
            dve.wait_ge(s["step"], 7)
            for k in range(2):
                nc.vector.tensor_tensor(hot[:, k], hot[:, k], g[:, k, :].unsqueeze(2).broadcast_to([P, TILES, E]),
                                        ALU.mult).then_inc(s["step"], 1)
            dve.wait_ge(s["step"], 9)
            nc.vector.tensor_tensor(m.comb[:, :, :], hot[:, 0], hot[:, 1], ALU.add).then_inc(s["step"], 1)
            if layer == 0:
                dve.wait_ge(s["step"], 10)
                nc.vector.tensor_tensor(m.comb[:, :, :], m.comb[:, :, :],
                                        m.alpha[:, :].unsqueeze(1).broadcast_to([P, TILES, E]),
                                        ALU.mult).then_inc(s["step"], 1)


def prepare_experts(m):
    nc, ps = m.nc, m.ps
    loaded, folded, products = m.sem("experts_in"), m.sem("fc1_scaled"), m.sem("ln_b_fc1")
    with ExitStack() as own, nc.Block() as block:
        lnw, lnb, b1 = (own.enter_context(nc.sbuf_tensor("pe_" + n, [P, w], F32)) for n, w in (
            ("lnw", E), ("lnb", E), ("b1", E * FC)))

        @block.sync
        def _(sp):
            for dst, src in ((lnw, "ln_wT"), (lnb, "ln_bT"), (b1, "b1_T"), (m.w1, "w1_0"), (m.w2, "w2_0"),
                             (m.alpha, "alpha")):
                sp.dma_start(dst[:, :], m.a[src]).then_inc(loaded, 16)
            sp.dma_start(m.b2[:, :], m.a["b2"]).then_inc(loaded, 16)

        @block.tensor
        def _(pe):
            pe.wait_ge(loaded, 16 * 7)
            for e in range(E):
                for f in range(FC):
                    k = e * FC + f
                    last = nc.tensor.matmul(ps[0][:, k:k + 1], m.w1[:, k * P:(k + 1) * P], lnb[:, e:e + 1],
                                            start=True, stop=True)
            last.then_inc(products, 1)

        @block.vector
        def _(dve):
            dve.wait_ge(loaded, 16 * 7)
            dve.wait_ge(products, 1)
            nc.vector.tensor_tensor(m.b1[:, :], ps[0][:, 0:E * FC], b1[:, :], ALU.add).then_inc(folded, 1)
            for e in range(E):
                w = m.w1[:, e * F:(e + 1) * F]
                nc.vector.tensor_scalar(w, w, lnw[:, e:e + 1], None, ALU.mult).then_inc(folded, 1)


def load_layer_one_experts(m):
    loaded = m.sem("experts_1_in")
    with m.nc.Block() as block:
        @block.sync
        def _(sp):
            sp.dma_start(m.w1[:, :], m.a["w1_1"]).then_inc(loaded, 16)
            sp.dma_start(m.w2[:, :], m.a["w2_1"]).then_inc(loaded, 16)
            sp.wait_ge(loaded, 32)


def experts(m, name, layer):
    nc, ps = m.nc, m.ps
    T4, GROUPS = 4, TILES // 4
    s = {n: m.sem(name + "_" + n) for n in ("comb", "combT_ps", "combT", "bias_ps", "h", "a", "y_ps", "added", "biased")}
    tail = Tail(m, name, [sinks(m, "z")])
    gelu = ACT.Gelu_apprx_tanh if layer == 0 else ACT.Gelu
    ident = m.const[:, C_ID:C_ID + P]
    biased = layer == 0
    with ExitStack() as own, nc.Block() as block:
        sb = lambda n, shape: own.enter_context(nc.sbuf_tensor(name + "_" + n, shape, F32))
        a = sb("a", [P, 4, T4 * P])
        comb, combT = sb("comb", [P, T4, E]), sb("combT", [E, T4, P])
        bank_h = lambda k: ps[k % 3]
        bank_y = lambda e: ps[3 + e % 2]

        def over_groups(eng, work):
            work(0, True)
            with eng.Fori(1, GROUPS) as q:
                work(q, False)

        @block.tensor
        def _(pe):
            def work(q, first):
                def fc1(k):
                    if k >= 3 or not first:
                        pe.wait_ge(s["a"], q * E * FC + k + 1 - 3)
                    nc.tensor.matmul(bank_h(k)[:, :], m.w1[:, k * P:(k + 1) * P],
                                     m.QV[:, DS(q * T4 * P, T4 * P)], start=True, stop=True).then_inc(s["h"], 1)

                def fc2(k):
                    e, f = k // FC, k % FC
                    pe.wait_ge(s["a"], q * E * FC + k + 1)
                    if f == 0 and (e >= 2 or not first):
                        pe.wait_ge(s["added"], (q * E + e + 1 - 2) * T4)
                    for j in range(T4):
                        last = nc.tensor.matmul(bank_y(e)[:, j * P:(j + 1) * P], a[:, k % 4, j * P:(j + 1) * P],
                                                m.w2[:, k * D:(k + 1) * D], start=(f == 0 and j == 0),
                                                stop=(f == FC - 1), skip_group_check=True)
                    last.then_inc(s["y_ps"], 1)
                if biased:
                    pe.wait_ge(s["comb"], q + 1)
                    if not first:
                        pe.wait_ge(s["combT"], q)
                        pe.wait_ge(s["biased"], q * T4)
                    for j in range(T4):
                        last = nc.tensor.transpose(ps[5][0:E, j * P:(j + 1) * P], comb[:, j, :], ident)
                    last.then_inc(s["combT_ps"], 1)
                    pe.wait_ge(s["combT"], q + 1)
                    for j in range(T4):
                        last = nc.tensor.matmul(ps[6][:, j * P:(j + 1) * P], combT[:, j, :], m.b2[:, :],
                                                start=True, stop=True)
                    last.then_inc(s["bias_ps"], 1)
                for k in range(E * FC):
                    fc1(k)
                    if k >= 2:
                        fc2(k - 2)
                fc2(E * FC - 2)
                fc2(E * FC - 1)
            over_groups(pe, work)

        @block.scalar
        def _(act):
            def work(q, first):
                if biased:
                    act.wait_ge(s["combT_ps"], q + 1)
                    if not first:
                        act.wait_ge(s["bias_ps"], q)
                    nc.scalar.activation(combT[:, :, :], ps[5][0:E, :].rearrange("p (j n) -> p j n", j=T4),
                                         ACT.Copy).then_inc(s["combT"], 1)
                for k in range(E * FC):
                    act.wait_ge(s["h"], q * E * FC + k + 1)
                    if k >= 4 or not first:
                        act.wait_ge(s["y_ps"], q * E * FC + k + 1 - 4)
                    more = dict(bias=m.b1[:, k:k + 1]) if biased else {}
                    nc.scalar.activation(a[:, k % 4, :], bank_h(k)[:, :], gelu, **more).then_inc(s["a"], 1)
            over_groups(act, work)

        @block.vector
        def _(dve):
            def work(q, first):
                x = lambda j: m.X[:, DS(q * T4 * P + j * P, P)]
                if not first:
                    dve.wait_ge(s["added"], q * E * T4)
                    if biased:
                        dve.wait_ge(s["combT_ps"], q)
                nc.vector.tensor_scalar(comb[:, :, :].rearrange("p j e -> p (j e)"),
                                        m.comb[:, :, :].rearrange("p t e -> p (t e)")[:, DS(q * T4 * E, T4 * E)],
                                        1.0, None, ALU.mult).then_inc(s["comb"], 1)
                dve.wait_ge(s["comb"], q + 1)
                if biased:
                    dve.wait_ge(s["bias_ps"], q + 1)
                    for j in range(T4):
                        nc.vector.tensor_tensor(x(j), ps[6][:, j * P:(j + 1) * P], x(j), ALU.add).then_inc(s["biased"], 1)
                for e in range(E):
                    dve.wait_ge(s["y_ps"], (q * E + e + 1) * FC)
                    if e:
                        dve.wait_ge(s["added"], (q * E + e) * T4)
                    elif biased:
                        dve.wait_ge(s["biased"], (q + 1) * T4)
                    for j in range(T4):
                        last = nc.vector.scalar_tensor_tensor(x(j), bank_y(e)[:, j * P:(j + 1) * P], comb[:, j, e:e + 1],
                                                              x(j), ALU.mult, ALU.add).then_inc(s["added"], 1)
                dve.wait_ge(s["added"], (q + 1) * E * T4)
                for j in range(T4):
                    t = Group(q, j, first)
                    nc.vector.memset(m.gate[:, 3:4], 0.0).then_inc(tail.x_new, 1)
                    tail.dve(dve, t)
            over_groups(dve, work)

        @block.gpsimd
        def _(pool):
            def work(q, first):
                for j in range(T4):
                    tail.pool(pool, Group(q, j, first))
            over_groups(pool, work)


class Group(Tile):

    def __init__(self, q, j, first):
        self.half, self.par, self.known, self.live = q * 2 + j // 2, j % 2, first, True


def experts_one(m):
    prepare_experts(m)
    route(m, "p5r", 0)
    m.end_pass()
    experts(m, "p5", 0)


def experts_two(m):
    load_layer_one_experts(m)
    route(m, "p9r", 1)
    m.end_pass()
    experts(m, "p9", 1)


def build(nc, a, out, upto=99):
    m = Chip()
    m.nc = nc
    with ExitStack() as ctx:
        in_use = []

        def sem(name):
            in_use.append(nc.alloc_semaphore(name=name))
            return in_use[-1]

        def end_pass():
            nc.clear_and_free_semaphores(in_use)
            in_use.clear()
            nc.all_engine_barrier()

        m.sem, m.end_pass = sem, end_pass
        sb = lambda name, shape, dt=F32: ctx.enter_context(nc.sbuf_tensor("sb_" + name, shape, dt))
        m.ps = [ctx.enter_context(nc.psum_tensor(f"bank{n}", [P, 512], F32)) for n in range(8)]
        m.X = sb("X", [P, TILES * D])
        m.MEAN, m.RZ, m.RN = sb("MEAN", [P, TILES]), sb("RZ", [P, TILES]), sb("RN", [P, TILES])
        m.const = sb("const", [P, C_ALL])
        m.bnst, m.mv, m.rstd = sb("bnst", [P, 2, 6]), sb("mv", [P, 2, 2]), sb("rstd", [P, 4])
        m.gate = sb("gate", [P, 4])
        m.M0, m.N0, m.c0 = sb("M0", [P, D]), sb("N0", [P, D]), sb("c0", [P, 1])
        m.b0, m.bA, m.bX = sb("b0", [P, D]), sb("bA", [P, D]), sb("bX", [P, D])
        m.ptab = sb("ptab", [P, H, 1 + LEN])
        m.QV = sb("QV", [P, TILES * P])
        m.comb, m.alpha = sb("comb", [P, TILES, E]), sb("alpha", [P, E])
        m.w1, m.w2 = sb("w1", [P, E * F]), sb("w2", [P, E * F])
        m.b1, m.b2 = sb("b1", [P, E * FC]), sb("b2", [E, D])
        m.a = a
        m.bqu = sb("bqu", [P, 2])
        m.cols, m.rows = sb("cols", [P, len(COLS)]), sb("rows", [1, 3 * D])
        m.colidx = {n: k for k, n in enumerate(COLS)}
        m.c_bq0 = m.colidx["bq0"]
        m.w = {n: sb("w_" + n, [P, w]) for n, w in WEIGHTS.items()}
        m.setup_loads = [(m.const[:, :], a["const"]), (m.cols[:, :], a["cols"]), (m.rows[:, :], a["rows"])]
        m.setup_loads += [(m.w[n][:, :], a[n]) for n in WEIGHTS]
        m.x_dram = a["x"].rearrange("(t b) i d -> t (b i) d", b=B4)
        m.ctxT_dram, m.ctxN_dram = a["ctxT"], a["ctxN"]
        m.bd_dram = nc.dram_tensor("bd_scores", [SEQS, LEN, H * LEN], F32).ap()
        passes = [setup_pass, cross_one_head, relative_project, relative_scores, relative_attention,
                  experts_one, cross_many_heads, causal_attention, experts_two]
        for f in passes[:upto]:
            f(m)
            m.end_pass()
        stored = m.sem("stored")
        with nc.Block() as block:
            @block.sync
            def _(sp):
                sp.dma_start(out.rearrange("(t b) i d -> (b i) t d", b=B4),
                             m.X[:, :].rearrange("p (t d) -> p t d", d=D)).then_inc(stored, 16)
                sp.wait_ge(stored, 16)


COLS = ("bq0", "bv0", "bv_a", "bq_a", "bk_a", "u", "v", "gamma", "beta", "norm_w")
WEIGHTS = {"Wq0": 128, "Wk0": 128, "Wv0": 128, "Wo0T": 128, "Wq_a": 128, "Wk_a": 128, "Wv_a": 128,
           "Wpos": 128, "Wf": 128, "WqT_x": 128, "WkT_x": 128, "WvT_x": 128, "WoT_x": 128,
           "w_q": 128, "w_k": 128, "w_v": 128, "w_o": 128}


def lay_out(i):
    f = {k: np.asarray(v) for k, v in i.items()}
    ctx = f["ctx_1024"]
    order = np.concatenate([np.arange(c, CTX, 3) for c in range(3)])
    padded = np.concatenate([ctx, np.zeros((SEQS, 1, D), np.float32)], 1)
    a = {
        "x": f["x"],
        "ctxT": ctx[:, order].transpose(2, 0, 1).reshape(D, SEQS * CTX),
        "ctxN": padded.reshape(TILES, B4, KC, 3, D).transpose(0, 2, 1, 3, 4).reshape(TILES, KC, B4 * 3 * D),
        "const": shape_constants(),
        "cols": np.stack([f["L0_xattn_bq"], f["L0_xattn_bv"], f["L0_attn_bv"], f["L0_attn_bq"], f["L0_attn_bk"],
                          f["L0_attn_u"].reshape(-1), f["L0_attn_v"].reshape(-1), f["L0_attn_gamma"],
                          f["L0_attn_beta"], f["L1_attn_norm_w"]], 1),
        "rows": np.concatenate([f["L0_xattn_bo"], f["L0_attn_bf"], f["L1_xattn_bo"]])[None],
        "Wq0": f["L0_xattn_Wq"], "Wk0": f["L0_xattn_Wk"], "Wv0": f["L0_xattn_Wv"], "Wo0T": f["L0_xattn_Wo"].T,
        "Wq_a": f["L0_attn_Wq"], "Wk_a": f["L0_attn_Wk"], "Wv_a": f["L0_attn_Wv"], "Wpos": f["L0_attn_Wpos"],
        "Wf": f["L0_attn_Wf"],
        "WqT_x": f["L1_xattn_Wq"].T, "WkT_x": f["L1_xattn_Wk"].T, "WvT_x": f["L1_xattn_Wv"].T,
        "WoT_x": f["L1_xattn_Wo"].T,
        "w_q": f["L1_attn_w_q"], "w_k": np.tile(f["L1_attn_w_k"], (1, G)),
        "w_v": np.tile(f["L1_attn_w_v"], (1, G)), "w_o": f["L1_attn_w_o"],
    }
    a.update(lay_out_experts(f))
    return {k: np.ascontiguousarray(v) for k, v in a.items()}


def kernel(**inputs):
    import concourse.bacc as bacc
    from concourse.bass_utils import run_bass_kernel_spmd

    arrays = lay_out(inputs)
    nc = bacc.Bacc("TRN2", target_bir_lowering=False, num_devices=1)
    views = {k: nc.dram_tensor(k, v.shape, mybir.dt.from_np(v.dtype), kind="ExternalInput").ap()
             for k, v in arrays.items()}
    out = nc.dram_tensor("latents_out", (SEQS, LEN, D), F32, kind="ExternalOutput").ap()
    build(nc, views, out)
    return run_bass_kernel_spmd(nc, [arrays], core_ids=[0]).results[0]["latents_out"]
```

```python
from contextlib import ExitStack

import numpy as np

import concourse.bass as bass
from concourse import mybir
from concourse.alu_op_type import AluOpType as ALU

F32 = mybir.dt.float32
I32 = mybir.dt.int32
U32 = mybir.dt.uint32
ACT = mybir.ActivationFunctionType
AX = mybir.AxisListType
DS = bass.ds

P = 128
D = 128
SEQS, LEN = 128, 32
CTX = 257
B4 = P // LEN
TILES = SEQS // B4
HALF = TILES // 2
H, HD = 16, 8
G, H4 = 4, 4
KC = 86
CHUNKS = ((0, 86), (86, 86), (172, 85))
E, F, FC = 8, 512, 4
TOPK = 2
TOKENS = SEQS * LEN
REGION = TOKENS + P
SPARE = E * REGION
JOBS = TOPK * TOKENS // P + E
LN_EPS = 1e-5
RMS_EPS = 1.1920929e-07
MASKED = -1.0e30
AROUND = 8

C_ID, C_M16, C_M4G, C_M4P, C_R4 = 0, 128, 144, 148, 152
C_CAUSAL, C_ROPE, C_PE, C_IOTA = 184, 216, 248, 280
C_TRI, C_ONES = 288, 416
C_JOB, C_BASE = 544, 544 + JOBS
C_POW = C_BASE + E
C_Z, C_LN, C_RMS = C_POW + 1, C_POW + 3, C_POW + 5
C_ALL = C_POW + 7


def shape_constants():
    c = np.zeros((P, C_ALL), np.float32)
    p = np.arange(P)
    c[:, C_ID:C_ID + P] = np.eye(P)
    c[p, C_M16 + p // HD] = 1.0
    c[p, C_M4G + (p // HD) % H4] = 1.0
    c[p, C_M4P + p // LEN] = 1.0
    c[p, C_R4 + p % LEN] = 1.0
    i, j = p[:, None] % LEN, np.arange(LEN)[None, :]
    c[:, C_CAUSAL:C_CAUSAL + LEN] = np.where(j <= i, 0.0, MASKED)
    d = np.arange(HD)
    theta = np.power(np.float32(10000.0), (-2.0 * (d // 2) / HD).astype(np.float32)).astype(np.float32)
    ang = np.arange(LEN, dtype=np.float32)[:, None] * theta[None, :]
    sign = np.where(np.arange(LEN) % 2 == 0, -1.0, 1.0)[:, None]
    rope = (np.cos(ang) + np.sin(ang) * sign).astype(np.float32)
    c[:, C_ROPE:C_ROPE + LEN] = rope.T[p % HD]
    inv = (1.0 / 10000.0 ** (np.arange(0.0, D, 2.0) / D)).astype(np.float32)
    pa = np.arange(LEN, dtype=np.float32)[:, None] * inv[None, :]
    pe = np.zeros((LEN, D), np.float32)
    pe[:, 0::2], pe[:, 1::2] = np.sin(pa), np.cos(pa)
    c[:, C_PE:C_PE + LEN] = pe.T
    c[:, C_IOTA:C_IOTA + E] = np.arange(E)
    c[:, C_TRI:C_TRI + P] = (p[:, None] < p[None, :])
    c[:, C_ONES:C_ONES + P] = 1.0
    c[:, C_JOB:C_JOB + JOBS] = np.arange(JOBS) * P
    c[:, C_BASE:C_BASE + E] = np.arange(E) * REGION
    c[:, C_POW] = -0.5
    c[:, C_Z:C_Z + 2] = 1.0, LN_EPS
    c[:, C_LN:C_LN + 2] = 1.0 + LN_EPS, LN_EPS * LN_EPS
    c[:, C_RMS:C_RMS + 2] = 1.0 + RMS_EPS, RMS_EPS * LN_EPS
    return c



class Tile:

    def __init__(self, step, p, stage, halves=HALF, unroll=2):
        self.half, self.par, self.unroll = step + (p - stage) // unroll, (p - stage) % unroll, unroll
        self.two = self.par % 2
        self.known = isinstance(step, int)
        self.live = not self.known or 0 <= self.half < halves

    @property
    def n(self):
        return self.half * self.unroll + self.par

    def cols(self, width=P):
        return DS(self.n * width, width) if not self.known else slice(self.n * width, (self.n + 1) * width)

    def nth(self, each=1):
        return (self.n + 1) * each

    def nth_of_pair(self, each=1):
        return (self.half + 1) * each

    def past(self, back=1):
        return not self.known or self.n >= back

    def unit(self, u, back=0, each=16):
        return self.n * each + u + 1 - back

    def past_unit(self, u, back, each=16):
        return not self.known or self.n * each + u >= back

    def before(self, back=1, each=1):
        return (self.n + 1 - back) * each


def over_tiles(eng, stages, work, halves=HALF, unroll=2):
    if unroll > 2:
        halves = halves * 2 // unroll
    lag = -(-stages // unroll)
    first = lag + 1
    for step in range(first):
        for p in range(unroll):
            work(lambda s, a=step, b=p: Tile(a, b, s, halves, unroll))
    with eng.Fori(first, halves) as step:
        for p in range(unroll):
            work(lambda s, a=step, b=p: Tile(a, b, s, halves, unroll))
    for step in range(halves, halves + lag):
        for p in range(unroll):
            work(lambda s, a=step, b=p: Tile(a, b, s, halves, unroll))





class Tail:

    def __init__(self, m, name, forms):
        self.m, self.forms = m, forms
        self.x_new = m.sem(name + "_x_new")
        self.stats_done = m.sem(name + "_stats_done")
        self.mv_ready = m.sem(name + "_mv_ready")
        self.kept = m.sem(name + "_mv_kept")
        self.pool_step = m.sem(name + "_norm_step")
        self.steps = 1 + 3 * len(forms)

    def dve(self, dve, t):
        m, nc = self.m, self.m.nc
        dve.wait_ge(self.x_new, t.nth())
        nc.vector.memset(m.gate[:, 0:1], 0.0)
        nc.vector.bn_stats(m.bnst[:, t.par, :], m.X[:, t.cols()]).then_inc(self.stats_done, 1)
        dve.wait_ge(self.stats_done, t.nth())
        if t.past(2):
            dve.wait_ge(self.pool_step, t.before(2, self.steps))
        nc.vector.memset(m.gate[:, 1:2], 0.0)
        nc.vector.bn_aggr(m.mv[:, t.par, :], m.bnst[:, t.par, :]).then_inc(self.mv_ready, 1)

    def dve_all(self, dve, t):
        m, nc = self.m, self.m.nc
        dve.wait_ge(self.x_new, t.nth())
        nc.vector.memset(m.gate[:, 0:1], 0.0)
        nc.vector.bn_stats(m.bnst[:, t.two, :], m.X[:, t.cols()]).then_inc(self.stats_done, 1)
        dve.wait_ge(self.stats_done, t.nth())
        nc.vector.memset(m.gate[:, 1:2], 0.0)
        nc.vector.bn_aggr(m.mv[:, t.two, :], m.bnst[:, t.two, :]).then_inc(self.mv_ready, 1)
        dve.wait_ge(self.mv_ready, t.nth())
        nc.vector.tensor_scalar(m.mv_all[:, t.cols(2)], m.mv[:, t.two, :], 1.0, None, ALU.mult).then_inc(self.kept, 1)

    def pool_all(self, pool):
        m, nc = self.m, self.m.nc
        pool.wait_ge(self.kept, TILES)
        mv = m.mv_all[:, :].rearrange("p (t k) -> p t k", k=2)
        f = m.factor[:, :]
        const = lambda k: m.const[:, k:k + 1].broadcast_to([P, TILES])
        step = 0
        for out, a, b in self.forms:
            for dst, x, y, op in ((f, mv[:, :, 1], a, ALU.mult), (f, f, b, ALU.add), (out[:, :], f, C_POW, ALU.pow)):
                if step:
                    pool.wait_ge(self.pool_step, step)
                nc.gpsimd.tensor_tensor(dst, x, const(y), op).then_inc(self.pool_step, 1)
                step += 1
        nc.gpsimd.tensor_tensor(m.MEAN[:, :], mv[:, :, 0], const(C_ONES), ALU.mult).then_inc(self.pool_step, 1)

    def pool(self, pool, t):
        m, nc = self.m, self.m.nc
        pool.wait_ge(self.mv_ready, t.nth())
        step = t.before(1, self.steps)
        if t.past():
            pool.wait_ge(self.pool_step, step)
        mv = m.mv[:, t.par, :]
        for out, a, b in self.forms:
            r = m.rstd[:, 0:1]
            for n, (dst, x, y, op) in enumerate(((r, mv[:, 1:2], a, ALU.mult), (r, r, b, ALU.add),
                                                 (out[:, t.cols(1)], r, C_POW, ALU.pow))):
                nc.gpsimd.tensor_tensor(dst, x, m.const[:, y:y + 1], op).then_inc(self.pool_step, 1)
                step = step + 1
                pool.wait_ge(self.pool_step, step)
        nc.gpsimd.tensor_tensor(m.MEAN[:, t.cols(1)], mv[:, 0:1], m.const[:, C_ONES:C_ONES + 1],
                                ALU.mult).then_inc(self.pool_step, 1)


def normed(m, out, t, factor):
    return m.nc.vector.tensor_scalar(out, m.X[:, t.cols()], m.MEAN[:, t.cols(1)], factor[:, t.cols(1)],
                                     ALU.subtract, ALU.mult)


class Chip:
    pass


def sinks(m, which):
    return {"z": (m.RZ, C_Z, C_Z + 1), "ln": (m.RN, C_LN, C_LN + 1), "rms": (m.RN, C_RMS, C_RMS + 1)}[which]


def setup_pass(m):
    nc = m.nc
    loaded = m.sem("weights_loaded")
    x_in = [m.sem("x_in_a"), m.sem("x_in_b")]
    folded = m.sem("folded")
    evac = m.sem("fold_evacuated")
    zeroed = m.sem("setup_zeroed")
    tail = Tail(m, "setup", [sinks(m, "z")])
    loads = m.setup_loads
    c = m.const
    ones_row = c[0:1, C_ONES:C_ONES + P]
    ws = m.w

    with nc.Block() as block:
        @block.sync
        def _(sp):
            for n in range(2):
                sp.dma_start(m.X[:, n * 2048:(n + 1) * 2048].rearrange("p (t d) -> p t d", d=D),
                             m.x_dram[n * 16:(n + 1) * 16].rearrange("t p d -> p t d")).then_inc(x_in[n], 16)
            for dst, src in loads:
                sp.dma_start(dst, src).then_inc(loaded, 16)

        @block.tensor
        def _(pe):
            pe.wait_ge(loaded, 16 * len(loads))
            mm = nc.tensor.matmul
            one = dict(start=True, stop=True)
            mm(m.ps[0][:, 0:D], ws["Wq0"][:, :], ws["Wk0"][:, :], **one)
            mm(m.ps[0][:, D:D + 1], ws["Wk0"][:, :], m.cols[:, m.c_bq0:m.c_bq0 + 1], **one)
            mm(m.ps[1][:, 0:D], ws["Wv0"][:, :], ws["Wo0T"][:, :], **one).then_inc(folded, 1)
            bias = [("bv0", "Wo0T", 0), ("bv_a", "Wf", 1), (None, None, 2)]
            for n, (vec, wt, row) in enumerate(bias):
                dst = m.ps[2 + n][:, 0:D]
                if vec:
                    k = m.colidx[vec]
                    mm(dst, m.cols[:, k:k + 1].broadcast_to([D, P]), ws[wt][:, :], start=True, stop=False)
                mm(dst, ones_row, m.rows[0:1, row * D:(row + 1) * D], start=not vec, stop=True).then_inc(folded, 1)
            mm(m.ps[5][:, 0:LEN], ws["Wpos"][:, :], c[:, C_PE:C_PE + LEN], **one).then_inc(folded, 1)

        @block.vector
        def _(dve):
            nc.vector.memset(m.ptab[:, :, :], 0.0).then_inc(zeroed, 1)
            for half in range(2):
                dve.wait_ge(x_in[half], 16)
                for n in range(16 * half, 16 * half + 16):
                    t = Tile(n // 2, n % 2, 0)
                    nc.vector.memset(m.gate[:, 2:3], 0.0).then_inc(tail.x_new, 1)
                    tail.dve_all(dve, t)
            dve.wait_ge(folded, 5)
            dve.wait_ge(zeroed, 1)
            s0 = float(D) ** -0.5
            nc.vector.tensor_scalar(m.M0[:, :], m.ps[0][:, 0:D], 1.0, None, ALU.mult).then_inc(evac, 1)
            nc.vector.tensor_scalar(m.c0[:, :], m.ps[0][:, D:D + 1], s0, None, ALU.mult).then_inc(evac, 1)
            nc.vector.tensor_copy(m.N0[:, :], m.ps[1][:, 0:D]).then_inc(evac, 1)
            for n, dst in enumerate((m.b0, m.bA, m.bX)):
                nc.vector.tensor_copy(dst[:, :], m.ps[2 + n][:, 0:D]).then_inc(evac, 1)
            nc.vector.tensor_tensor(
                m.ptab[:, :, 1:1 + LEN],
                m.ps[5][:, 0:LEN].unsqueeze(1).broadcast_to([P, H, LEN]),
                c[:, C_M16:C_M16 + H].unsqueeze(2).broadcast_to([P, H, LEN]), ALU.mult).then_inc(evac, 1)
            for k, (a, b) in enumerate(((m.colidx["bq_a"], m.colidx["u"]), (m.colidx["bq_a"], m.colidx["v"]))):
                nc.vector.tensor_tensor(m.bqu[:, k:k + 1], m.cols[:, a:a + 1], m.cols[:, b:b + 1],
                                        ALU.add).then_inc(evac, 1)

        @block.gpsimd
        def _(pool):
            pool.wait_ge(loaded, 16 * len(loads))
            tail.pool_all(pool)


def cross_one_head(m):
    nc = m.nc
    ctx_in = [m.sem("p1_ctx_in_a"), m.sem("p1_ctx_in_b")]
    rows_in = [m.sem("p1_rows_in_a"), m.sem("p1_rows_in_b")]
    s = {n: m.sem("p1_" + n) for n in (
        "zT_ps", "zT", "q_ps", "q", "scores", "maxed", "probs", "pT_ps", "pT", "o_ps", "o", "oT_ps", "oT", "y_ps",
        "recip", "xb", "z")}
    tail = Tail(m, "p1", [sinks(m, "ln")])
    ident = m.const[:, C_ID:C_ID + P]
    ps = m.ps
    s0 = float(D) ** -0.5
    with ExitStack() as own, nc.Block() as block:
        sb = lambda n, shape: own.enter_context(nc.sbuf_tensor("p1_" + n, shape, F32))
        ctxT = sb("ctxT", [P, 2, B4, CTX])
        ctxN = sb("ctxN", [KC, 2, B4, 3, D])
        z, o, zT, qT, oT = sb("z", [P, 2, D]), sb("o", [P, 2, D]), sb("zT", [P, 2, P]), sb("qT", [P, 2, P]), sb("oT", [P, 2, P])
        prob = sb("prob", [P, 2, CTX])
        pT = sb("pT", [KC, 2, 3, P])
        xb = sb("xb", [P, 2, D])
        nmax, total, recip = sb("nmax", [P, 2]), sb("total", [P, 4]), sb("recip", [P, 2])
        STAGES = 6

        @block.sync
        def _(sp):
            def work(at):
                t = at(2)
                if t.live:
                    if t.past(2):
                        sp.wait_ge(s["o_ps"], t.before(2))
                    sp.dma_start(ctxN[:, t.par], m.ctxN_dram[DS(t.n, 1)].rearrange(
                        "a p (b c d) -> p (a b) c d", b=B4, c=3)).then_inc(rows_in[t.par], 16)
                t = at(0)
                if t.live:
                    if t.past(2):
                        sp.wait_ge(s["scores"], t.before(2))
                    sp.dma_start(ctxT[:, t.par], m.ctxT_dram[:, t.cols(B4 * CTX)].rearrange(
                        "d (b k) -> d b k", k=CTX)).then_inc(ctx_in[t.par], 16)
            over_tiles(sp, 2, work)

        @block.tensor
        def _(pe):
            def work(at):
                t = at(2)
                if t.live:
                    pe.wait_ge(s["q"], t.nth())
                    pe.wait_ge(ctx_in[t.par], t.nth_of_pair(16))
                    if t.past(2):
                        pe.wait_ge(s["probs"], t.before(2))
                    for b in range(B4):
                        last = nc.tensor.matmul(ps[3 + t.par][b * LEN:(b + 1) * LEN, 0:CTX],
                                                qT[:, t.par, b * LEN:(b + 1) * LEN], ctxT[:, t.par, b, :],
                                                start=True, stop=True, tile_position=(0, b * LEN))
                    last.then_inc(s["scores"], 1)
                t = at(3)
                if t.live:
                    pe.wait_ge(s["probs"], t.nth())
                    if t.past():
                        pe.wait_ge(s["pT"], t.before())
                    for c, (k0, rows) in enumerate(CHUNKS):
                        last = nc.tensor.transpose(ps[5][:rows, c * P:(c + 1) * P], prob[:, t.par, k0:k0 + rows], ident)
                    last.then_inc(s["pT_ps"], 1)
                t = at(1)
                if t.live:
                    pe.wait_ge(s["zT"], t.nth())
                    if t.past():
                        pe.wait_ge(s["q"], t.before())
                    nc.tensor.matmul(ps[2][:, 0:P], m.M0[:, :], zT[:, t.par, :], start=True, stop=True).then_inc(s["q_ps"], 1)
                t = at(0)
                if t.live:
                    pe.wait_ge(s["z"], t.nth())
                    if t.past():
                        pe.wait_ge(s["zT"], t.before())
                    nc.tensor.transpose(ps[0][:, 0:P], z[:, t.par, :], ident).then_inc(s["zT_ps"], 1)
                t = at(6)
                if t.live:
                    pe.wait_ge(s["oT"], t.nth())
                    if t.past():
                        pe.wait_ge(tail.x_new, t.before())
                    nc.tensor.matmul(ps[7][:, 0:D], oT[:, t.par, :], m.N0[:, :], start=True, stop=True).then_inc(s["y_ps"], 1)
                t = at(5)
                if t.live:
                    pe.wait_ge(s["o"], t.nth())
                    if t.past():
                        pe.wait_ge(s["oT"], t.before())
                    nc.tensor.transpose(ps[1][:, 0:P], o[:, t.par, :], ident).then_inc(s["oT_ps"], 1)
                t = at(4)
                if t.live:
                    pe.wait_ge(s["pT"], t.nth())
                    pe.wait_ge(rows_in[t.par], t.nth_of_pair(16))
                    if t.past():
                        pe.wait_ge(s["o"], t.before())
                    for c, (_, rows) in enumerate(CHUNKS):
                        for b in range(B4):
                            last = nc.tensor.matmul(ps[6][b * LEN:(b + 1) * LEN, 0:D],
                                                    pT[:rows, t.par, c, b * LEN:(b + 1) * LEN],
                                                    ctxN[:rows, t.par, b, c, :], start=(c == 0), stop=(c == 2),
                                                    tile_position=(0, b * LEN))
                    last.then_inc(s["o_ps"], 1)
            over_tiles(pe, STAGES, work)

        @block.scalar
        def _(act):
            def work(at):
                t = at(2)
                if t.live:
                    act.wait_ge(s["maxed"], t.nth())
                    if t.past(2):
                        act.wait_ge(s["pT_ps"], t.before(2))
                        act.wait_ge(s["recip"], t.before(2))
                    nc.scalar.activation(prob[:, t.par, :], ps[3 + t.par][:, 0:CTX], ACT.Exp,
                                         bias=nmax[:, t.par:t.par + 1],
                                         accum_out=total[:, t.par:t.par + 1]).then_inc(s["probs"], 1)
                t = at(1)
                if t.live:
                    act.wait_ge(s["q_ps"], t.nth())
                    if t.past(2):
                        act.wait_ge(s["scores"], t.before(2))
                    nc.scalar.activation(qT[:, t.par, :], ps[2][:, 0:P], ACT.Identity, scale=s0,
                                         bias=m.c0[:, 0:1]).then_inc(s["q"], 1)
                t = at(0)
                if t.live:
                    act.wait_ge(s["zT_ps"], t.nth())
                    if t.past(2):
                        act.wait_ge(s["q_ps"], t.before(2))
                    nc.scalar.activation(zT[:, t.par, :], ps[0][:, 0:P], ACT.Copy).then_inc(s["zT"], 1)
                t = at(5)
                if t.live:
                    act.wait_ge(s["oT_ps"], t.nth())
                    if t.past(2):
                        act.wait_ge(s["y_ps"], t.before(2))
                    nc.scalar.activation(oT[:, t.par, :], ps[1][:, 0:P], ACT.Copy).then_inc(s["oT"], 1)
                t = at(4)
                if t.live:
                    act.wait_ge(s["o_ps"], t.nth())
                    act.wait_ge(s["recip"], t.nth())
                    if t.past(2):
                        act.wait_ge(s["oT_ps"], t.before(2))
                    nc.scalar.activation(o[:, t.par, :], ps[6][:, 0:D], ACT.Copy,
                                         scale=recip[:, t.par:t.par + 1]).then_inc(s["o"], 1)
            over_tiles(act, STAGES, work)

        @block.vector
        def _(dve):
            def work(at):
                t = at(2)
                if t.live:
                    dve.wait_ge(s["scores"], t.nth())
                    if t.past(2):
                        dve.wait_ge(s["probs"], t.before(2))
                    nc.vector.tensor_reduce(nmax[:, t.par:t.par + 1], ps[3 + t.par][:, 0:CTX], AX.X, ALU.max,
                                            negate=True).then_inc(s["maxed"], 1)
                t = at(3)
                if t.live:
                    dve.wait_ge(s["pT_ps"], t.nth())
                    if t.past(2):
                        dve.wait_ge(s["o_ps"], t.before(2))
                    nc.vector.tensor_copy(pT[:85, t.par, 2, :], ps[5][:85, 2 * P:3 * P])
                    nc.vector.tensor_copy(pT[:KC, t.par, 0:2, :], ps[5][:KC, 0:2 * P]).then_inc(s["pT"], 1)
                    if t.past(2):
                        dve.wait_ge(s["o"], t.before(2))
                    nc.vector.reciprocal(recip[:, t.par:t.par + 1], total[:, t.par:t.par + 1]).then_inc(s["recip"], 1)
                t = at(0)
                if t.live:
                    if t.past(2):
                        dve.wait_ge(s["zT_ps"], t.before(2))
                    normed(m, z[:, t.par, :], t, m.RZ).then_inc(s["z"], 1)
                t = at(6)
                if t.live:
                    dve.wait_ge(s["y_ps"], t.nth())
                    dve.wait_ge(s["xb"], t.nth())
                    nc.vector.tensor_tensor(m.X[:, t.cols()], ps[7][:, 0:D], xb[:, t.par, :],
                                            ALU.add).then_inc(tail.x_new, 1)
                    tail.dve(dve, t)
            over_tiles(dve, STAGES, work)

        @block.gpsimd
        def _(pool):
            def work(at):
                t = at(4)
                if t.live:
                    if t.past(2):
                        pool.wait_ge(tail.x_new, t.before(2))
                    nc.gpsimd.tensor_tensor(xb[:, t.par, :], m.X[:, t.cols()], m.b0[:, :], ALU.add).then_inc(s["xb"], 1)
                t = at(6)
                if t.live:
                    tail.pool(pool, t)
            over_tiles(pool, STAGES, work)


def relative_project(m):
    nc, ps = m.nc, m.ps
    s = {n: m.sem("p2_" + n) for n in ("z", "zT_ps", "zT", "q_ps", "q")}
    ident = m.const[:, C_ID:C_ID + P]
    gamma, beta = m.colidx["gamma"], m.colidx["beta"]
    with ExitStack() as own, nc.Block() as block:
        sb = lambda n, shape: own.enter_context(nc.sbuf_tensor("p2_" + n, shape, F32))
        z, zT = sb("z", [P, 2, D]), sb("zT", [P, 2, P])

        @block.vector
        def _(dve):
            def work(at):
                t = at(0)
                if t.live:
                    if t.past(2):
                        dve.wait_ge(s["zT_ps"], t.before(2))
                    normed(m, z[:, t.par, :], t, m.RN).then_inc(s["z"], 1)
                t = at(2)
                if t.live:
                    dve.wait_ge(s["q_ps"], t.nth())
                    nc.vector.tensor_scalar(m.QV[:, t.cols()], ps[2 + t.par][:, 0:P], m.bqu[:, 1:2], None,
                                            ALU.add).then_inc(s["q"], 1)
            over_tiles(dve, 2, work)

        @block.scalar
        def _(act):
            def work(at):
                t = at(1)
                if t.live:
                    act.wait_ge(s["zT_ps"], t.nth())
                    if t.past(2):
                        act.wait_ge(s["q_ps"], t.before(2))
                    nc.scalar.activation(zT[:, t.par, :], ps[t.par][:, 0:P], ACT.Identity,
                                         scale=m.cols[:, gamma:gamma + 1],
                                         bias=m.cols[:, beta:beta + 1]).then_inc(s["zT"], 1)
            over_tiles(act, 2, work)

        @block.tensor
        def _(pe):
            def work(at):
                t = at(1)
                if t.live:
                    pe.wait_ge(s["z"], t.nth())
                    if t.past(2):
                        pe.wait_ge(s["zT"], t.before(2))
                    nc.tensor.transpose(ps[t.par][:, 0:P], z[:, t.par, :], ident).then_inc(s["zT_ps"], 1)
                t = at(2)
                if t.live:
                    pe.wait_ge(s["zT"], t.nth())
                    if t.past(2):
                        pe.wait_ge(s["q"], t.before(2))
                    nc.tensor.matmul(ps[2 + t.par][:, 0:P], m.w["Wq_a"][:, :], zT[:, t.par, :],
                                     start=True, stop=True).then_inc(s["q_ps"], 1)
            over_tiles(pe, 2, work)


def relative_scores(m):
    nc, ps = m.nc, m.ps
    done, moved, stored = m.sem("p3_done"), m.sem("p3_moved"), [m.sem(f"p3_stored{n}") for n in range(4)]
    moved_a = m.sem("p3_moved_a")
    with ExitStack() as own, nc.Block() as block:
        rows = own.enter_context(nc.sbuf_tensor("p3_rows", [P, 4, H * LEN], F32))

        @block.tensor
        def _(pe):
            for i in range(LEN):
                if i >= 8:
                    pe.wait_ge(moved_a if i % 2 else moved, (i - 8) // 2 + 1)
                bank = ps[i % 8][:, :].rearrange("p (h j) -> p h j", j=LEN)
                last = nc.tensor.matmul(bank[:, :, 0:i + 1], m.QV[:, i::LEN], m.ptab[:, :, LEN - i:LEN + 1],
                                        start=True, stop=(i == LEN - 1))
                if i < LEN - 1:
                    last = nc.tensor.matmul(bank[:, :, i + 1:LEN], m.QV[:, i + 1::LEN], m.ptab[:, :, 0:LEN - 1 - i],
                                            start=False, stop=True)
                last.then_inc(done, 1)

        @block.vector
        def _(dve):
            for i in range(0, LEN, 2):
                dve.wait_ge(done, i + 1)
                if i >= 4:
                    dve.wait_ge(stored[i % 4], 16 * (i // 4))
                nc.vector.tensor_copy(rows[:, i % 4, :], ps[i % 8][:, :]).then_inc(moved, 1)

        @block.scalar
        def _(act):
            for i in range(1, LEN, 2):
                act.wait_ge(done, i + 1)
                if i >= 4:
                    act.wait_ge(stored[i % 4], 16 * (i // 4))
                nc.scalar.activation(rows[:, i % 4, :], ps[i % 8][:, :], ACT.Copy).then_inc(moved_a, 1)

        @block.sync
        def _(sp):
            for i in range(LEN):
                sp.wait_ge(moved_a if i % 2 else moved, i // 2 + 1)
                sp.dma_start(m.bd_dram[:, i, :], rows[:, i % 4, :]).then_inc(stored[i % 4], 16)
            for n in range(4):
                sp.wait_ge(stored[n], 16 * (LEN // 4))


def self_attention(m, name, relative):
    nc, ps, c = m.nc, m.ps, m.const
    s = {n: m.sem(name + "_" + n) for n in (
        "z", "zT_ps", "zT", "qk_ps", "v_ps", "q", "k", "v", "k_dve", "k_pool", "scores", "summed", "maxed",
        "shifted", "probs", "pT_ps", "pT", "o_ps", "recip", "o", "oT_ps", "oT", "y_ps", "xb", "zres", "ones")}
    bd_in = [m.sem(name + "_bd_in_a"), m.sem(name + "_bd_in_b")]
    tail = Tail(m, name, [sinks(m, "z")] + ([sinks(m, "ln")] if relative else []))
    ident = c[:, C_ID:C_ID + P]
    col = lambda n: m.cols[:, m.colidx[n]:m.colidx[n] + 1]
    scale = float(D if relative else HD) ** -0.5
    STAGES = 5
    with ExitStack() as own, nc.Block() as block:
        sb = lambda n, shape: own.enter_context(nc.sbuf_tensor(name + "_" + n, shape, F32))
        z, qT, kT = (sb(n, [P, 2, P]) for n in ("z", "qT", "kT"))
        zT4 = sb("zT4", [P, 2, B4, H4, LEN])
        k_all = sb("k_all", [P, 2, B4, H, LEN])
        v_all = sb("v_all", [P, 2, B4 * G, H4, HD + 1])
        bd = sb("bd", [P, 2, H * LEN])
        score, prob = sb("score", [P, 2, H * LEN]), sb("prob", [P, 2, H * LEN])
        mx, recip = sb("mx", [P, 2, H]), sb("recip", [P, 2, H])
        pT = sb("pT", [P, 2, G, P])
        o, oT, xb, zres = (sb(n, [P, 2, P]) for n in ("o", "oT", "xb", "zres"))
        wq = m.w["Wq_a" if relative else "w_q"][:, :]
        if relative:
            wk, wv = m.w["Wk_a"][:, :], m.w["Wv_a"][:, :]
        else:
            wk, wv = m.w["w_k"][:, :], m.w["w_v"][:, :]
        wo = m.w["Wf" if relative else "w_o"][:, :]
        rope = c[:, C_ROPE:C_ROPE + LEN].unsqueeze(1).broadcast_to([P, B4, LEN])
        by_seq = lambda ap: ap.rearrange("p (b i) -> p b i", i=LEN)
        by_head = lambda ap: ap.rearrange("p (h j) -> p h j", j=LEN)

        @block.sync
        def _(sp):
            def work(at):
                t = at(2)
                if t.live:
                    if t.past(2):
                        sp.wait_ge(s["summed"], t.before(2))
                    sp.dma_start(bd[:, t.par, :], m.bd_dram.rearrange("s i n -> (s i) n")[t.cols(), :]
                                 ).then_inc(bd_in[t.par], 16)
            if relative:
                over_tiles(sp, 2, work)

        @block.tensor
        def _(pe):
            def work(at):
                t = at(3)
                if t.live:
                    pe.wait_ge(s["q"], t.nth())
                    pe.wait_ge(s["k_dve"], t.nth(2))
                    pe.wait_ge(s["k_pool"], t.nth(2))
                    if t.past(2):
                        pe.wait_ge(s["summed"], t.before(2))
                    for b in range(B4):
                        last = nc.tensor.matmul(ps[3 + t.par][b * LEN:(b + 1) * LEN, :],
                                                qT[:, t.par, b * LEN:(b + 1) * LEN], k_all[:, t.par, b],
                                                start=True, stop=True, tile_position=(0, b * LEN))
                    last.then_inc(s["scores"], 1)
                t = at(1)
                if t.live:
                    pe.wait_ge(s["zT"], t.nth())
                    if t.past():
                        pe.wait_ge(s["q"], t.before())
                        pe.wait_ge(s["k"], t.before())
                    nc.tensor.matmul(ps[1][:, 0:P], wq, zT4[:, t.par, :, 0, :], start=True, stop=True)
                    nc.tensor.matmul(ps[1][:, P:2 * P], wk, zT4[:, t.par, :, 0, :], start=True, stop=True).then_inc(s["qk_ps"], 1)
                t = at(4)
                if t.live:
                    pe.wait_ge(s["probs"], t.nth())
                    if t.past():
                        pe.wait_ge(s["pT"], t.before())
                    for g in range(G):
                        last = nc.tensor.transpose(ps[5][:, g * P:(g + 1) * P], prob[:, t.par, g * P:(g + 1) * P], ident)
                    last.then_inc(s["pT_ps"], 1)
                t = at(2)
                if t.live:
                    if t.past():
                        pe.wait_ge(s["v"], t.before())
                    for b in range(B4):
                        last = nc.tensor.matmul(ps[2][:, b * D:(b + 1) * D], zT4[:, t.par, b], wv, start=True, stop=True)
                    last.then_inc(s["v_ps"], 1)
                t = at(5)
                if t.live:
                    pe.wait_ge(s["o"], t.nth())
                    if t.past():
                        pe.wait_ge(tail.x_new, t.before())
                    nc.tensor.transpose(ps[7][:, P:2 * P], o[:, t.par, :], ident).then_inc(s["oT_ps"], 1)
                t = at(4)
                if t.live:
                    pe.wait_ge(s["pT"], t.nth())
                    pe.wait_ge(s["v"], t.nth())
                    if t.past():
                        pe.wait_ge(s["o"], t.before())
                    for b in range(B4):
                        for g in range(G):
                            w = H4 * (HD + 1)
                            last = nc.tensor.matmul(ps[6][b * LEN:(b + 1) * LEN, g * w:(g + 1) * w],
                                                    pT[:, t.par, g, b * LEN:(b + 1) * LEN],
                                                    v_all[:, t.par, b * G + g], start=True, stop=True,
                                                    tile_position=(0, b * LEN))
                    last.then_inc(s["o_ps"], 1)
                t = at(5)
                if t.live:
                    pe.wait_ge(s["oT"], t.nth())
                    nc.tensor.matmul(ps[7][:, 0:D], oT[:, t.par, :], wo, start=True, stop=True).then_inc(s["y_ps"], 1)
                t = at(0)
                if t.live:
                    pe.wait_ge(s["z"], t.nth())
                    if t.past():
                        pe.wait_ge(s["zT"], t.before())
                    nc.tensor.transpose(ps[0][:, 0:P], z[:, t.par, :], ident).then_inc(s["zT_ps"], 1)
            over_tiles(pe, STAGES, work)

        @block.scalar
        def _(act):
            def work(at):
                t = at(1)
                if t.live and relative:
                    act.wait_ge(s["qk_ps"], t.nth())
                    if t.past(2):
                        act.wait_ge(s["scores"], t.before(2))
                    nc.scalar.activation(qT[:, t.par, :], ps[1][:, 0:P], ACT.Identity,
                                         bias=m.bqu[:, 0:1]).then_inc(s["q"], 1)
                    if t.past(2):
                        act.wait_ge(s["k_dve"], t.before(2, 2))
                        act.wait_ge(s["k_pool"], t.before(2, 2))
                    nc.scalar.activation(kT[:, t.par, :], ps[1][:, P:2 * P], ACT.Identity,
                                         bias=col("bk_a")).then_inc(s["k"], 1)
                t = at(4)
                if t.live:
                    act.wait_ge(s["pT_ps"], t.nth())
                    if t.past(2):
                        act.wait_ge(s["o_ps"], t.before(2))
                    nc.scalar.activation(pT[:, t.par], ps[5][:, :].rearrange("p (g n) -> p g n", g=G),
                                         ACT.Copy).then_inc(s["pT"], 1)
                t = at(5)
                if t.live:
                    act.wait_ge(s["oT_ps"], t.nth())
                    if t.past(2):
                        act.wait_ge(s["y_ps"], t.before(2))
                    nc.scalar.activation(oT[:, t.par, :], ps[7][:, P:2 * P], ACT.Copy).then_inc(s["oT"], 1)
                t = at(3)
                if t.live:
                    act.wait_ge(s["shifted"], t.nth())
                    if t.past(2):
                        act.wait_ge(s["pT_ps"], t.before(2))
                    nc.scalar.activation(prob[:, t.par, :], score[:, t.par, :], ACT.Exp, scale=scale).then_inc(s["probs"], 1)
                t = at(0)
                if t.live:
                    act.wait_ge(s["zT_ps"], t.nth())
                    if t.past(2):
                        act.wait_ge(s["v_ps"], t.before(2))
                    four = by_seq(ps[0][:, 0:P]).unsqueeze(2).broadcast_to([P, B4, H4, LEN])
                    if relative:
                        nc.scalar.activation(zT4[:, t.par], four, ACT.Identity, scale=col("gamma"),
                                             bias=col("beta")).then_inc(s["zT"], 1)
                    else:
                        nc.scalar.activation(zT4[:, t.par], four, ACT.Copy,
                                             scale=col("norm_w")).then_inc(s["zT"], 1)
            over_tiles(act, STAGES, work)

        @block.vector
        def _(dve):
            def spread(t, b):
                return nc.vector.tensor_tensor(
                    k_all[:, t.par, b], kT[:, t.par, b * LEN:(b + 1) * LEN].unsqueeze(1).broadcast_to([P, H, LEN]),
                    c[:, C_M16:C_M16 + H].unsqueeze(2).broadcast_to([P, H, LEN]), ALU.mult)

            nc.vector.memset(v_all[:, :, :, :, :], 0.0).then_inc(s["ones"], 1)
            dve.wait_ge(s["ones"], 1)
            for par in range(2):
                nc.vector.tensor_copy(v_all[:, par, :, :, HD], c[:, C_M4P:C_M4P + H4].unsqueeze(1).broadcast_to(
                    [P, B4 * G, H4])).then_inc(s["ones"], 1)

            def work(at):
                t = at(2)
                if t.live:
                    dve.wait_ge(s["k"], t.nth())
                    if t.past(2):
                        dve.wait_ge(s["scores"], t.before(2))
                    for b in (0, 1):
                        spread(t, b).then_inc(s["k_dve"], 1)
                t = at(0)
                if t.live:
                    if t.past(2):
                        dve.wait_ge(s["zT_ps"], t.before(2))
                    normed(m, z[:, t.par, :], t, m.RN).then_inc(s["z"], 1)
                t = at(4)
                if t.live and not relative:
                    if t.past(2):
                        dve.wait_ge(s["xb"], t.before(2))
                    normed(m, zres[:, t.par, :], t, m.RZ).then_inc(s["zres"], 1)
                t = at(3)
                if t.live:
                    dve.wait_ge(s["scores"], t.nth())
                    if t.past(2):
                        dve.wait_ge(s["probs"], t.before(2))
                    if relative:
                        dve.wait_ge(bd_in[t.par], t.nth_of_pair(16))
                        more = by_head(bd[:, t.par, :])
                    else:
                        more = c[:, C_CAUSAL:C_CAUSAL + LEN].unsqueeze(1).broadcast_to([P, H, LEN])
                    nc.vector.tensor_tensor(by_head(score[:, t.par, :]), by_head(ps[3 + t.par][:, :]), more,
                                            ALU.add).then_inc(s["summed"], 1)
                    dve.wait_ge(s["summed"], t.nth())
                    if t.past(2):
                        dve.wait_ge(s["shifted"], t.before(2))
                    nc.vector.tensor_reduce(mx[:, t.par, :], by_head(score[:, t.par, :]), AX.X,
                                            ALU.max).then_inc(s["maxed"], 1)
                t = at(1)
                if t.live and not relative:
                    dve.wait_ge(s["qk_ps"], t.nth())
                    if t.past(2):
                        dve.wait_ge(s["scores"], t.before(2))
                        dve.wait_ge(s["k_pool"], t.before(2, 2))
                    nc.vector.tensor_tensor(by_seq(qT[:, t.par, :]), by_seq(ps[1][:, 0:P]), rope,
                                            ALU.mult).then_inc(s["q"], 1)
                    nc.vector.tensor_tensor(by_seq(kT[:, t.par, :]), by_seq(ps[1][:, P:2 * P]), rope,
                                            ALU.mult).then_inc(s["k"], 1)
                t = at(4)
                if t.live:
                    dve.wait_ge(s["o_ps"], t.nth())
                    if t.past(2):
                        dve.wait_ge(s["oT_ps"], t.before(2))
                    heads = ps[6][:, 0:H * (HD + 1)].rearrange("p (h n) -> p h n", n=HD + 1)
                    nc.vector.reciprocal(recip[:, t.par, :], heads[:, :, HD]).then_inc(s["recip"], 1)
                    dve.wait_ge(s["recip"], t.nth())
                    nc.vector.tensor_tensor(o[:, t.par, :].rearrange("p (h d) -> p h d", d=HD), heads[:, :, 0:HD],
                                            recip[:, t.par, :].unsqueeze(2).broadcast_to([P, H, HD]),
                                            ALU.mult).then_inc(s["o"], 1)
                t = at(2)
                if t.live:
                    dve.wait_ge(s["v_ps"], t.nth())
                    dve.wait_ge(s["ones"], 3)
                    if t.past(2):
                        dve.wait_ge(s["o_ps"], t.before(2))
                    nc.vector.tensor_tensor(v_all[:, t.par, :, :, 0:HD],
                                            ps[2][:, :].rearrange("p (n h d) -> p n h d", h=H4, d=HD),
                                            c[:, C_M4P:C_M4P + H4].unsqueeze(1).unsqueeze(3).broadcast_to(
                                                [P, B4 * G, H4, HD]), ALU.mult).then_inc(s["v"], 1)
                t = at(5)
                if t.live:
                    dve.wait_ge(s["y_ps"], t.nth())
                    dve.wait_ge(s["xb"], t.nth())
                    nc.vector.tensor_tensor(m.X[:, t.cols()], ps[7][:, 0:D], xb[:, t.par, :],
                                            ALU.add).then_inc(tail.x_new, 1)
                    tail.dve(dve, t)
            over_tiles(dve, STAGES, work)

        @block.gpsimd
        def _(pool):
            def work(at):
                t = at(2)
                if t.live:
                    pool.wait_ge(s["k"], t.nth())
                    if t.past(2):
                        pool.wait_ge(s["scores"], t.before(2))
                    for b in (2, 3):
                        nc.gpsimd.tensor_tensor(
                            k_all[:, t.par, b],
                            kT[:, t.par, b * LEN:(b + 1) * LEN].unsqueeze(1).broadcast_to([P, H, LEN]),
                            c[:, C_M16:C_M16 + H].unsqueeze(2).broadcast_to([P, H, LEN]), ALU.mult).then_inc(s["k_pool"], 1)
                t = at(4)
                if t.live:
                    if t.past(2):
                        pool.wait_ge(tail.x_new, t.before(2))
                    if relative:
                        more = m.bA[:, :]
                    else:
                        pool.wait_ge(s["zres"], t.nth())
                        more = zres[:, t.par, :]
                    nc.gpsimd.tensor_tensor(xb[:, t.par, :], m.X[:, t.cols()], more, ALU.add).then_inc(s["xb"], 1)
                t = at(3)
                if t.live:
                    pool.wait_ge(s["maxed"], t.nth())
                    sc = by_head(score[:, t.par, :])
                    nc.gpsimd.tensor_tensor(sc, sc, mx[:, t.par, :].unsqueeze(2).broadcast_to([P, H, LEN]),
                                            ALU.subtract).then_inc(s["shifted"], 1)
                t = at(5)
                if t.live:
                    tail.pool(pool, t)
            over_tiles(pool, STAGES, work)


def relative_attention(m):
    self_attention(m, "p4", True)


def causal_attention(m):
    self_attention(m, "p8", False)


def cross_many_heads(m):
    nc, ps, c = m.nc, m.ps, m.const
    N = B4 * G
    AHEAD = 4
    LAST = 2 * P
    s = {n: m.sem("p6_" + n) for n in (
        "z", "zT_ps", "zT", "q_ps", "q", "k_ps", "k", "v_ps", "v", "v_last", "scores", "maxed", "probs", "recip",
        "normed", "pT_ps", "pT", "last_ps", "last", "o_ps", "masked", "oT", "y_ps", "xb")}
    ctx_in = [m.sem("p6_ctx_in_a"), m.sem("p6_ctx_in_b")]
    tail = Tail(m, "p6", [sinks(m, "z"), sinks(m, "rms")])
    ident = c[:, C_ID:C_ID + P]
    s0 = float(D) ** -0.5
    with ExitStack() as own, nc.Block() as block:
        sb = lambda n, shape: own.enter_context(nc.sbuf_tensor("p6_" + n, shape, F32))
        ctxT = sb("ctxT", [P, 2, B4, CTX])
        z, zT, oT, xb = (sb(n, [P, 2, P]) for n in ("z", "zT", "oT", "xb"))
        q_all = sb("q_all", [P, 2, B4, H4, LEN])
        kT = sb("kT", [P, 2, CTX])
        v, v_last = sb("v", [P, 2, 2, P]), sb("v_last", [G, 2, P])
        prob = sb("prob", [P, 2, G, CTX])
        nmax, total, recip = (sb(n, [P, N]) for n in ("nmax", "total", "recip"))
        pT, p_last = sb("pT", [P, 2, 2, P]), sb("p_last", [G, 2, P])
        masked = sb("masked", [P, H4, LEN])

        @block.sync
        def _(sp):
            def work(at):
                t = at(0)
                if t.live:
                    if t.past(2):
                        sp.wait_ge(s["v_ps"], t.before(2, B4))
                    sp.dma_start(ctxT[:, t.par], m.ctxT_dram[:, t.cols(B4 * CTX)].rearrange(
                        "d (b k) -> d b k", k=CTX)).then_inc(ctx_in[t.par], 16)
            over_tiles(sp, 1, work)

        @block.tensor
        def _(pe):
            def scores(t, u):
                b, g = u // G, u % G
                pe.wait_ge(s["q"], t.nth())
                pe.wait_ge(s["k"], t.unit(b, 0, B4))
                if t.past_unit(u, 2):
                    pe.wait_ge(s["probs"], t.unit(u, 2))
                rows = slice(32 * g, 32 * g + 32)
                nc.tensor.matmul(ps[3 + u % 2][:, 0:CTX], q_all[rows, t.par, b], kT[rows, b % 2, :],
                                 start=True, stop=True, tile_position=(32 * g, 0)).then_inc(s["scores"], 1)

            def keys(t, b):
                pe.wait_ge(ctx_in[t.par], t.nth_of_pair(16))
                if t.past_unit(b, 1, B4):
                    pe.wait_ge(s["k"], t.unit(b, 1, B4))
                nc.tensor.matmul(ps[1][:, 0:CTX], m.w["WkT_x"][:, :], ctxT[:, t.par, b, :],
                                 start=True, stop=True).then_inc(s["k_ps"], 1)

            def values(t, b):
                pe.wait_ge(ctx_in[t.par], t.nth_of_pair(16))
                if t.past_unit(b, 1, B4):
                    pe.wait_ge(s["v"], t.unit(b, 1, B4))
                    pe.wait_ge(s["v_last"], t.unit(b, 1, B4))
                for n in range(2):
                    nc.tensor.matmul(ps[2][:, n * P:(n + 1) * P], ctxT[:, t.par, b, n * P:(n + 1) * P],
                                     m.w["WvT_x"][:, :], start=True, stop=True)
                nc.tensor.matmul(ps[2][0:G, LAST:LAST + P], ctxT[:, t.par, b, LAST:LAST + 1].broadcast_to([P, G]),
                                 m.w["WvT_x"][:, :], start=True, stop=True).then_inc(s["v_ps"], 1)

            def turn(t, u):
                b, g = u // G, u % G
                pe.wait_ge(s["normed"], t.unit(u))
                bank = ps[5 + u % 2]
                if t.past_unit(u, 2):
                    pe.wait_ge(s["pT"], t.unit(u, 2))
                if u % 2 and t.past_unit(b, 1, B4):
                    pe.wait_ge(s["last"], t.unit(b, 1, B4))
                for n in range(2):
                    last = nc.tensor.transpose(bank[:, n * P:(n + 1) * P], prob[:, b % 2, g, n * P:(n + 1) * P], ident)
                last.then_inc(s["pT_ps"], 1)
                if g == G - 1:
                    nc.tensor.transpose(bank[0:G, LAST:LAST + P], prob[:, b % 2, :, LAST], ident).then_inc(s["last_ps"], 1)

            def weigh(t, u):
                b, g = u // G, u % G
                pe.wait_ge(s["pT"], t.unit(u))
                pe.wait_ge(s["v"], t.unit(b, 0, B4))
                if g == 0 and t.past_unit(b, 1, B4):
                    pe.wait_ge(s["masked"], t.unit(b, 1, B4))
                for n in range(2):
                    nc.tensor.matmul(ps[7][32 * g:32 * g + 32, 0:P], v[:, b % 2, n, 32 * g:32 * g + 32],
                                     pT[:, u % 2, n, :], start=(n == 0), stop=(n == 1),
                                     tile_position=(0, 32 * g), skip_group_check=True).then_inc(s["o_ps"], 1)
                if g == G - 1:
                    pe.wait_ge(s["last"], t.unit(b, 0, B4))
                    pe.wait_ge(s["v_last"], t.unit(b, 0, B4))
                    nc.tensor.matmul(ps[7][:, 0:P], v_last[:, b % 2, :], p_last[:, b % 2, :], start=False, stop=True,
                                     skip_group_check=True).then_inc(s["o_ps"], 1)

            def steps(at):
                cur, nxt, prev = at(1), at(0), at(2)
                for n in range(N):
                    t, u = (cur, n + AHEAD) if n + AHEAD < N else (nxt, n + AHEAD - N)
                    if t.live:
                        scores(t, u)
                    t, b = (cur, n // G + 2) if n // G + 2 < B4 else (nxt, n // G + 2 - B4)
                    if n % G == 1 and t.live:
                        keys(t, b)
                    t, b = (cur, n // G + 1) if n // G + 1 < B4 else (nxt, 0)
                    if n % G == 2 and t.live:
                        values(t, b)
                    if cur.live:
                        turn(cur, n)
                    t, u = (cur, n - 1) if n else (prev, N - 1)
                    if t.live:
                        weigh(t, u)
                    if n == 3 and prev.live:
                        pe.wait_ge(s["oT"], prev.nth(B4))
                        nc.tensor.matmul(ps[0][:, 2 * P:3 * P], oT[:, prev.par, :], m.w["WoT_x"][:, :],
                                         start=True, stop=True).then_inc(s["y_ps"], 1)
                    if n == 5 and nxt.live:
                        pe.wait_ge(s["z"], nxt.nth())
                        if nxt.past(2):
                            pe.wait_ge(tail.x_new, nxt.before(2))
                        nc.tensor.transpose(ps[0][:, 0:P], z[:, nxt.par, :], ident).then_inc(s["zT_ps"], 1)
                    if n == 7 and nxt.live:
                        pe.wait_ge(s["zT"], nxt.nth())
                        nc.tensor.matmul(ps[0][:, P:2 * P], m.w["WqT_x"][:, :], zT[:, nxt.par, :],
                                         start=True, stop=True).then_inc(s["q_ps"], 1)
            over_tiles(pe, 2, steps)

        @block.scalar
        def _(act):
            def steps(at):
                cur, nxt = at(1), at(0)
                for n in range(N):
                    t, u = (cur, n + AHEAD) if n + AHEAD < N else (nxt, n + AHEAD - N)
                    if t.live:
                        act.wait_ge(s["maxed"], t.unit(u))
                        if t.past_unit(u, 8):
                            act.wait_ge(s["pT_ps"], t.unit(u, 8))
                        if u % G == 0 and t.past_unit(u // G, 2, B4):
                            act.wait_ge(s["last_ps"], t.unit(u // G, 2, B4))
                        nc.scalar.activation(prob[:, u // G % 2, u % G, :], ps[3 + u % 2][:, 0:CTX], ACT.Exp,
                                             bias=nmax[:, u:u + 1], accum_out=total[:, u:u + 1]).then_inc(s["probs"], 1)
                    t, b = (cur, n // G + 2) if n // G + 2 < B4 else (nxt, n // G + 2 - B4)
                    if n % G == 1 and t.live:
                        act.wait_ge(s["k_ps"], t.unit(b, 0, B4))
                        if t.past_unit(b, 2, B4):
                            act.wait_ge(s["scores"], t.unit(b * G + G - 1, 2 * G))
                        nc.scalar.activation(kT[:, b % 2, :], ps[1][:, 0:CTX], ACT.Copy).then_inc(s["k"], 1)
                    t, b = (cur, n // G + 1) if n // G + 1 < B4 else (nxt, 0)
                    if n % G == 2 and t.live:
                        act.wait_ge(s["v_ps"], t.unit(b, 0, B4))
                        act.wait_ge(s["v_last"], t.unit(b, 0, B4))
                        if t.past_unit(b, 2, B4):
                            act.wait_ge(s["o_ps"], t.unit(b, 2, B4) * 9)
                        nc.scalar.activation(v[:, b % 2], ps[2][:, 0:2 * P].rearrange("p (n d) -> p n d", n=2),
                                             ACT.Copy).then_inc(s["v"], 1)
                    if n % G == 3 and cur.live:
                        b = n // G
                        act.wait_ge(s["last_ps"], cur.unit(b, 0, B4))
                        act.wait_ge(s["pT"], cur.unit(n))
                        if cur.past_unit(b, 2, B4):
                            act.wait_ge(s["o_ps"], cur.unit(b, 2, B4) * 9)
                        nc.scalar.activation(p_last[:, b % 2, :], ps[6][0:G, LAST:LAST + P], ACT.Copy).then_inc(s["last"], 1)
                    if n == 5 and nxt.live:
                        act.wait_ge(s["zT_ps"], nxt.nth())
                        if nxt.past(2):
                            act.wait_ge(s["q_ps"], nxt.before(2))
                        nc.scalar.activation(zT[:, nxt.par, :], ps[0][:, 0:P], ACT.Copy, scale=s0).then_inc(s["zT"], 1)
            over_tiles(act, 2, steps)

        @block.vector
        def _(dve):
            def steps(at):
                cur, nxt, prev = at(1), at(0), at(2)
                for n in range(N):
                    t, u = (cur, n + AHEAD - 1) if n + AHEAD - 1 < N else (nxt, n + AHEAD - 1 - N)
                    if t.live:
                        dve.wait_ge(s["probs"], t.unit(u))
                        if t.past_unit(u, N):
                            dve.wait_ge(s["normed"], t.unit(u, N))
                        nc.vector.reciprocal(recip[:, u:u + 1], total[:, u:u + 1]).then_inc(s["recip"], 1)
                    t, u = (cur, n + AHEAD) if n + AHEAD < N else (nxt, n + AHEAD - N)
                    if t.live:
                        dve.wait_ge(s["scores"], t.unit(u))
                        nc.vector.tensor_reduce(nmax[:, u:u + 1], ps[3 + u % 2][:, 0:CTX], AX.X, ALU.max,
                                                negate=True).then_inc(s["maxed"], 1)
                    t, b = (cur, n // G + 1) if n // G + 1 < B4 else (nxt, 0)
                    if n % G == 2 and t.live:
                        dve.wait_ge(s["v_ps"], t.unit(b, 0, B4))
                        if t.past_unit(b, 2, B4):
                            dve.wait_ge(s["o_ps"], t.unit(b, 2, B4) * 9)
                        nc.vector.tensor_tensor(v_last[:, b % 2, :].rearrange("p (g n) -> p g n", g=G),
                                                ps[2][0:G, LAST:LAST + P].rearrange("p (g n) -> p g n", g=G),
                                                c[0:G, C_ID:C_ID + G].unsqueeze(2).broadcast_to([G, G, 32]),
                                                ALU.mult).then_inc(s["v_last"], 1)
                    if cur.live:
                        dve.wait_ge(s["pT_ps"], cur.unit(n))
                        if n % G == G - 1:
                            dve.wait_ge(s["last_ps"], cur.unit(n // G, 0, B4))
                        if cur.past_unit(n, 2):
                            b2, g2 = (n - 2) // G, (n - 2) % G
                            dve.wait_ge(s["o_ps"], (cur.n * B4 + b2) * 9 + 2 * g2 + 2)
                        nc.vector.tensor_copy(pT[:, n % 2], ps[5 + n % 2][:, 0:2 * P].rearrange(
                            "p (n k) -> p n k", n=2)).then_inc(s["pT"], 1)
                    t, b = (cur, n // G - 1) if n else (prev, B4 - 1)
                    if n % G == 0 and t.live:
                        dve.wait_ge(s["o_ps"], t.unit(b, 0, B4) * 9)
                        if t.past_unit(b, 1, B4):
                            dve.wait_ge(s["oT"], t.unit(b, 1, B4))
                        nc.vector.tensor_tensor(masked[:, :, :], ps[7][:, 0:P].rearrange("p (h i) -> p h i", h=H4),
                                                c[:, C_M4G:C_M4G + H4].unsqueeze(2).broadcast_to([P, H4, LEN]),
                                                ALU.mult).then_inc(s["masked"], 1)
                        dve.wait_ge(s["masked"], t.unit(b, 0, B4))
                        if b == 0 and t.past(2):
                            dve.wait_ge(s["y_ps"], t.before(2))
                        nc.vector.tensor_reduce(oT[:, t.par, b * LEN:(b + 1) * LEN],
                                                masked[:, :, :].rearrange("p h i -> p i h"), AX.X,
                                                ALU.add).then_inc(s["oT"], 1)
                    if n == 3 and nxt.live:
                        if nxt.past(2):
                            dve.wait_ge(s["zT_ps"], nxt.before(2))
                        normed(m, z[:, nxt.par, :], nxt, m.RZ).then_inc(s["z"], 1)
                    if n == 4 and prev.live:
                        dve.wait_ge(s["y_ps"], prev.nth())
                        dve.wait_ge(s["xb"], prev.nth())
                        nc.vector.tensor_tensor(m.X[:, prev.cols()], ps[0][:, 2 * P:3 * P], xb[:, prev.par, :],
                                                ALU.add).then_inc(tail.x_new, 1)
                        tail.dve(dve, prev)
                    if n == 8 and nxt.live:
                        dve.wait_ge(s["q_ps"], nxt.nth())
                        if nxt.past(2):
                            dve.wait_ge(s["scores"], nxt.before(2, N))
                        nc.vector.tensor_tensor(
                            q_all[:, nxt.par],
                            ps[0][:, P:2 * P].rearrange("p (b i) -> p b i", i=LEN).unsqueeze(2).broadcast_to(
                                [P, B4, H4, LEN]),
                            c[:, C_M4G:C_M4G + H4].unsqueeze(1).unsqueeze(3).broadcast_to([P, B4, H4, LEN]),
                            ALU.mult).then_inc(s["q"], 1)
            over_tiles(dve, 2, steps)

        @block.gpsimd
        def _(pool):
            def steps(at):
                cur, nxt, prev = at(1), at(0), at(2)
                for n in range(N):
                    t, u = (cur, n + AHEAD - 1) if n + AHEAD - 1 < N else (nxt, n + AHEAD - 1 - N)
                    if t.live:
                        pool.wait_ge(s["recip"], t.unit(u))
                        p = prob[:, u // G % 2, u % G, :]
                        nc.gpsimd.tensor_tensor(p, p, recip[:, u:u + 1].broadcast_to([P, CTX]),
                                                ALU.mult).then_inc(s["normed"], 1)
                    if n == 2 and prev.live:
                        if prev.past(2):
                            pool.wait_ge(tail.x_new, prev.before(2))
                        nc.gpsimd.tensor_tensor(xb[:, prev.par, :], m.X[:, prev.cols()], m.bX[:, :], ALU.add).then_inc(s["xb"], 1)
                    if n == 5 and prev.live:
                        tail.pool(pool, prev)
            over_tiles(pool, 2, steps)


def lay_out_experts(f):
    def first(w):
        return w.transpose(1, 0, 2).reshape(D, E * F)

    def second(w):
        return w.reshape(E, FC, P, D).transpose(2, 0, 1, 3).reshape(P, E * FC * D)

    return {
        "Wg": f["L0_ffn_Wg"], "router_T": f["L1_ffn_router_w"].T,
        "w1_0": first(f["L0_ffn_fc1_w"]), "w2_0": second(f["L0_ffn_fc2_w"]),
        "w1_1": first(f["L1_ffn_w1"]), "w2_1": second(f["L1_ffn_w2"]),
        "ln_wT": f["L0_ffn_ln_w"].T, "ln_bT": f["L0_ffn_ln_b"].T, "b1": f["L0_ffn_fc1_b"].reshape(1, E * F),
        "b2": np.tile(f["L0_ffn_fc2_b"].reshape(1, E * D), (P, 1)), "alpha": np.tile(f["L0_ffn_alpha"][None], (P, 1)),
    }


def route(m, name, layer):
    nc, ps, c = m.nc, m.ps, m.const
    s = {n: m.sem(name + "_" + n) for n in (
        "loaded", "z", "zT_ps", "zT", "logit_ps", "logits", "best", "which", "whichf", "hot", "gap", "cum", "rank_ps",
        "ranked", "prod", "slotf", "slot", "kept", "x", "go", "count_ps", "step", "exp", "mapped", "gaps",
        "b1_ps", "b1", "scaled")}
    SETS = 4
    scattered = [m.sem(name + f"_scattered{n}") for n in range(SETS)]
    ident = c[:, C_ID:C_ID + P]
    tri, ones = c[:, C_TRI:C_TRI + P], c[:, C_ONES:C_ONES + P]
    iota, base = c[:, C_IOTA:C_IOTA + E], c[:, C_BASE:C_BASE + E]
    STAGES = 6
    folds = layer == 0
    LOADS = 7 if folds else 3
    with ExitStack() as own, nc.Block() as block:
        sb = lambda n, shape, dt=F32: own.enter_context(nc.sbuf_tensor(name + "_" + n, shape, dt))
        z, zT, x = sb("z", [P, 2, P]), sb("zT", [P, 2, P]), sb("x", [P, SETS, P])
        wg = sb("wg", [P, E])
        logits, best, which = sb("logits", [P, 2, E]), sb("best", [P, 2, E]), sb("which", [P, 2, E], U32)
        whichf = sb("whichf", [P, 2, TOPK])
        hot = sb("hot", [P, TILES * TOPK * E])
        cum = sb("cum", [P, 2, TOPK * E])
        rank, prod = sb("rank", [P, 2, E]), sb("prod", [P, 2, TOPK, E])
        slotf, slot = sb("slotf", [P, 2, TOPK]), sb("slot", [P, SETS, TOPK], I32)
        gap, ex, den = sb("gap", [P, TILES]), sb("ex", [P, TILES]), sb("den", [P, TILES])
        zeros = sb("zeros", [P, P])
        tiny = sb("tiny", [P, 1])
        count, jobs, first, end, q = (sb(n, [P, E]) for n in ("count", "jobs", "first", "end", "q"))
        count_i = sb("count_i", [P, E], I32)
        full, before = sb("full", [P, E, TILES]), sb("before", [P, E, E])
        owner, upper, value = (sb(n, [P, JOBS, E]) for n in ("owner", "upper", "value"))
        job = sb("job", [P, JOBS])
        picked, moved = sb("picked", [P, TILES * TOPK, E]), sb("moved", [P, TILES * TOPK])
        alpha = sb("alpha", [P, E])
        if folds:
            lnw, lnb, b1_row = sb("lnw", [P, E]), sb("lnb", [P, E]), sb("b1_row", [1, E * F])

        @block.sync
        def _(sp):
            sp.dma_start(wg[:, :], m.a["Wg" if folds else "router_T"]).then_inc(s["loaded"], 16)
            for dst, src in ((m.w1, "w1_0" if folds else "w1_1"), (m.w2, "w2_0" if folds else "w2_1")) + ((
                    (lnw, "ln_wT"), (lnb, "ln_bT"), (b1_row, "b1"), (alpha, "alpha")) if folds else ()):
                sp.dma_start(dst[:, :], m.a[src]).then_inc(s["loaded"], 16)
            if folds:
                sp.dma_start(m.b2[:, :].rearrange("p (e f) -> p e f", e=E)[:, :, 0:D],
                             m.a["b2"].rearrange("p (e d) -> p e d", e=E)).then_inc(s["mapped"], 16)
            sp.wait_ge(s["gaps"], 1)
            for e in range(E):
                n = sp.value_load(count_i[0:1, e:e + 1], min_val=0, max_val=TOKENS)
                sp.dma_start(m.xs_dram[DS(n + e * REGION, P), :], zeros[:, :]).then_inc(s["mapped"], 16)
            sp.dma_start(m.xs_dram[SPARE:SPARE + P, :], zeros[:, :]).then_inc(s["mapped"], 16)
            sp.wait_ge(s["mapped"], 16 * (E + 1 + folds))

        @block.tensor
        def _(pe):
            pe.wait_ge(s["loaded"], 16 * LOADS)

            def work(at):
                t = at(4)
                if t.live:
                    pe.wait_ge(s["hot"], t.nth())
                    pe.wait_ge(s["cum"], t.nth())
                    if t.past(2):
                        pe.wait_ge(s["ranked"], t.before(2))
                    out = ps[6 + t.two][:, 0:E]
                    for k in range(TOPK):
                        nc.tensor.matmul(out, tri, hot[:, DS(t.n * TOPK * E + k * E, E)] if not t.known else
                                         hot[:, t.n * TOPK * E + k * E:t.n * TOPK * E + k * E + E],
                                         start=(k == 0), stop=False)
                    for k in range(TOPK):
                        last = nc.tensor.matmul(out, ones, cum[:, t.two, k * E:(k + 1) * E], start=False,
                                                stop=(k == TOPK - 1))
                    last.then_inc(s["rank_ps"], 1)
                t = at(2)
                if t.live:
                    pe.wait_ge(s["zT"], t.nth())
                    if t.past(2):
                        pe.wait_ge(s["logits"], t.before(2))
                    nc.tensor.matmul(ps[4 + t.two][:, 0:E], zT[:, t.two, :], wg[:, :],
                                     start=True, stop=True).then_inc(s["logit_ps"], 1)
                t = at(1)
                if t.live:
                    pe.wait_ge(s["z"], t.nth())
                    if t.past(2):
                        pe.wait_ge(s["zT"], t.before(2))
                    nc.tensor.transpose(ps[t.two][:, 0:P], z[:, t.two, :], ident).then_inc(s["zT_ps"], 1)
            over_tiles(pe, STAGES, work, unroll=SETS)
            pe.wait_ge(s["cum"], TILES + 1)
            pe.wait_ge(s["logits"], TILES)
            for k in range(TOPK):
                last = nc.tensor.matmul(ps[4][:, 0:E], ones, cum[:, TILES % 2, k * E:(k + 1) * E],
                                        start=(k == 0), stop=(k == TOPK - 1))
            last.then_inc(s["count_ps"], 1)
            if folds:
                for e in range(E):
                    if e >= 2:
                        pe.wait_ge(s["b1"], e - 1)
                    bank = ps[2 + e % 2]
                    nc.tensor.matmul(bank[:, :], lnb[:, e:e + 1].broadcast_to([P, P]), m.w1[:, e * F:(e + 1) * F],
                                     start=True, stop=False)
                    nc.tensor.matmul(bank[:, :], c[0:1, C_ONES:C_ONES + P], b1_row[0:1, e * F:(e + 1) * F],
                                     start=False, stop=True).then_inc(s["b1_ps"], 1)

        @block.scalar
        def _(act):
            def work(at):
                t = at(1)
                if t.live:
                    act.wait_ge(s["zT_ps"], t.nth())
                    if t.past(2):
                        act.wait_ge(s["logit_ps"], t.before(2))
                    nc.scalar.activation(zT[:, t.two, :], ps[t.two][:, 0:P], ACT.Copy).then_inc(s["zT"], 1)
                t = at(2)
                if t.live:
                    act.wait_ge(s["logit_ps"], t.nth())
                    if t.past(2):
                        act.wait_ge(s["which"], t.before(2))
                    nc.scalar.activation(logits[:, t.two, :], ps[4 + t.two][:, 0:E], ACT.Copy).then_inc(s["logits"], 1)
                t = at(5)
                if t.live:
                    act.wait_ge(s["slotf"], t.nth())
                    if t.past(SETS):
                        act.wait_ge(scattered[t.par], t.half * 16 * TOPK)
                    nc.scalar.activation(slot[:, t.par, :], slotf[:, t.two, :], ACT.Copy).then_inc(s["slot"], 1)
            over_tiles(act, STAGES, work, unroll=SETS)
            if folds:
                act.wait_ge(s["loaded"], 16 * LOADS)
                for e in range(E):
                    act.wait_ge(s["b1_ps"], e + 1)
                    nc.scalar.activation(m.QV[:, e * F:(e + 1) * F], ps[2 + e % 2][:, :], ACT.Copy).then_inc(s["b1"], 1)
            act.wait_ge(s["gap"], TILES)
            nc.scalar.activation(ex[:, :], gap[:, :], ACT.Exp).then_inc(s["exp"], 1)

        @block.vector
        def _(dve):
            nc.vector.memset(zeros[:, :], 0.0)
            nc.vector.memset(m.job_expert[:, :], 0)
            nc.vector.memset(cum[:, 0, :], 0.0).then_inc(s["cum"], 1)

            def work(at):
                t = at(5)
                if t.live:
                    dve.wait_ge(s["rank_ps"], t.nth())
                    nc.vector.tensor_tensor(rank[:, t.two, :], ps[6 + t.two][:, 0:E], base, ALU.add).then_inc(s["ranked"], 1)
                    dve.wait_ge(s["ranked"], t.nth())
                    nc.vector.tensor_tensor(prod[:, t.two], hot[:, t.cols(TOPK * E)].rearrange("p (k e) -> p k e", e=E),
                                            rank[:, t.two, :].unsqueeze(1).broadcast_to([P, TOPK, E]),
                                            ALU.mult).then_inc(s["prod"], 1)
                t = at(0)
                if t.live:
                    if t.past(2):
                        dve.wait_ge(s["zT_ps"], t.before(2))
                    normed(m, z[:, t.two, :], t, m.RZ).then_inc(s["z"], 1)
                t = at(5)
                if t.live:
                    dve.wait_ge(s["prod"], t.nth())
                    if t.past(2):
                        dve.wait_ge(s["slot"], t.before(2))
                    nc.vector.tensor_reduce(slotf[:, t.two, :], prod[:, t.two], AX.X, ALU.add).then_inc(s["slotf"], 1)
                t = at(3)
                if t.live:
                    dve.wait_ge(s["logits"], t.nth())
                    nc.vector.memset(m.gate[:, 0:1], 0.0)
                    nc.vector.max(best[:, t.two, :], logits[:, t.two, :]).then_inc(s["best"], 1)
                t = at(5)
                if t.live:
                    dve.wait_ge(s["slotf"], t.nth())
                    nc.vector.tensor_scalar(m.slot[:, t.cols(TOPK)], slotf[:, t.two, :], 1.0, None,
                                            ALU.mult).then_inc(s["kept"], 1)
                t = at(3)
                if t.live:
                    dve.wait_ge(s["best"], t.nth())
                    nc.vector.memset(m.gate[:, 1:2], 0.0)
                    nc.vector.max_index(which[:, t.two, :], best[:, t.two, :], logits[:, t.two, :]).then_inc(s["which"], 1)
                t = at(5)
                if t.live:
                    if t.past(SETS):
                        dve.wait_ge(scattered[t.par], t.half * 16 * TOPK)
                    normed(m, x[:, t.par, :], t, m.RN if folds else m.RZ).then_inc(s["x"], 1)
                t = at(3)
                if t.live:
                    dve.wait_ge(s["which"], t.nth())
                    nc.vector.memset(m.gate[:, 2:3], 0.0)
                    nc.vector.tensor_copy(whichf[:, t.two, :], which[:, t.two, 0:TOPK]).then_inc(s["whichf"], 1)
                    nc.vector.tensor_tensor(gap[:, t.cols(1)], best[:, t.two, 1:2], best[:, t.two, 0:1],
                                            ALU.subtract).then_inc(s["gap"], 1)
                    dve.wait_ge(s["whichf"], t.nth())
                    nc.vector.tensor_tensor(hot[:, t.cols(TOPK * E)].rearrange("p (k e) -> p k e", e=E),
                                            iota.unsqueeze(1).broadcast_to([P, TOPK, E]),
                                            whichf[:, t.two, :].unsqueeze(2).broadcast_to([P, TOPK, E]),
                                            ALU.is_equal).then_inc(s["hot"], 1)
                    dve.wait_ge(s["hot"], t.nth())
                    if t.past():
                        dve.wait_ge(s["rank_ps"], t.before())
                    nc.vector.tensor_tensor(cum[:, 1 - t.two, :], cum[:, t.two, :], hot[:, t.cols(TOPK * E)],
                                            ALU.add).then_inc(s["cum"], 1)
            over_tiles(dve, STAGES, work, unroll=SETS)

            dve.wait_ge(s["exp"], 1)
            nc.vector.tensor_scalar(den[:, :], ex[:, :], 1.0, None, ALU.add).then_inc(s["step"], 1)
            dve.wait_ge(s["step"], 1)
            nc.vector.reciprocal(m.gates[:, :, 0], den[:, :]).then_inc(s["step"], 1)
            dve.wait_ge(s["step"], 2)
            nc.vector.tensor_tensor(m.gates[:, :, 1], ex[:, :], m.gates[:, :, 0], ALU.mult).then_inc(s["step"], 1)

            dve.wait_ge(s["count_ps"], 1)
            by_job = lambda ap: ap.unsqueeze(1).broadcast_to([P, JOBS, E])
            by_expert = lambda ap: ap.unsqueeze(2).broadcast_to([P, E, E])
            row = c[:, C_JOB:C_JOB + JOBS].unsqueeze(2).broadcast_to([P, JOBS, E])
            hots = hot[:, :].rearrange("p (n e) -> p n e", e=E)
            tt, ts, red = nc.vector.tensor_tensor, nc.vector.tensor_scalar, nc.vector.tensor_reduce
            by_token = lambda ap: ap.unsqueeze(1).broadcast_to([P, TILES * TOPK, E])
            stages = [
                lambda: ts(count[:, :], ps[4][:, 0:E], 1.0, None, ALU.mult),
                lambda: ts(count_i[:, :], count[:, :], 1.0, None, ALU.mult),
                lambda: tt(full[:, :, :], count[:, :].unsqueeze(2).broadcast_to([P, E, TILES]),
                           c[:, C_JOB:C_JOB + TILES].unsqueeze(1).broadcast_to([P, E, TILES]), ALU.is_gt),
                lambda: red(jobs[:, :], full[:, :, :], AX.X, ALU.add),
                lambda: tt(before[:, :, :], by_expert(iota), iota.unsqueeze(1).broadcast_to([P, E, E]), ALU.is_gt),
                lambda: tt(before[:, :, :], before[:, :, :], jobs[:, :].unsqueeze(1).broadcast_to([P, E, E]), ALU.mult),
                lambda: red(first[:, :], before[:, :, :], AX.X, ALU.add),
                lambda: ts(first[:, :], first[:, :], float(P), None, ALU.mult),
                lambda: nc.vector.scalar_tensor_tensor(end[:, :], jobs[:, :], c[:, C_JOB + 1:C_JOB + 2], first[:, :],
                                                       ALU.mult, ALU.add),
                lambda: tt(q[:, :], base, first[:, :], ALU.subtract),
                lambda: tt(owner[:, :, :], row, by_job(first[:, :]), ALU.is_ge),
                lambda: tt(upper[:, :, :], row, by_job(end[:, :]), ALU.is_lt),
                lambda: tt(owner[:, :, :], owner[:, :, :], upper[:, :, :], ALU.mult),
                lambda: tt(upper[:, :, :], owner[:, :, :], by_job(iota), ALU.mult),
                lambda: red(job[:, :], upper[:, :, :], AX.X, ALU.add),
                lambda: ts(m.job_expert[:, AROUND:AROUND + JOBS], job[:, :], float(F), None, ALU.mult),
                lambda: tt(value[:, :, :], row, by_job(q[:, :]), ALU.add),
                lambda: ts(value[:, :, :], value[:, :, :], float(SPARE), None, ALU.subtract),
                lambda: tt(value[:, :, :], value[:, :, :], owner[:, :, :], ALU.mult),
                lambda: red(job[:, :], value[:, :, :], AX.X, ALU.add),
                lambda: ts(m.job_row[:, :], job[:, :], float(SPARE), None, ALU.add),
                lambda: tt(picked[:, :, :], hots, by_token(q[:, :]), ALU.mult),
                lambda: red(moved[:, :], picked[:, :, :], AX.X, ALU.add),
                lambda: tt(m.slot[:, :], m.slot[:, :], moved[:, :], ALU.subtract),
            ]
            if folds:
                gates = m.gates[:, :, :].rearrange("p t k -> p (t k)")
                stages += [
                    lambda: tt(picked[:, :, :], hots, by_token(alpha[:, :]), ALU.mult),
                    lambda: red(moved[:, :], picked[:, :, :], AX.X, ALU.add),
                    lambda: tt(gates, gates, moved[:, :], ALU.mult),
                ]
            for n, stage in enumerate(stages):
                dve.wait_ge(s["step"], 3 + n)
                stage().then_inc(s["step"], 1)
                if n == 1:
                    dve.wait_ge(s["step"], 5)
                    nc.vector.memset(m.gate[:, 3:4], 0.0).then_inc(s["gaps"], 1)
            if folds:
                dve.wait_ge(s["b1_ps"], E)
                for e in range(E):
                    w = m.w1[:, e * F:(e + 1) * F]
                    nc.vector.tensor_scalar(w, w, lnw[:, e:e + 1], None, ALU.mult).then_inc(s["scaled"], 1)

        @block.gpsimd
        def _(pool):
            def work(at):
                t = at(6)
                if t.live:
                    pool.wait_ge(s["slot"], t.nth())
                    pool.wait_ge(s["x"], t.nth())
                    if t.past():
                        pool.wait_ge(s["go"], t.before())
                    nc.gpsimd.tensor_tensor(tiny[:, :], c[:, 0:1], c[:, 0:1], ALU.mult).then_inc(s["go"], 1)
                    for k in range(TOPK):
                        nc.gpsimd.indirect_dma_start(
                            m.xs_dram[:, :], bass.IndirectOffsetOnAxis(ap=slot[:, t.par, k:k + 1], axis=0),
                            x[:, t.par, :], None).then_inc(scattered[t.par], 16)
            over_tiles(pool, STAGES, work, unroll=SETS)
            for sem in scattered:
                pool.wait_ge(sem, TILES // SETS * 16 * TOPK)


def experts(m, name, layer):
    nc, ps = m.nc, m.ps
    s = {n: m.sem(name + "_" + n) for n in ("xT_ps", "xT", "h_ps", "h", "a", "aT_ps", "aT", "y_ps", "y")}
    x_in = [m.sem(name + f"_x_in{n}") for n in range(4)]
    stored = [m.sem(name + f"_stored{n}") for n in range(4)]
    gelu = ACT.Gelu_apprx_tanh if layer == 0 else ACT.Gelu
    ident = m.const[:, C_ID:C_ID + P]
    biased = layer == 0
    HALVES, STAGES, SETS = JOBS // 2, 7, 4
    FIRST, SECOND = 2, 6
    EngineType = mybir.EngineType
    with ExitStack() as own, nc.Block() as block:
        sb = lambda n, shape: own.enter_context(nc.sbuf_tensor(name + "_" + n, shape, F32))
        x, xT, y = (sb(n, [P, k, P]) for n, k in (("x", SETS), ("xT", 2), ("y", SETS)))
        h, a, aT = (sb(n, [P, 2, F]) for n in ("h", "a", "aT"))

        def experts_of(engine, half):
            n = SETS * half - SECOND + AROUND
            window = SETS + SECOND - FIRST
            ap = m.job_expert[0:1, n:n + window] if isinstance(half, int) else m.job_expert[0:1, DS(n, window)]
            return nc.values_load_multi_w_load_instructions(
                ap, engines=[engine], min_val=0, max_val=(E - 1) * F, skip_runtime_bounds_check_because=
                "route() sums one expert's first column, or none, into each entry")[1]

        @block.sync
        def _(sp):
            def work(at):
                t = at(0)
                if t.live:
                    if t.past(SETS):
                        sp.wait_ge(s["xT_ps"], t.before(SETS))
                    row = sp.value_load(m.job_row[0:1, t.cols(1)], min_val=0, max_val=SPARE)
                    sp.dma_start(x[:, t.par, :], m.xs_dram[DS(row, P), :]).then_inc(x_in[t.par], 16)
                t = at(7)
                if t.live:
                    sp.wait_ge(s["y"], t.nth())
                    sp.dma_start(m.ys_dram[t.cols(), :], y[:, t.par, :]).then_inc(stored[t.par], 16)
            over_tiles(sp, STAGES, work, HALVES, SETS)
            for sem in stored:
                sp.wait_ge(sem, 16 * JOBS // SETS)

        @block.tensor
        def _(pe):
            held = []

            def work(at):
                p = at(0).par
                if p == 0:
                    held[:] = experts_of(EngineType.PE, at(0).half)
                e1, e2 = held[p + SECOND - FIRST], held[p]

                def turn(chunks):
                    t = at(4)
                    if t.live:
                        pe.wait_ge(s["a"], t.nth())
                        if t.past(2):
                            pe.wait_ge(s["aT"], t.before(2))
                        for f in chunks:
                            nc.tensor.transpose(ps[4 + t.two][:, f * P:(f + 1) * P], a[:, t.two, f * P:(f + 1) * P],
                                                ident).then_inc(s["aT_ps"], 1)

                turn((0, 1))
                t = at(SECOND)
                if t.live:
                    pe.wait_ge(s["aT"], t.nth())
                    if t.past(2):
                        pe.wait_ge(s["y"], t.before(2))
                    for f in range(FC):
                        last = nc.tensor.matmul(ps[6 + t.two][:, 0:D], aT[:, t.two, f * P:(f + 1) * P],
                                                m.w2[:, DS(e2 + f * D, D)], start=(f == 0), stop=(f == FC - 1))
                    last.then_inc(s["y_ps"], 1)
                t = at(1)
                if t.live:
                    pe.wait_ge(x_in[t.par], t.nth_of_pair(16))
                    if t.past(2):
                        pe.wait_ge(s["xT"], t.before(2))
                    nc.tensor.transpose(ps[t.two][:, 0:P], x[:, t.par, :], ident).then_inc(s["xT_ps"], 1)
                turn((2, 3))
                t = at(FIRST)
                if t.live:
                    pe.wait_ge(s["xT"], t.nth())
                    if t.past(2):
                        pe.wait_ge(s["h" if biased else "a"], t.before(2))
                    nc.tensor.matmul(ps[2 + t.two][:, :], xT[:, t.two, :], m.w1[:, DS(e1, F)],
                                     start=True, stop=True).then_inc(s["h_ps"], 1)
            over_tiles(pe, STAGES, work, HALVES, SETS)

        @block.scalar
        def _(act):
            def work(at):
                t = at(3)
                if t.live:
                    act.wait_ge(s["h" if biased else "h_ps"], t.nth())
                    if t.past(2):
                        act.wait_ge(s["aT_ps"], t.before(2, FC))
                    nc.scalar.activation(a[:, t.two, :], h[:, t.two, :] if biased else ps[2 + t.two][:, :],
                                         gelu).then_inc(s["a"], 1)
                t = at(1)
                if t.live:
                    act.wait_ge(s["xT_ps"], t.nth())
                    if t.past(2):
                        act.wait_ge(s["h_ps"], t.before(2))
                    nc.scalar.activation(xT[:, t.two, :], ps[t.two][:, 0:P], ACT.Copy).then_inc(s["xT"], 1)
            over_tiles(act, STAGES, work, HALVES, SETS)

        @block.vector
        def _(dve):
            held = []

            def work(at):
                p = at(0).par
                if biased:
                    if p == 0:
                        held[:] = experts_of(EngineType.DVE, at(0).half)
                    e1, e2 = held[p + SECOND - FIRST], held[p]
                t = at(4)
                if t.live:
                    dve.wait_ge(s["aT_ps"], t.nth(FC))
                    if t.past(2):
                        dve.wait_ge(s["y_ps"], t.before(2))
                    nc.vector.tensor_scalar(aT[:, t.two, :], ps[4 + t.two][:, :], 1.0, None, ALU.mult).then_inc(s["aT"], 1)
                t = at(SECOND)
                if t.live:
                    dve.wait_ge(s["y_ps"], t.nth())
                    if t.past(SETS):
                        dve.wait_ge(stored[t.par], t.half * 16)
                    if biased:
                        nc.vector.tensor_tensor(y[:, t.par, :], ps[6 + t.two][:, 0:D], m.b2[:, DS(e2, D)],
                                                ALU.add).then_inc(s["y"], 1)
                    else:
                        nc.vector.tensor_scalar(y[:, t.par, :], ps[6 + t.two][:, 0:D], 1.0, None,
                                                ALU.mult).then_inc(s["y"], 1)
                t = at(FIRST)
                if t.live and biased:
                    dve.wait_ge(s["h_ps"], t.nth())
                    if t.past(2):
                        dve.wait_ge(s["a"], t.before(2))
                    nc.vector.tensor_tensor(h[:, t.two, :], ps[2 + t.two][:, :], m.QV[:, DS(e1, F)],
                                            ALU.add).then_inc(s["h"], 1)
            over_tiles(dve, STAGES, work, HALVES, SETS)


def combine(m, name, final):
    nc = m.nc
    s = {n: m.sem(name + "_" + n) for n in ("slot", "added", "go")}
    SETS = 4
    fetched = [m.sem(name + f"_fetched{n}") for n in range(SETS)]
    stored = m.sem(name + "_stored")
    tail = Tail(m, name, [sinks(m, "z")])
    STAGES = 5
    with ExitStack() as own, nc.Block() as block:
        slot = own.enter_context(nc.sbuf_tensor(name + "_slot", [P, SETS, TOPK], I32))
        y = own.enter_context(nc.sbuf_tensor(name + "_y", [P, SETS, TOPK, D], F32))
        tiny = own.enter_context(nc.sbuf_tensor(name + "_tiny", [P, 1], F32))
        gates = m.gates[:, :, :].rearrange("p t k -> p (t k)")

        def gate(t, k):
            n = t.n * TOPK + k
            return gates[:, n:n + 1] if t.known else gates[:, DS(n, 1)]

        @block.vector
        def _(dve):
            def work(at):
                t = at(0)
                if t.live:
                    if t.past(SETS):
                        dve.wait_ge(fetched[t.par], t.half * 16 * TOPK)
                    nc.vector.tensor_scalar(slot[:, t.par, :], m.slot[:, t.cols(TOPK)], 1.0, None,
                                            ALU.mult).then_inc(s["slot"], 1)
                t = at(4)
                if t.live:
                    dve.wait_ge(fetched[t.par], t.nth_of_pair(16 * TOPK))
                    x = m.X[:, t.cols()]
                    nc.vector.scalar_tensor_tensor(x, y[:, t.par, 0, :], gate(t, 0), x, ALU.mult,
                                                   ALU.add).then_inc(s["added"], 1)
                    dve.wait_ge(s["added"], t.nth())
                    nc.vector.scalar_tensor_tensor(x, y[:, t.par, 1, :], gate(t, 1), x, ALU.mult,
                                                   ALU.add).then_inc(tail.x_new, 1)
                    if not final:
                        tail.dve_all(dve, t)
            over_tiles(dve, STAGES, work, unroll=SETS)

        @block.gpsimd
        def _(pool):
            def work(at):
                t = at(1)
                if t.live:
                    pool.wait_ge(s["slot"], t.nth())
                    if t.past(SETS):
                        pool.wait_ge(tail.x_new, t.before(SETS))
                    if t.past():
                        pool.wait_ge(s["go"], t.before())
                    nc.gpsimd.tensor_tensor(tiny[:, :], m.const[:, 0:1], m.const[:, 0:1], ALU.mult).then_inc(s["go"], 1)
                    for k in range(TOPK):
                        nc.gpsimd.indirect_dma_start(
                            y[:, t.par, k, :], None, m.ys_dram[:, :],
                            bass.IndirectOffsetOnAxis(ap=slot[:, t.par, k:k + 1], axis=0)).then_inc(fetched[t.par], 16)
            over_tiles(pool, STAGES, work, unroll=SETS)
            if not final:
                tail.pool_all(pool)

        @block.sync
        def _(sp):
            def work(at):
                t = at(5)
                if t.live:
                    sp.wait_ge(tail.x_new, t.nth())
                    out = m.out_dram[t.n] if t.known else m.out_dram[DS(t.n, 1)].rearrange("a p d -> (a p) d")
                    sp.dma_start(out, m.X[:, t.cols()]).then_inc(stored, 16)
            if final:
                over_tiles(sp, STAGES, work, unroll=SETS)
                sp.wait_ge(stored, 16 * TILES)


def mixture(m, name, layer):
    route(m, name + "_route", layer)
    m.end_pass()
    experts(m, name + "_experts", layer)
    m.end_pass()
    combine(m, name + "_combine", final=(layer == 1))


def experts_one(m):
    mixture(m, "m0", 0)


def experts_two(m):
    mixture(m, "m1", 1)


def build(nc, a, out, upto=99):
    m = Chip()
    m.nc = nc
    with ExitStack() as ctx:
        in_use = []

        def sem(name):
            in_use.append(nc.alloc_semaphore(name=name))
            return in_use[-1]

        def end_pass():
            nc.clear_and_free_semaphores(in_use)
            in_use.clear()
            nc.all_engine_barrier()

        m.sem, m.end_pass = sem, end_pass
        sb = lambda name, shape, dt=F32: ctx.enter_context(nc.sbuf_tensor("sb_" + name, shape, dt))
        m.ps = [ctx.enter_context(nc.psum_tensor(f"bank{n}", [P, 512], F32)) for n in range(8)]
        m.X = sb("X", [P, TILES * D])
        m.MEAN, m.RZ, m.RN = sb("MEAN", [P, TILES]), sb("RZ", [P, TILES]), sb("RN", [P, TILES])
        m.const = sb("const", [P, C_ALL])
        m.bnst, m.mv, m.rstd = sb("bnst", [P, 2, 6]), sb("mv", [P, 2, 2]), sb("rstd", [P, 4])
        m.mv_all, m.factor = sb("mv_all", [P, 2 * TILES]), sb("factor", [P, TILES])
        m.gate = sb("gate", [P, 4])
        m.M0, m.N0, m.c0 = sb("M0", [P, D]), sb("N0", [P, D]), sb("c0", [P, 1])
        m.b0, m.bA, m.bX = sb("b0", [P, D]), sb("bA", [P, D]), sb("bX", [P, D])
        m.ptab = sb("ptab", [P, H, 1 + LEN])
        m.QV = sb("QV", [P, TILES * P])
        m.gates, m.slot = sb("gates", [P, TILES, TOPK]), sb("slot", [P, TILES * TOPK])
        m.job_row, m.job_expert = sb("job_row", [P, JOBS], I32), sb("job_expert", [P, AROUND + JOBS + AROUND], I32)
        m.w1, m.w2 = sb("w1", [P, E * F]), sb("w2", [P, E * F])
        m.b2 = sb("b2", [P, E * F])
        m.a = a
        m.bqu = sb("bqu", [P, 2])
        m.cols, m.rows = sb("cols", [P, len(COLS)]), sb("rows", [1, 3 * D])
        m.colidx = {n: k for k, n in enumerate(COLS)}
        m.c_bq0 = m.colidx["bq0"]
        m.w = {n: sb("w_" + n, [P, w]) for n, w in WEIGHTS.items()}
        m.setup_loads = [(m.const[:, :], a["const"]), (m.cols[:, :], a["cols"]), (m.rows[:, :], a["rows"])]
        m.setup_loads += [(m.w[n][:, :], a[n]) for n in WEIGHTS]
        m.x_dram = a["x"].rearrange("(t b) i d -> t (b i) d", b=B4)
        m.ctxT_dram, m.ctxN_dram = a["ctxT"], a["ctxN"]
        m.bd_dram = nc.dram_tensor("bd_scores", [SEQS, LEN, H * LEN], F32).ap()
        m.xs_dram = nc.dram_tensor("expert_inputs", [SPARE + P, D], F32).ap()
        m.ys_dram = nc.dram_tensor("expert_outputs", [JOBS * P, D], F32).ap()
        m.out_dram = out.rearrange("(t b) i d -> t (b i) d", b=B4)
        passes = [setup_pass, cross_one_head, relative_project, relative_scores, relative_attention,
                  experts_one, cross_many_heads, causal_attention, experts_two]
        for f in passes[:upto]:
            f(m)
            m.end_pass()


COLS = ("bq0", "bv0", "bv_a", "bq_a", "bk_a", "u", "v", "gamma", "beta", "norm_w")
WEIGHTS = {"Wq0": 128, "Wk0": 128, "Wv0": 128, "Wo0T": 128, "Wq_a": 128, "Wk_a": 128, "Wv_a": 128,
           "Wpos": 128, "Wf": 128, "WqT_x": 128, "WkT_x": 128, "WvT_x": 128, "WoT_x": 128,
           "w_q": 128, "w_k": 128, "w_v": 128, "w_o": 128}


def lay_out(i):
    f = {k: np.asarray(v) for k, v in i.items()}
    ctx = f["ctx_1024"]
    order = np.concatenate([np.arange(c, CTX, 3) for c in range(3)])
    padded = np.concatenate([ctx, np.zeros((SEQS, 1, D), np.float32)], 1)
    a = {
        "x": f["x"],
        "ctxT": ctx[:, order].transpose(2, 0, 1).reshape(D, SEQS * CTX),
        "ctxN": padded.reshape(TILES, B4, KC, 3, D).transpose(0, 2, 1, 3, 4).reshape(TILES, KC, B4 * 3 * D),
        "const": shape_constants(),
        "cols": np.stack([f["L0_xattn_bq"], f["L0_xattn_bv"], f["L0_attn_bv"], f["L0_attn_bq"], f["L0_attn_bk"],
                          f["L0_attn_u"].reshape(-1), f["L0_attn_v"].reshape(-1), f["L0_attn_gamma"],
                          f["L0_attn_beta"], f["L1_attn_norm_w"]], 1),
        "rows": np.concatenate([f["L0_xattn_bo"], f["L0_attn_bf"], f["L1_xattn_bo"]])[None],
        "Wq0": f["L0_xattn_Wq"], "Wk0": f["L0_xattn_Wk"], "Wv0": f["L0_xattn_Wv"], "Wo0T": f["L0_xattn_Wo"].T,
        "Wq_a": f["L0_attn_Wq"], "Wk_a": f["L0_attn_Wk"], "Wv_a": f["L0_attn_Wv"], "Wpos": f["L0_attn_Wpos"],
        "Wf": f["L0_attn_Wf"],
        "WqT_x": f["L1_xattn_Wq"].T, "WkT_x": f["L1_xattn_Wk"].T, "WvT_x": f["L1_xattn_Wv"].T,
        "WoT_x": f["L1_xattn_Wo"].T,
        "w_q": f["L1_attn_w_q"], "w_k": np.tile(f["L1_attn_w_k"], (1, G)),
        "w_v": np.tile(f["L1_attn_w_v"], (1, G)), "w_o": f["L1_attn_w_o"],
    }
    a.update(lay_out_experts(f))
    return {k: np.ascontiguousarray(v) for k, v in a.items()}


def kernel(**inputs):
    import concourse.bacc as bacc
    from concourse.bass_utils import run_bass_kernel_spmd

    arrays = lay_out(inputs)
    nc = bacc.Bacc("TRN2", target_bir_lowering=False, num_devices=1)
    views = {k: nc.dram_tensor(k, v.shape, mybir.dt.from_np(v.dtype), kind="ExternalInput").ap()
             for k, v in arrays.items()}
    out = nc.dram_tensor("latents_out", (SEQS, LEN, D), F32, kind="ExternalOutput").ap()
    build(nc, views, out)
    return run_bass_kernel_spmd(nc, [arrays], core_ids=[0]).results[0]["latents_out"]
```

```python
from contextlib import ExitStack

import numpy as np

import concourse.bass as bass
from concourse import mybir
from concourse.alu_op_type import AluOpType as ALU

F32 = mybir.dt.float32
I32 = mybir.dt.int32
U32 = mybir.dt.uint32
ACT = mybir.ActivationFunctionType
AX = mybir.AxisListType
DS = bass.ds

P = 128
D = 128
SEQS, LEN = 128, 32
CTX = 257
B4 = P // LEN
TILES = SEQS // B4
HALF = TILES // 2
H, HD = 16, 8
G, H4 = 4, 4
KC = 86
CHUNKS = ((0, 86), (86, 86), (172, 85))
E, F, FC = 8, 512, 4
TOPK = 2
TOKENS = SEQS * LEN
REGION = TOKENS + P
SPARE = E * REGION
WIDTH = D + 1
PADS = 2 * E
JOBS = TOPK * TOKENS // P + E
LN_EPS = 1e-5
RMS_EPS = 1.1920929e-07
MASKED = -1.0e30
AROUND = 8

C_ID, C_M16, C_M4G, C_M4P, C_R4 = 0, 128, 144, 148, 152
C_CAUSAL, C_ROPE, C_PE, C_IOTA = 184, 216, 248, 280
C_TRI, C_ONES = 288, 416
C_JOB, C_BASE = 544, 544 + JOBS
C_DEST, C_PAD = C_BASE + E, C_BASE + E + TOPK * TILES
C_POW = C_PAD + PADS
C_Z, C_LN, C_RMS = C_POW + 1, C_POW + 3, C_POW + 5
C_ALL = C_POW + 7


def shape_constants():
    c = np.zeros((P, C_ALL), np.float32)
    p = np.arange(P)
    c[:, C_ID:C_ID + P] = np.eye(P)
    c[p, C_M16 + p // HD] = 1.0
    c[p, C_M4G + (p // HD) % H4] = 1.0
    c[p, C_M4P + p // LEN] = 1.0
    c[p, C_R4 + p % LEN] = 1.0
    i, j = p[:, None] % LEN, np.arange(LEN)[None, :]
    c[:, C_CAUSAL:C_CAUSAL + LEN] = np.where(j <= i, 0.0, MASKED)
    d = np.arange(HD)
    theta = np.power(np.float32(10000.0), (-2.0 * (d // 2) / HD).astype(np.float32)).astype(np.float32)
    ang = np.arange(LEN, dtype=np.float32)[:, None] * theta[None, :]
    sign = np.where(np.arange(LEN) % 2 == 0, -1.0, 1.0)[:, None]
    rope = (np.cos(ang) + np.sin(ang) * sign).astype(np.float32)
    c[:, C_ROPE:C_ROPE + LEN] = rope.T[p % HD]
    inv = (1.0 / 10000.0 ** (np.arange(0.0, D, 2.0) / D)).astype(np.float32)
    pa = np.arange(LEN, dtype=np.float32)[:, None] * inv[None, :]
    pe = np.zeros((LEN, D), np.float32)
    pe[:, 0::2], pe[:, 1::2] = np.sin(pa), np.cos(pa)
    c[:, C_PE:C_PE + LEN] = pe.T
    c[:, C_IOTA:C_IOTA + E] = np.arange(E)
    c[:, C_TRI:C_TRI + P] = (p[:, None] < p[None, :])
    c[:, C_ONES:C_ONES + P] = 1.0
    c[:, C_JOB:C_JOB + JOBS] = np.arange(JOBS) * P
    c[:, C_BASE:C_BASE + E] = np.arange(E) * REGION
    c[:, C_DEST:C_DEST + TOPK * TILES] = TOPK * p[:, None] + [TOPK * P * t + k for t in range(TILES) for k in range(TOPK)]
    c[:, C_PAD:C_PAD + PADS] = TOPK * TOKENS + P * np.arange(PADS) + p[:, None]
    c[:, C_POW] = -0.5
    c[:, C_Z:C_Z + 2] = 1.0, LN_EPS
    c[:, C_LN:C_LN + 2] = 1.0 + LN_EPS, LN_EPS * LN_EPS
    c[:, C_RMS:C_RMS + 2] = 1.0 + RMS_EPS, RMS_EPS * LN_EPS
    return c



class Tile:

    def __init__(self, step, p, stage, halves=HALF, unroll=2):
        self.half, self.par, self.unroll = step + (p - stage) // unroll, (p - stage) % unroll, unroll
        self.two = self.par % 2
        self.known = isinstance(step, int)
        self.live = not self.known or 0 <= self.half < halves

    @property
    def n(self):
        return self.half * self.unroll + self.par

    def cols(self, width=P):
        return DS(self.n * width, width) if not self.known else slice(self.n * width, (self.n + 1) * width)

    def nth(self, each=1):
        return (self.n + 1) * each

    def nth_of_pair(self, each=1):
        return (self.half + 1) * each

    def past(self, back=1):
        return not self.known or self.n >= back

    def unit(self, u, back=0, each=16):
        return self.n * each + u + 1 - back

    def past_unit(self, u, back, each=16):
        return not self.known or self.n * each + u >= back

    def before(self, back=1, each=1):
        return (self.n + 1 - back) * each


def over_tiles(eng, stages, work, halves=HALF, unroll=2):
    if unroll > 2:
        halves = halves * 2 // unroll
    lag = -(-stages // unroll)
    first = lag + 1
    for step in range(first):
        for p in range(unroll):
            work(lambda s, a=step, b=p: Tile(a, b, s, halves, unroll))
    with eng.Fori(first, halves) as step:
        for p in range(unroll):
            work(lambda s, a=step, b=p: Tile(a, b, s, halves, unroll))
    for step in range(halves, halves + lag):
        for p in range(unroll):
            work(lambda s, a=step, b=p: Tile(a, b, s, halves, unroll))





class Tail:

    def __init__(self, m, name, forms, scratch=None):
        self.m, self.forms = m, forms
        self.bnst, self.mv, self.rstd = scratch or (m.bnst, m.mv, m.rstd)
        self.x_new = m.sem(name + "_x_new")
        self.stats_done = m.sem(name + "_stats_done")
        self.mv_ready = m.sem(name + "_mv_ready")
        self.kept = m.sem(name + "_mv_kept")
        self.pool_step = m.sem(name + "_norm_step")
        self.steps = 1 + 3 * len(forms)

    def dve(self, dve, t):
        m, nc = self.m, self.m.nc
        dve.wait_ge(self.x_new, t.nth())
        nc.vector.memset(m.gate[:, 0:1], 0.0)
        nc.vector.bn_stats(self.bnst[:, t.par, :], m.X[:, t.cols()]).then_inc(self.stats_done, 1)
        dve.wait_ge(self.stats_done, t.nth())
        if t.past(2):
            dve.wait_ge(self.pool_step, t.before(2, self.steps))
        nc.vector.memset(m.gate[:, 1:2], 0.0)
        nc.vector.bn_aggr(self.mv[:, t.par, :], self.bnst[:, t.par, :]).then_inc(self.mv_ready, 1)

    def dve_all(self, dve, x_in):
        m, nc = self.m, self.m.nc
        for n in range(TILES + 1):
            if n < TILES:
                if n % HALF == 0:
                    dve.wait_ge(x_in[n // HALF], 16)
                if n >= 2:
                    dve.wait_ge(self.kept, n - 1)
                nc.vector.bn_stats(self.bnst[:, n % 2, :], m.X[:, n * D:(n + 1) * D]).then_inc(self.stats_done, 1)
            if n >= 1:
                dve.wait_ge(self.stats_done, n)
                nc.vector.bn_aggr(m.mv_all[:, 2 * (n - 1):2 * n], self.bnst[:, (n - 1) % 2, :]).then_inc(self.kept, 1)

    def pool_all(self, pool):
        m, nc = self.m, self.m.nc
        pool.wait_ge(self.kept, TILES)
        mv = m.mv_all[:, :].rearrange("p (t k) -> p t k", k=2)
        f = m.factor[:, :]
        const = lambda k: m.const[:, k:k + 1].broadcast_to([P, TILES])
        step = 0
        for out, a, b in self.forms:
            for dst, x, y, op in ((f, mv[:, :, 1], a, ALU.mult), (f, f, b, ALU.add), (out[:, :], f, C_POW, ALU.pow)):
                if step:
                    pool.wait_ge(self.pool_step, step)
                nc.gpsimd.tensor_tensor(dst, x, const(y), op).then_inc(self.pool_step, 1)
                step += 1
        nc.gpsimd.tensor_tensor(m.MEAN[:, :], mv[:, :, 0], const(C_ONES), ALU.mult).then_inc(self.pool_step, 1)

    def pool(self, pool, t):
        m, nc = self.m, self.m.nc
        pool.wait_ge(self.mv_ready, t.nth())
        step = t.before(1, self.steps)
        if t.past():
            pool.wait_ge(self.pool_step, step)
        mv = self.mv[:, t.par, :]
        for out, a, b in self.forms:
            r = self.rstd[:, 0:1]
            for n, (dst, x, y, op) in enumerate(((r, mv[:, 1:2], a, ALU.mult), (r, r, b, ALU.add),
                                                 (out[:, t.cols(1)], r, C_POW, ALU.pow))):
                nc.gpsimd.tensor_tensor(dst, x, m.const[:, y:y + 1], op).then_inc(self.pool_step, 1)
                step = step + 1
                pool.wait_ge(self.pool_step, step)
        nc.gpsimd.tensor_tensor(m.MEAN[:, t.cols(1)], mv[:, 0:1], m.const[:, C_ONES:C_ONES + 1],
                                ALU.mult).then_inc(self.pool_step, 1)


def normed(m, out, t, factor):
    return m.nc.vector.tensor_scalar(out, m.X[:, t.cols()], m.MEAN[:, t.cols(1)], factor[:, t.cols(1)],
                                     ALU.subtract, ALU.mult)


class Chip:
    pass


def sinks(m, which):
    return {"z": (m.RZ, C_Z, C_Z + 1), "ln": (m.RN, C_LN, C_LN + 1), "rms": (m.RN, C_RMS, C_RMS + 1)}[which]


def setup_pass(m):
    nc = m.nc
    loaded = m.sem("weights_loaded")
    x_in = [m.sem("x_in_a"), m.sem("x_in_b")]
    folded = m.sem("folded")
    evac = m.sem("fold_evacuated")
    zeroed = m.sem("setup_zeroed")
    tail = Tail(m, "setup", [sinks(m, "z")])
    loads = m.setup_loads
    c = m.const
    ones_row = c[0:1, C_ONES:C_ONES + P]
    ws = m.w

    with nc.Block() as block:
        @block.sync
        def _(sp):
            for n in range(2):
                sp.dma_start(m.X[:, n * 2048:(n + 1) * 2048].rearrange("p (t d) -> p t d", d=D),
                             m.x_dram[n * 16:(n + 1) * 16].rearrange("t p d -> p t d")).then_inc(x_in[n], 16)
            for dst, src in loads:
                sp.dma_start(dst, src).then_inc(loaded, 16)

        @block.tensor
        def _(pe):
            pe.wait_ge(loaded, 16 * len(loads))
            mm = nc.tensor.matmul
            one = dict(start=True, stop=True)
            mm(m.ps[0][:, 0:D], ws["Wq0"][:, :], ws["Wk0"][:, :], **one)
            mm(m.ps[0][:, D:D + 1], ws["Wk0"][:, :], m.cols[:, m.c_bq0:m.c_bq0 + 1], **one)
            mm(m.ps[1][:, 0:D], ws["Wv0"][:, :], ws["Wo0T"][:, :], **one).then_inc(folded, 1)
            bias = [("bv0", "Wo0T", 0), ("bv_a", "Wf", 1), (None, None, 2)]
            for n, (vec, wt, row) in enumerate(bias):
                dst = m.ps[2 + n][:, 0:D]
                if vec:
                    k = m.colidx[vec]
                    mm(dst, m.cols[:, k:k + 1].broadcast_to([D, P]), ws[wt][:, :], start=True, stop=False)
                mm(dst, ones_row, m.rows[0:1, row * D:(row + 1) * D], start=not vec, stop=True).then_inc(folded, 1)
            mm(m.ps[5][:, 0:LEN], ws["Wpos"][:, :], c[:, C_PE:C_PE + LEN], **one).then_inc(folded, 1)

        @block.vector
        def _(dve):
            nc.vector.memset(m.ptab[:, :, :], 0.0).then_inc(zeroed, 1)
            tail.dve_all(dve, x_in)
            dve.wait_ge(folded, 5)
            dve.wait_ge(zeroed, 1)
            s0 = float(D) ** -0.5
            nc.vector.tensor_scalar(m.M0[:, :], m.ps[0][:, 0:D], 1.0, None, ALU.mult).then_inc(evac, 1)
            nc.vector.tensor_scalar(m.c0[:, :], m.ps[0][:, D:D + 1], s0, None, ALU.mult).then_inc(evac, 1)
            nc.vector.tensor_copy(m.N0[:, :], m.ps[1][:, 0:D]).then_inc(evac, 1)
            for n, dst in enumerate((m.b0, m.bA, m.bX)):
                nc.vector.tensor_copy(dst[:, :], m.ps[2 + n][:, 0:D]).then_inc(evac, 1)
            nc.vector.tensor_tensor(
                m.ptab[:, :, 1:1 + LEN],
                m.ps[5][:, 0:LEN].unsqueeze(1).broadcast_to([P, H, LEN]),
                c[:, C_M16:C_M16 + H].unsqueeze(2).broadcast_to([P, H, LEN]), ALU.mult).then_inc(evac, 1)
            for k, (a, b) in enumerate(((m.colidx["bq_a"], m.colidx["u"]), (m.colidx["bq_a"], m.colidx["v"]))):
                nc.vector.tensor_tensor(m.bqu[:, k:k + 1], m.cols[:, a:a + 1], m.cols[:, b:b + 1],
                                        ALU.add).then_inc(evac, 1)

        @block.gpsimd
        def _(pool):
            pool.wait_ge(loaded, 16 * len(loads))
            tail.pool_all(pool)


def cross_one_head(m):
    nc = m.nc
    ctx_in = [m.sem("p1_ctx_in_a"), m.sem("p1_ctx_in_b")]
    rows_in = [m.sem("p1_rows_in_a"), m.sem("p1_rows_in_b")]
    s = {n: m.sem("p1_" + n) for n in (
        "zT_ps", "zT", "q_ps", "q", "scores", "maxed", "probs", "pT_ps", "pT", "o_ps", "o", "oT_ps", "oT", "y_ps",
        "recip", "xb", "z", "z2", "z2T_ps", "z2T", "q2_ps", "q2")}
    gamma, beta = m.colidx["gamma"], m.colidx["beta"]
    tail = Tail(m, "p1", [sinks(m, "ln")])
    ident = m.const[:, C_ID:C_ID + P]
    ps = m.ps
    s0 = float(D) ** -0.5
    with ExitStack() as own, nc.Block() as block:
        sb = lambda n, shape: own.enter_context(nc.sbuf_tensor("p1_" + n, shape, F32))
        ctxT = sb("ctxT", [P, 2, B4, CTX])
        ctxN = sb("ctxN", [KC, 2, B4, 3, D])
        z, o, zT, qT, oT = sb("z", [P, 2, D]), sb("o", [P, 2, D]), sb("zT", [P, 2, P]), sb("qT", [P, 2, P]), sb("oT", [P, 2, P])
        prob = sb("prob", [P, 2, CTX])
        pT = sb("pT", [KC, 2, 3, P])
        xb = sb("xb", [P, 2, D])
        z2, z2T = sb("z2", [P, 2, D]), sb("z2T", [P, 2, P])
        nmax, total, recip = sb("nmax", [P, 2]), sb("total", [P, 4]), sb("recip", [P, 2])
        STAGES = 9

        def bank_read(pe, a, b, read_a, read_b):
            if a.known and not a.live:
                pe.wait_ge(s[read_a], TILES)
            elif a.past():
                pe.wait_ge(s[read_a], a.before())
            if b.live and b.past():
                pe.wait_ge(s[read_b], b.before())

        @block.sync
        def _(sp):
            def work(at):
                t = at(0)
                if t.live:
                    if t.past(2):
                        sp.wait_ge(s["scores"], t.before(2))
                    sp.dma_start(ctxT[:, t.par], m.ctxT_dram[:, t.cols(B4 * CTX)].rearrange(
                        "d (b k) -> d b k", k=CTX)).then_inc(ctx_in[t.par], 16)
                t = at(2)
                if t.live:
                    if t.past(2):
                        sp.wait_ge(s["o_ps"], t.before(2))
                    sp.dma_start(ctxN[:, t.par], m.ctxN_dram[DS(t.n, 1)].rearrange(
                        "a p (b c d) -> p (a b) c d", b=B4, c=3)).then_inc(rows_in[t.par], 16)
            over_tiles(sp, 2, work)

        @block.tensor
        def _(pe):
            def work(at):
                t = at(2)
                if t.live:
                    pe.wait_ge(s["q"], t.nth())
                    pe.wait_ge(ctx_in[t.par], t.nth_of_pair(16))
                    if t.past(2):
                        pe.wait_ge(s["probs"], t.before(2))
                    for b in range(B4):
                        last = nc.tensor.matmul(ps[3 + t.par][b * LEN:(b + 1) * LEN, 0:CTX],
                                                qT[:, t.par, b * LEN:(b + 1) * LEN], ctxT[:, t.par, b, :],
                                                start=True, stop=True, tile_position=(0, b * LEN))
                    last.then_inc(s["scores"], 1)
                t = at(3)
                if t.live:
                    pe.wait_ge(s["probs"], t.nth())
                    if t.past():
                        pe.wait_ge(s["pT"], t.before())
                    for c, (k0, rows) in enumerate(CHUNKS):
                        last = nc.tensor.transpose(ps[5][:rows, c * P:(c + 1) * P], prob[:, t.par, k0:k0 + rows], ident)
                    last.then_inc(s["pT_ps"], 1)
                t = at(6)
                if t.live:
                    pe.wait_ge(s["oT"], t.nth())
                    if t.past():
                        pe.wait_ge(tail.x_new, t.before())
                    nc.tensor.matmul(ps[7][:, 0:D], oT[:, t.par, :], m.N0[:, :], start=True, stop=True).then_inc(s["y_ps"], 1)
                t, t2 = at(1), at(9)
                if t.live or t2.live:
                    bank_read(pe, t, t2, "q", "q2")
                if t.live:
                    pe.wait_ge(s["zT"], t.nth())
                    nc.tensor.matmul(ps[2][:, 0:P], m.M0[:, :], zT[:, t.par, :], start=True, stop=True).then_inc(s["q_ps"], 1)
                if t2.live:
                    pe.wait_ge(s["z2T"], t2.nth())
                    nc.tensor.matmul(ps[2][:, P:2 * P], m.w["Wq_a"][:, :], z2T[:, t2.par, :],
                                     start=True, stop=True).then_inc(s["q2_ps"], 1)
                t = at(5)
                if t.live:
                    pe.wait_ge(s["o"], t.nth())
                    if t.past():
                        pe.wait_ge(s["oT"], t.before())
                    nc.tensor.transpose(ps[1][:, 0:P], o[:, t.par, :], ident).then_inc(s["oT_ps"], 1)
                t, t2 = at(0), at(8)
                if t.live or t2.live:
                    bank_read(pe, t, t2, "zT", "z2T")
                if t.live:
                    pe.wait_ge(s["z"], t.nth())
                    nc.tensor.transpose(ps[0][:, 0:P], z[:, t.par, :], ident).then_inc(s["zT_ps"], 1)
                if t2.live:
                    pe.wait_ge(s["z2"], t2.nth())
                    nc.tensor.transpose(ps[0][:, P:2 * P], z2[:, t2.par, :], ident).then_inc(s["z2T_ps"], 1)
                t = at(4)
                if t.live:
                    pe.wait_ge(s["pT"], t.nth())
                    pe.wait_ge(rows_in[t.par], t.nth_of_pair(16))
                    if t.past():
                        pe.wait_ge(s["o"], t.before())
                    for c, (_, rows) in enumerate(CHUNKS):
                        for b in range(B4):
                            last = nc.tensor.matmul(ps[6][b * LEN:(b + 1) * LEN, 0:D],
                                                    pT[:rows, t.par, c, b * LEN:(b + 1) * LEN],
                                                    ctxN[:rows, t.par, b, c, :], start=(c == 0), stop=(c == 2),
                                                    tile_position=(0, b * LEN))
                    last.then_inc(s["o_ps"], 1)
            over_tiles(pe, STAGES, work)

        @block.scalar
        def _(act):
            def work(at):
                t, t2 = at(1), at(9)
                if t2.live:
                    act.wait_ge(s["q2_ps"], t2.nth())
                if t.live:
                    act.wait_ge(s["q_ps"], t.nth())
                    if t.past(2):
                        act.wait_ge(s["scores"], t.before(2))
                    nc.scalar.activation(qT[:, t.par, :], ps[2][:, 0:P], ACT.Identity, scale=s0,
                                         bias=m.c0[:, 0:1]).then_inc(s["q"], 1)
                if t2.live:
                    nc.scalar.activation(m.QV[:, t2.cols()], ps[2][:, P:2 * P], ACT.Identity,
                                         bias=m.bqu[:, 1:2]).then_inc(s["q2"], 1)
                t = at(2)
                if t.live:
                    act.wait_ge(s["maxed"], t.nth())
                    if t.past(2):
                        act.wait_ge(s["pT_ps"], t.before(2))
                        act.wait_ge(s["recip"], t.before(2))
                    nc.scalar.activation(prob[:, t.par, :], ps[3 + t.par][:, 0:CTX], ACT.Exp,
                                         bias=nmax[:, t.par:t.par + 1],
                                         accum_out=total[:, t.par:t.par + 1]).then_inc(s["probs"], 1)
                t, t2 = at(0), at(8)
                if t2.live:
                    act.wait_ge(s["z2T_ps"], t2.nth())
                if t.live:
                    act.wait_ge(s["zT_ps"], t.nth())
                    if t.past(2):
                        act.wait_ge(s["q_ps"], t.before(2))
                    nc.scalar.activation(zT[:, t.par, :], ps[0][:, 0:P], ACT.Copy).then_inc(s["zT"], 1)
                if t2.live:
                    if t2.past(2):
                        act.wait_ge(s["q2_ps"], t2.before(2))
                    nc.scalar.activation(z2T[:, t2.par, :], ps[0][:, P:2 * P], ACT.Identity,
                                         scale=m.cols[:, gamma:gamma + 1],
                                         bias=m.cols[:, beta:beta + 1]).then_inc(s["z2T"], 1)
                t = at(5)
                if t.live:
                    act.wait_ge(s["oT_ps"], t.nth())
                    if t.past(2):
                        act.wait_ge(s["y_ps"], t.before(2))
                    nc.scalar.activation(oT[:, t.par, :], ps[1][:, 0:P], ACT.Copy).then_inc(s["oT"], 1)
                t = at(4)
                if t.live:
                    act.wait_ge(s["o_ps"], t.nth())
                    act.wait_ge(s["recip"], t.nth())
                    if t.past(2):
                        act.wait_ge(s["oT_ps"], t.before(2))
                    nc.scalar.activation(o[:, t.par, :], ps[6][:, 0:D], ACT.Copy,
                                         scale=recip[:, t.par:t.par + 1]).then_inc(s["o"], 1)
            over_tiles(act, STAGES, work)

        @block.vector
        def _(dve):
            def work(at):
                t = at(0)
                if t.live:
                    if t.past(2):
                        dve.wait_ge(s["zT_ps"], t.before(2))
                    normed(m, z[:, t.par, :], t, m.RZ).then_inc(s["z"], 1)
                t = at(2)
                if t.live:
                    dve.wait_ge(s["scores"], t.nth())
                    if t.past(2):
                        dve.wait_ge(s["probs"], t.before(2))
                    nc.vector.tensor_reduce(nmax[:, t.par:t.par + 1], ps[3 + t.par][:, 0:CTX], AX.X, ALU.max,
                                            negate=True).then_inc(s["maxed"], 1)
                t = at(3)
                if t.live:
                    dve.wait_ge(s["pT_ps"], t.nth())
                    if t.past(2):
                        dve.wait_ge(s["o_ps"], t.before(2))
                    nc.vector.tensor_copy(pT[:85, t.par, 2, :], ps[5][:85, 2 * P:3 * P])
                    nc.vector.tensor_copy(pT[:KC, t.par, 0:2, :], ps[5][:KC, 0:2 * P]).then_inc(s["pT"], 1)
                    if t.past(2):
                        dve.wait_ge(s["o"], t.before(2))
                    nc.vector.reciprocal(recip[:, t.par:t.par + 1], total[:, t.par:t.par + 1]).then_inc(s["recip"], 1)
                t = at(6)
                if t.live:
                    dve.wait_ge(s["y_ps"], t.nth())
                    dve.wait_ge(s["xb"], t.nth())
                    nc.vector.tensor_tensor(m.X[:, t.cols()], ps[7][:, 0:D], xb[:, t.par, :],
                                            ALU.add).then_inc(tail.x_new, 1)
                    tail.dve(dve, t)
                t = at(7)
                if t.live:
                    dve.wait_ge(tail.pool_step, t.nth(tail.steps))
                    if t.past(2):
                        dve.wait_ge(s["z2T_ps"], t.before(2))
                    normed(m, z2[:, t.par, :], t, m.RN).then_inc(s["z2"], 1)
            over_tiles(dve, STAGES, work)

        @block.gpsimd
        def _(pool):
            def work(at):
                t = at(4)
                if t.live:
                    if t.past(2):
                        pool.wait_ge(tail.x_new, t.before(2))
                    nc.gpsimd.tensor_tensor(xb[:, t.par, :], m.X[:, t.cols()], m.b0[:, :], ALU.add).then_inc(s["xb"], 1)
                t = at(6)
                if t.live:
                    tail.pool(pool, t)
            over_tiles(pool, STAGES, work)


def relative_scores(m):
    nc, ps = m.nc, m.ps
    done, moved, stored = m.sem("p3_done"), m.sem("p3_moved"), [m.sem(f"p3_stored{n}") for n in range(4)]
    moved_a = m.sem("p3_moved_a")
    with ExitStack() as own, nc.Block() as block:
        rows = own.enter_context(nc.sbuf_tensor("p3_rows", [P, 4, H * LEN], F32))

        @block.tensor
        def _(pe):
            for i in range(LEN):
                if i >= 8:
                    pe.wait_ge(moved_a if i % 2 else moved, (i - 8) // 2 + 1)
                bank = ps[i % 8][:, :].rearrange("p (h j) -> p h j", j=LEN)
                last = nc.tensor.matmul(bank[:, :, 0:i + 1], m.QV[:, i::LEN], m.ptab[:, :, LEN - i:LEN + 1],
                                        start=True, stop=(i == LEN - 1))
                if i < LEN - 1:
                    last = nc.tensor.matmul(bank[:, :, i + 1:LEN], m.QV[:, i + 1::LEN], m.ptab[:, :, 0:LEN - 1 - i],
                                            start=False, stop=True)
                last.then_inc(done, 1)

        @block.vector
        def _(dve):
            for i in range(0, LEN, 2):
                dve.wait_ge(done, i + 1)
                if i >= 4:
                    dve.wait_ge(stored[i % 4], 16 * (i // 4))
                nc.vector.tensor_copy(rows[:, i % 4, :], ps[i % 8][:, :]).then_inc(moved, 1)

        @block.scalar
        def _(act):
            for i in range(1, LEN, 2):
                act.wait_ge(done, i + 1)
                if i >= 4:
                    act.wait_ge(stored[i % 4], 16 * (i // 4))
                nc.scalar.activation(rows[:, i % 4, :], ps[i % 8][:, :], ACT.Copy).then_inc(moved_a, 1)

        @block.sync
        def _(sp):
            for i in range(LEN):
                sp.wait_ge(moved_a if i % 2 else moved, i // 2 + 1)
                sp.dma_start(m.bd_dram[:, i, :], rows[:, i % 4, :]).then_inc(stored[i % 4], 16)
            for n in range(4):
                sp.wait_ge(stored[n], 16 * (LEN // 4))


def self_attention(m, name, relative):
    nc, ps, c = m.nc, m.ps, m.const
    s = {n: m.sem(name + "_" + n) for n in (
        "z", "zT_ps", "zT", "qk_ps", "v_ps", "q", "k", "v", "k_dve", "k_pool", "scores", "summed", "maxed",
        "shifted", "probs", "pT_ps", "pT", "o_ps", "recip", "o", "oT_ps", "oT", "y_ps", "xb", "zres", "ones",
        "experts_in", "b1_ps", "scaled")}
    bd_in = [m.sem(name + "_bd_in_a"), m.sem(name + "_bd_in_b")]
    tail = Tail(m, name, [sinks(m, "z")] + ([sinks(m, "ln")] if relative else []))
    ident = c[:, C_ID:C_ID + P]
    col = lambda n: m.cols[:, m.colidx[n]:m.colidx[n] + 1]
    scale = float(D if relative else HD) ** -0.5
    STAGES = 5
    BY_DVE = 3 if relative else 2
    BY_POOL = B4 - BY_DVE
    with ExitStack() as own, nc.Block() as block:
        sb = lambda n, shape: own.enter_context(nc.sbuf_tensor(name + "_" + n, shape, F32))
        z, qT, kT = (sb(n, [P, 2, P]) for n in ("z", "qT", "kT"))
        zT4 = sb("zT4", [P, 2, B4, H4, LEN])
        k_all = sb("k_all", [P, 2, B4, H, LEN])
        v_all = sb("v_all", [P, 2, B4 * G, H4, HD + 1])
        bd = sb("bd", [P, 2, H * LEN])
        score, prob = sb("score", [P, 2, H * LEN]), sb("prob", [P, 2, H * LEN])
        mx, recip = sb("mx", [P, 2, H]), sb("recip", [P, 2, H])
        pT = sb("pT", [P, 2, G, P])
        o, oT, xb, zres = (sb(n, [P, 2, P]) for n in ("o", "oT", "xb", "zres"))
        wq = m.w["Wq_a" if relative else "w_q"][:, :]
        if relative:
            wk, wv = m.w["Wk_a"][:, :], m.w["Wv_a"][:, :]
        else:
            wk, wv = m.w["w_k"][:, :], m.w["w_v"][:, :]
        wo = m.w["Wf" if relative else "w_o"][:, :]
        rope = c[:, C_ROPE:C_ROPE + LEN].unsqueeze(1).broadcast_to([P, B4, LEN])
        by_seq = lambda ap: ap.rearrange("p (b i) -> p b i", i=LEN)
        by_head = lambda ap: ap.rearrange("p (h j) -> p h j", j=LEN)

        @block.sync
        def _(sp):
            def work(at):
                t = at(2)
                if t.live:
                    if t.past(2):
                        sp.wait_ge(s["summed"], t.before(2))
                    sp.dma_start(bd[:, t.par, :], m.bd_dram.rearrange("s i n -> (s i) n")[t.cols(), :]
                                 ).then_inc(bd_in[t.par], 16)
            if relative:
                for dst, src in ((m.w1, "w1_0"), (m.w2, "w2_0"), (m.ln_w, "ln_wT"), (m.ln_b, "ln_bT"), (m.b1, "b1_T")):
                    sp.dma_start(dst[:, :], m.a[src]).then_inc(s["experts_in"], 16)
                sp.dma_start(m.bias[:, :].rearrange("p (e f) -> p e f", e=E)[:, :, 0:D],
                             m.a["b2"].rearrange("p (e d) -> p e d", e=E)).then_inc(s["experts_in"], 16)
                over_tiles(sp, 2, work)
                sp.wait_ge(s["experts_in"], 16 * 6)

        @block.tensor
        def _(pe):
            def work(at):
                t = at(3)
                if t.live:
                    pe.wait_ge(s["q"], t.nth())
                    pe.wait_ge(s["k_dve"], t.nth(BY_DVE))
                    pe.wait_ge(s["k_pool"], t.nth(BY_POOL))
                    if t.past(2):
                        pe.wait_ge(s["summed"], t.before(2))
                    for b in range(B4):
                        last = nc.tensor.matmul(ps[3 + t.par][b * LEN:(b + 1) * LEN, :],
                                                qT[:, t.par, b * LEN:(b + 1) * LEN], k_all[:, t.par, b],
                                                start=True, stop=True, tile_position=(0, b * LEN))
                    last.then_inc(s["scores"], 1)
                t = at(1)
                if t.live:
                    pe.wait_ge(s["zT"], t.nth())
                    if t.past():
                        pe.wait_ge(s["q"], t.before())
                        pe.wait_ge(s["k"], t.before())
                    nc.tensor.matmul(ps[1][:, 0:P], wq, zT4[:, t.par, :, 0, :], start=True, stop=True)
                    nc.tensor.matmul(ps[1][:, P:2 * P], wk, zT4[:, t.par, :, 0, :], start=True, stop=True).then_inc(s["qk_ps"], 1)
                t = at(4)
                if t.live:
                    pe.wait_ge(s["probs"], t.nth())
                    if t.past():
                        pe.wait_ge(s["pT"], t.before())
                    for g in range(G):
                        last = nc.tensor.transpose(ps[5][:, g * P:(g + 1) * P], prob[:, t.par, g * P:(g + 1) * P], ident)
                    last.then_inc(s["pT_ps"], 1)
                t = at(2)
                if t.live:
                    if t.past():
                        pe.wait_ge(s["v"], t.before(1, H4))
                    for b in range(B4):
                        last = nc.tensor.matmul(ps[2][:, b * D:(b + 1) * D], zT4[:, t.par, b], wv, start=True, stop=True)
                    last.then_inc(s["v_ps"], 1)
                t = at(5)
                if t.live:
                    pe.wait_ge(s["o"], t.nth())
                    if t.past():
                        pe.wait_ge(tail.x_new, t.before())
                    nc.tensor.transpose(ps[7][:, P:2 * P], o[:, t.par, :], ident).then_inc(s["oT_ps"], 1)
                t = at(4)
                if t.live:
                    pe.wait_ge(s["pT"], t.nth())
                    pe.wait_ge(s["v"], t.nth(H4))
                    if t.past():
                        pe.wait_ge(s["o"], t.before())
                    for b in range(B4):
                        for g in range(G):
                            w = H4 * (HD + 1)
                            last = nc.tensor.matmul(ps[6][b * LEN:(b + 1) * LEN, g * w:(g + 1) * w],
                                                    pT[:, t.par, g, b * LEN:(b + 1) * LEN],
                                                    v_all[:, t.par, b * G + g], start=True, stop=True,
                                                    tile_position=(0, b * LEN))
                    last.then_inc(s["o_ps"], 1)
                t = at(5)
                if t.live:
                    pe.wait_ge(s["oT"], t.nth())
                    nc.tensor.matmul(ps[7][:, 0:D], oT[:, t.par, :], wo, start=True, stop=True).then_inc(s["y_ps"], 1)
                t = at(0)
                if t.live:
                    pe.wait_ge(s["z"], t.nth())
                    if t.past():
                        pe.wait_ge(s["zT"], t.before())
                    nc.tensor.transpose(ps[0][:, 0:P], z[:, t.par, :], ident).then_inc(s["zT_ps"], 1)
                t = at(0)
                if relative and t.known and t.n in range(TILES, TILES + E // 2):
                    pe.wait_ge(s["experts_in"], 16 * 6)
                    pe.wait_ge(s["zT"], TILES)
                    for e in range(2 * (t.n - TILES), 2 * (t.n - TILES) + 2):
                        for k in range(e * FC, (e + 1) * FC):
                            last = nc.tensor.matmul(ps[0][:, k:k + 1], m.w1[:, k * P:(k + 1) * P], m.ln_b[:, e:e + 1],
                                                    start=True, stop=True)
                        last.then_inc(s["b1_ps"], 1)
            over_tiles(pe, STAGES, work)

        @block.scalar
        def _(act):
            def work(at):
                t = at(1)
                if t.live and relative:
                    act.wait_ge(s["qk_ps"], t.nth())
                    if t.past(2):
                        act.wait_ge(s["scores"], t.before(2))
                    nc.scalar.activation(qT[:, t.par, :], ps[1][:, 0:P], ACT.Identity,
                                         bias=m.bqu[:, 0:1]).then_inc(s["q"], 1)
                    if t.past(2):
                        act.wait_ge(s["k_dve"], t.before(2, BY_DVE))
                        act.wait_ge(s["k_pool"], t.before(2, BY_POOL))
                    nc.scalar.activation(kT[:, t.par, :], ps[1][:, P:2 * P], ACT.Identity,
                                         bias=col("bk_a")).then_inc(s["k"], 1)
                t = at(4)
                if t.live:
                    act.wait_ge(s["pT_ps"], t.nth())
                    if t.past(2):
                        act.wait_ge(s["o_ps"], t.before(2))
                    nc.scalar.activation(pT[:, t.par], ps[5][:, :].rearrange("p (g n) -> p g n", g=G),
                                         ACT.Copy).then_inc(s["pT"], 1)
                t = at(5)
                if t.live:
                    act.wait_ge(s["oT_ps"], t.nth())
                    if t.past(2):
                        act.wait_ge(s["y_ps"], t.before(2))
                    nc.scalar.activation(oT[:, t.par, :], ps[7][:, P:2 * P], ACT.Copy).then_inc(s["oT"], 1)
                t = at(2)
                if t.live:
                    act.wait_ge(s["v_ps"], t.nth())
                    act.wait_ge(s["ones"], 3)
                    if t.past(2):
                        act.wait_ge(s["o_ps"], t.before(2))
                    for h in range(H4):
                        rows = slice(h * LEN, (h + 1) * LEN)
                        nc.scalar.activation(v_all[rows, t.par, :, h, 0:HD],
                                             ps[2][rows, :].rearrange("p (n h d) -> p n h d", h=H4, d=HD)[:, :, h, :],
                                             ACT.Copy).then_inc(s["v"], 1)
                t = at(0)
                if t.live:
                    act.wait_ge(s["zT_ps"], t.nth())
                    if t.past(2):
                        act.wait_ge(s["v_ps"], t.before(2))
                    four = by_seq(ps[0][:, 0:P]).unsqueeze(2).broadcast_to([P, B4, H4, LEN])
                    if relative:
                        nc.scalar.activation(zT4[:, t.par], four, ACT.Identity, scale=col("gamma"),
                                             bias=col("beta")).then_inc(s["zT"], 1)
                    else:
                        nc.scalar.activation(zT4[:, t.par], four, ACT.Copy,
                                             scale=col("norm_w")).then_inc(s["zT"], 1)
                t = at(3)
                if t.live:
                    act.wait_ge(s["shifted"], t.nth())
                    if t.past(2):
                        act.wait_ge(s["pT_ps"], t.before(2))
                    nc.scalar.activation(prob[:, t.par, :], score[:, t.par, :], ACT.Exp, scale=scale).then_inc(s["probs"], 1)
                t = at(1)
                if relative and t.known and t.n in range(TILES, TILES + E // 2):
                    for e in range(2 * (t.n - TILES), 2 * (t.n - TILES) + 2):
                        act.wait_ge(s["b1_ps"], e + 1)
                        w = m.w1[:, e * F:(e + 1) * F]
                        nc.scalar.activation(w, w, ACT.Copy, scale=m.ln_w[:, e:e + 1]).then_inc(s["scaled"], 1)
            over_tiles(act, STAGES, work)

        @block.vector
        def _(dve):
            def spread(t, b):
                return nc.vector.tensor_tensor(
                    k_all[:, t.par, b], kT[:, t.par, b * LEN:(b + 1) * LEN].unsqueeze(1).broadcast_to([P, H, LEN]),
                    c[:, C_M16:C_M16 + H].unsqueeze(2).broadcast_to([P, H, LEN]), ALU.mult)

            nc.vector.memset(v_all[:, :, :, :, :], 0.0).then_inc(s["ones"], 1)
            dve.wait_ge(s["ones"], 1)
            for par in range(2):
                nc.vector.tensor_copy(v_all[:, par, :, :, HD], c[:, C_M4P:C_M4P + H4].unsqueeze(1).broadcast_to(
                    [P, B4 * G, H4])).then_inc(s["ones"], 1)

            def work(at):
                t = at(2)
                if t.live:
                    dve.wait_ge(s["k"], t.nth())
                    if t.past(2):
                        dve.wait_ge(s["scores"], t.before(2))
                    for b in range(BY_DVE):
                        spread(t, b).then_inc(s["k_dve"], 1)
                t = at(0)
                if t.live:
                    if t.past(2):
                        dve.wait_ge(s["zT_ps"], t.before(2))
                    normed(m, z[:, t.par, :], t, m.RN).then_inc(s["z"], 1)
                t = at(4)
                if t.live and not relative:
                    if t.past(2):
                        dve.wait_ge(s["xb"], t.before(2))
                    normed(m, zres[:, t.par, :], t, m.RZ).then_inc(s["zres"], 1)
                t = at(1)
                if t.live and not relative:
                    dve.wait_ge(s["qk_ps"], t.nth())
                    if t.past(2):
                        dve.wait_ge(s["scores"], t.before(2))
                        dve.wait_ge(s["k_pool"], t.before(2, BY_POOL))
                    nc.vector.tensor_tensor(by_seq(qT[:, t.par, :]), by_seq(ps[1][:, 0:P]), rope,
                                            ALU.mult).then_inc(s["q"], 1)
                    nc.vector.tensor_tensor(by_seq(kT[:, t.par, :]), by_seq(ps[1][:, P:2 * P]), rope,
                                            ALU.mult).then_inc(s["k"], 1)
                t = at(3)
                if t.live:
                    dve.wait_ge(s["scores"], t.nth())
                    if t.past(2):
                        dve.wait_ge(s["probs"], t.before(2))
                    if relative:
                        dve.wait_ge(bd_in[t.par], t.nth_of_pair(16))
                        more = by_head(bd[:, t.par, :])
                    else:
                        more = c[:, C_CAUSAL:C_CAUSAL + LEN].unsqueeze(1).broadcast_to([P, H, LEN])
                    nc.vector.tensor_tensor(by_head(score[:, t.par, :]), by_head(ps[3 + t.par][:, :]), more,
                                            ALU.add).then_inc(s["summed"], 1)
                    dve.wait_ge(s["summed"], t.nth())
                    if t.past(2):
                        dve.wait_ge(s["shifted"], t.before(2))
                    nc.vector.tensor_reduce(mx[:, t.par, :], by_head(score[:, t.par, :]), AX.X,
                                            ALU.max).then_inc(s["maxed"], 1)
                t = at(4)
                if t.live:
                    dve.wait_ge(s["o_ps"], t.nth())
                    if t.past(2):
                        dve.wait_ge(s["oT_ps"], t.before(2))
                    heads = ps[6][:, 0:H * (HD + 1)].rearrange("p (h n) -> p h n", n=HD + 1)
                    nc.vector.reciprocal(recip[:, t.par, :], heads[:, :, HD]).then_inc(s["recip"], 1)
                    dve.wait_ge(s["recip"], t.nth())
                    nc.vector.tensor_tensor(o[:, t.par, :].rearrange("p (h d) -> p h d", d=HD), heads[:, :, 0:HD],
                                            recip[:, t.par, :].unsqueeze(2).broadcast_to([P, H, HD]),
                                            ALU.mult).then_inc(s["o"], 1)
                t = at(5)
                if t.live:
                    dve.wait_ge(s["y_ps"], t.nth())
                    dve.wait_ge(s["xb"], t.nth())
                    nc.vector.tensor_tensor(m.X[:, t.cols()], ps[7][:, 0:D], xb[:, t.par, :],
                                            ALU.add).then_inc(tail.x_new, 1)
                    tail.dve(dve, t)
            over_tiles(dve, STAGES, work)
            if relative:
                dve.wait_ge(s["b1_ps"], E)
                nc.vector.tensor_tensor(m.bias[:, :].rearrange("p (e f) -> p e f", e=E)[:, :, D:D + FC],
                                        ps[0][:, 0:E * FC].rearrange("p (e f) -> p e f", f=FC),
                                        m.b1[:, :].rearrange("p (e f) -> p e f", f=FC), ALU.add).then_inc(s["scaled"], 1)

        @block.gpsimd
        def _(pool):
            def work(at):
                t = at(2)
                if t.live:
                    pool.wait_ge(s["k"], t.nth())
                    if t.past(2):
                        pool.wait_ge(s["scores"], t.before(2))
                    for b in range(BY_DVE, B4):
                        nc.gpsimd.tensor_tensor(
                            k_all[:, t.par, b],
                            kT[:, t.par, b * LEN:(b + 1) * LEN].unsqueeze(1).broadcast_to([P, H, LEN]),
                            c[:, C_M16:C_M16 + H].unsqueeze(2).broadcast_to([P, H, LEN]), ALU.mult).then_inc(s["k_pool"], 1)
                t = at(3)
                if t.live:
                    pool.wait_ge(s["maxed"], t.nth())
                    sc = by_head(score[:, t.par, :])
                    nc.gpsimd.tensor_tensor(sc, sc, mx[:, t.par, :].unsqueeze(2).broadcast_to([P, H, LEN]),
                                            ALU.subtract).then_inc(s["shifted"], 1)
                t = at(6)
                if t.live:
                    tail.pool(pool, t)
                t = at(4)
                if t.live:
                    if t.past(2):
                        pool.wait_ge(tail.x_new, t.before(2))
                    if relative:
                        more = m.bA[:, :]
                    else:
                        pool.wait_ge(s["zres"], t.nth())
                        more = zres[:, t.par, :]
                    nc.gpsimd.tensor_tensor(xb[:, t.par, :], m.X[:, t.cols()], more, ALU.add).then_inc(s["xb"], 1)
            over_tiles(pool, STAGES + 1, work)


def relative_attention(m):
    self_attention(m, "p4", True)


def causal_attention(m):
    self_attention(m, "p8", False)


def cross_many_heads(m):
    nc, ps, c = m.nc, m.ps, m.const
    N = B4 * G
    AHEAD = 4
    LAST = 2 * P
    s = {n: m.sem("p6_" + n) for n in (
        "z", "zT_ps", "zT", "q_ps", "q", "k_ps", "k", "v_ps", "v", "v_last", "scores", "maxed", "probs", "recip",
        "normed", "pT_ps", "pT", "last_ps", "last", "o_ps", "masked", "oT", "y_ps", "xb")}
    ctx_in = [m.sem("p6_ctx_in_a"), m.sem("p6_ctx_in_b")]
    experts_in = m.sem("p6_experts_in")
    y_in, added = [m.sem("p6_y_in_a"), m.sem("p6_y_in_b")], m.sem("p6_added")
    tail = Tail(m, "p6", [sinks(m, "z"), sinks(m, "rms")])
    ident = c[:, C_ID:C_ID + P]
    s0 = float(D) ** -0.5
    with ExitStack() as own, nc.Block() as block:
        sb = lambda n, shape: own.enter_context(nc.sbuf_tensor("p6_" + n, shape, F32))
        ctxT = sb("ctxT", [P, 2, B4, CTX])
        z, zT, oT, xb = (sb(n, [P, 2, P]) for n in ("z", "zT", "oT", "xb"))
        q_all = sb("q_all", [P, 2, B4, H4, LEN])
        kT = sb("kT", [P, 2, CTX])
        v, v_last = sb("v", [P, 2, 2, P]), sb("v_last", [G, 2, P])
        prob = sb("prob", [P, 2, G, CTX])
        nmax, total, recip = (sb(n, [P, N]) for n in ("nmax", "total", "recip"))
        pT, p_last = sb("pT", [P, 2, 2, P]), sb("p_last", [G, 2, P])
        masked = sb("masked", [P, H4, LEN])
        y = sb("y", [P, 2, TOPK * D])
        joined = Tail(m, "p6_joined", [sinks(m, "z")], (sb("bnst", [P, 2, 6]), sb("mv", [P, 2, 2]), sb("rstd", [P, 4])))
        gates = m.gates[:, :, :].rearrange("p t k -> p (t k)")
        results = m.ys_dram[0:TOPK * TOKENS, :].rearrange("(n k) d -> n (k d)", k=TOPK)

        @block.sync
        def _(sp):
            def work(at):
                t = at(0)
                if t.live:
                    if t.past(2):
                        sp.wait_ge(joined.x_new, t.before(2))
                    sp.dma_start(y[:, t.par, :], results[t.cols(), :]).then_inc(y_in[t.par], 16)
                t = at(2)
                if t.live:
                    if t.past(2):
                        sp.wait_ge(s["v_ps"], t.before(2, B4))
                    sp.dma_start(ctxT[:, t.par], m.ctxT_dram[:, t.cols(B4 * CTX)].rearrange(
                        "d (b k) -> d b k", k=CTX)).then_inc(ctx_in[t.par], 16)
            sp.dma_start(m.w1[:, :], m.a["w1_1"]).then_inc(experts_in, 16)
            sp.dma_start(m.w2[:, :], m.a["w2_1"]).then_inc(experts_in, 16)
            over_tiles(sp, 2, work)
            sp.wait_ge(experts_in, 32)

        @block.tensor
        def _(pe):
            def scores(t, u):
                b, g = u // G, u % G
                pe.wait_ge(s["q"], t.nth())
                pe.wait_ge(s["k"], t.unit(b, 0, B4))
                if t.past_unit(u, 2):
                    pe.wait_ge(s["probs"], t.unit(u, 2))
                rows = slice(32 * g, 32 * g + 32)
                nc.tensor.matmul(ps[3 + u % 2][:, 0:CTX], q_all[rows, t.par, b], kT[rows, b % 2, :],
                                 start=True, stop=True, tile_position=(32 * g, 0)).then_inc(s["scores"], 1)

            def keys(t, b):
                pe.wait_ge(ctx_in[t.par], t.nth_of_pair(16))
                if t.past_unit(b, 1, B4):
                    pe.wait_ge(s["k"], t.unit(b, 1, B4))
                nc.tensor.matmul(ps[1][:, 0:CTX], m.w["WkT_x"][:, :], ctxT[:, t.par, b, :],
                                 start=True, stop=True).then_inc(s["k_ps"], 1)

            def values(t, b):
                pe.wait_ge(ctx_in[t.par], t.nth_of_pair(16))
                if t.past_unit(b, 1, B4):
                    pe.wait_ge(s["v"], t.unit(b, 1, B4))
                    pe.wait_ge(s["v_last"], t.unit(b, 1, B4))
                for n in range(2):
                    nc.tensor.matmul(ps[2][:, n * P:(n + 1) * P], ctxT[:, t.par, b, n * P:(n + 1) * P],
                                     m.w["WvT_x"][:, :], start=True, stop=True)
                nc.tensor.matmul(ps[2][0:G, LAST:LAST + P], ctxT[:, t.par, b, LAST:LAST + 1].broadcast_to([P, G]),
                                 m.w["WvT_x"][:, :], start=True, stop=True).then_inc(s["v_ps"], 1)

            def turn(t, u):
                b, g = u // G, u % G
                pe.wait_ge(s["normed"], t.unit(u))
                bank = ps[5 + u % 2]
                if t.past_unit(u, 2):
                    pe.wait_ge(s["pT"], t.unit(u, 2))
                if u % 2 and t.past_unit(b, 1, B4):
                    pe.wait_ge(s["last"], t.unit(b, 1, B4))
                for n in range(2):
                    last = nc.tensor.transpose(bank[:, n * P:(n + 1) * P], prob[:, b % 2, g, n * P:(n + 1) * P], ident)
                last.then_inc(s["pT_ps"], 1)
                if g == G - 1:
                    nc.tensor.transpose(bank[0:G, LAST:LAST + P], prob[:, b % 2, :, LAST], ident).then_inc(s["last_ps"], 1)

            def weigh(t, u):
                b, g = u // G, u % G
                pe.wait_ge(s["pT"], t.unit(u))
                pe.wait_ge(s["v"], t.unit(b, 0, B4))
                if g == 0 and t.past_unit(b, 1, B4):
                    pe.wait_ge(s["masked"], t.unit(b, 1, B4))
                for n in range(2):
                    nc.tensor.matmul(ps[7][32 * g:32 * g + 32, 0:P], v[:, b % 2, n, 32 * g:32 * g + 32],
                                     pT[:, u % 2, n, :], start=(n == 0), stop=(n == 1),
                                     tile_position=(0, 32 * g), skip_group_check=True).then_inc(s["o_ps"], 1)
                if g == G - 1:
                    pe.wait_ge(s["last"], t.unit(b, 0, B4))
                    pe.wait_ge(s["v_last"], t.unit(b, 0, B4))
                    nc.tensor.matmul(ps[7][:, 0:P], v_last[:, b % 2, :], p_last[:, b % 2, :], start=False, stop=True,
                                     skip_group_check=True).then_inc(s["o_ps"], 1)

            def steps(at):
                cur, nxt, prev = at(3), at(2), at(4)
                for n in range(N):
                    t, b = (cur, n // G + 2) if n // G + 2 < B4 else (nxt, n // G + 2 - B4)
                    if n % G == 1 and t.live:
                        keys(t, b)
                    t, u = (cur, n + AHEAD) if n + AHEAD < N else (nxt, n + AHEAD - N)
                    if t.live:
                        scores(t, u)
                    t, b = (cur, n // G + 1) if n // G + 1 < B4 else (nxt, 0)
                    if n % G == 2 and t.live:
                        values(t, b)
                    if cur.live:
                        turn(cur, n)
                    t, u = (cur, n - 1) if n else (prev, N - 1)
                    if t.live:
                        weigh(t, u)
                    if n == 3 and prev.live:
                        pe.wait_ge(s["oT"], prev.nth(B4))
                        nc.tensor.matmul(ps[0][:, 2 * P:3 * P], oT[:, prev.par, :], m.w["WoT_x"][:, :],
                                         start=True, stop=True).then_inc(s["y_ps"], 1)
                    if n == 5 and nxt.live:
                        pe.wait_ge(s["z"], nxt.nth())
                        if nxt.past(2):
                            pe.wait_ge(tail.x_new, nxt.before(2))
                        nc.tensor.transpose(ps[0][:, 0:P], z[:, nxt.par, :], ident).then_inc(s["zT_ps"], 1)
                    if n == 7 and nxt.live:
                        pe.wait_ge(s["zT"], nxt.nth())
                        nc.tensor.matmul(ps[0][:, P:2 * P], m.w["WqT_x"][:, :], zT[:, nxt.par, :],
                                         start=True, stop=True).then_inc(s["q_ps"], 1)
            over_tiles(pe, 4, steps)

        @block.scalar
        def _(act):
            def steps(at):
                cur, nxt = at(3), at(2)
                for n in range(N):
                    t, u = (cur, n + AHEAD) if n + AHEAD < N else (nxt, n + AHEAD - N)
                    if t.live:
                        act.wait_ge(s["maxed"], t.unit(u))
                        if t.past_unit(u, 8):
                            act.wait_ge(s["pT_ps"], t.unit(u, 8))
                        if u % G == 0 and t.past_unit(u // G, 2, B4):
                            act.wait_ge(s["last_ps"], t.unit(u // G, 2, B4))
                        nc.scalar.activation(prob[:, u // G % 2, u % G, :], ps[3 + u % 2][:, 0:CTX], ACT.Exp,
                                             bias=nmax[:, u:u + 1], accum_out=total[:, u:u + 1]).then_inc(s["probs"], 1)
                    t, b = (cur, n // G + 2) if n // G + 2 < B4 else (nxt, n // G + 2 - B4)
                    if n % G == 1 and t.live:
                        act.wait_ge(s["k_ps"], t.unit(b, 0, B4))
                        if t.past_unit(b, 2, B4):
                            act.wait_ge(s["scores"], t.unit(b * G + G - 1, 2 * G))
                        nc.scalar.activation(kT[:, b % 2, :], ps[1][:, 0:CTX], ACT.Copy).then_inc(s["k"], 1)
                    t, b = (cur, n // G + 1) if n // G + 1 < B4 else (nxt, 0)
                    if n % G == 2 and t.live:
                        act.wait_ge(s["v_ps"], t.unit(b, 0, B4))
                        act.wait_ge(s["v_last"], t.unit(b, 0, B4))
                        if t.past_unit(b, 2, B4):
                            act.wait_ge(s["o_ps"], t.unit(b, 2, B4) * 9)
                        nc.scalar.activation(v[:, b % 2], ps[2][:, 0:2 * P].rearrange("p (n d) -> p n d", n=2),
                                             ACT.Copy).then_inc(s["v"], 1)
                    if n % G == 3 and cur.live:
                        b = n // G
                        act.wait_ge(s["last_ps"], cur.unit(b, 0, B4))
                        act.wait_ge(s["pT"], cur.unit(n))
                        if cur.past_unit(b, 2, B4):
                            act.wait_ge(s["o_ps"], cur.unit(b, 2, B4) * 9)
                        nc.scalar.activation(p_last[:, b % 2, :], ps[6][0:G, LAST:LAST + P], ACT.Copy).then_inc(s["last"], 1)
                    if n == 5 and nxt.live:
                        act.wait_ge(s["zT_ps"], nxt.nth())
                        if nxt.past(2):
                            act.wait_ge(s["q_ps"], nxt.before(2))
                        nc.scalar.activation(zT[:, nxt.par, :], ps[0][:, 0:P], ACT.Copy, scale=s0).then_inc(s["zT"], 1)
            over_tiles(act, 4, steps)

        def gate(t, k):
            n = t.n * TOPK + k
            return gates[:, n:n + 1] if t.known else gates[:, DS(n, 1)]

        @block.vector
        def _(dve):
            def steps(at):
                cur, nxt, prev = at(3), at(2), at(4)
                for n in range(N):
                    t, u = (cur, n + AHEAD) if n + AHEAD < N else (nxt, n + AHEAD - N)
                    if t.live:
                        dve.wait_ge(s["scores"], t.unit(u))
                        nc.vector.tensor_reduce(nmax[:, u:u + 1], ps[3 + u % 2][:, 0:CTX], AX.X, ALU.max,
                                                negate=True).then_inc(s["maxed"], 1)
                    t, b = (cur, n // G + 1) if n // G + 1 < B4 else (nxt, 0)
                    if n % G == 2 and t.live:
                        dve.wait_ge(s["v_ps"], t.unit(b, 0, B4))
                        if t.past_unit(b, 2, B4):
                            dve.wait_ge(s["o_ps"], t.unit(b, 2, B4) * 9)
                        nc.vector.tensor_tensor(v_last[:, b % 2, :].rearrange("p (g n) -> p g n", g=G),
                                                ps[2][0:G, LAST:LAST + P].rearrange("p (g n) -> p g n", g=G),
                                                c[0:G, C_ID:C_ID + G].unsqueeze(2).broadcast_to([G, G, 32]),
                                                ALU.mult).then_inc(s["v_last"], 1)
                    if cur.live:
                        dve.wait_ge(s["pT_ps"], cur.unit(n))
                        if n % G == G - 1:
                            dve.wait_ge(s["last_ps"], cur.unit(n // G, 0, B4))
                        if cur.past_unit(n, 2):
                            b2, g2 = (n - 2) // G, (n - 2) % G
                            dve.wait_ge(s["o_ps"], (cur.n * B4 + b2) * 9 + 2 * g2 + 2)
                        nc.vector.tensor_copy(pT[:, n % 2], ps[5 + n % 2][:, 0:2 * P].rearrange(
                            "p (n k) -> p n k", n=2)).then_inc(s["pT"], 1)
                    t, b = (cur, n // G - 1) if n else (prev, B4 - 1)
                    if n % G == 0 and t.live:
                        dve.wait_ge(s["o_ps"], t.unit(b, 0, B4) * 9)
                        if t.past_unit(b, 1, B4):
                            dve.wait_ge(s["oT"], t.unit(b, 1, B4))
                        nc.vector.tensor_tensor(masked[:, :, :], ps[7][:, 0:P].rearrange("p (h i) -> p h i", h=H4),
                                                c[:, C_M4G:C_M4G + H4].unsqueeze(2).broadcast_to([P, H4, LEN]),
                                                ALU.mult).then_inc(s["masked"], 1)
                        dve.wait_ge(s["masked"], t.unit(b, 0, B4))
                        if b == 0 and t.past(2):
                            dve.wait_ge(s["y_ps"], t.before(2))
                        nc.vector.tensor_reduce(oT[:, t.par, b * LEN:(b + 1) * LEN],
                                                masked[:, :, :].rearrange("p h i -> p i h"), AX.X,
                                                ALU.add).then_inc(s["oT"], 1)
                    t, u = (cur, n + AHEAD - 1) if n + AHEAD - 1 < N else (nxt, n + AHEAD - 1 - N)
                    if t.live:
                        dve.wait_ge(s["probs"], t.unit(u))
                        if t.past_unit(u, N):
                            dve.wait_ge(s["normed"], t.unit(u, N))
                        nc.vector.reciprocal(recip[:, u:u + 1], total[:, u:u + 1]).then_inc(s["recip"], 1)
                    t = at(1)
                    if n == 9 and t.live:
                        dve.wait_ge(y_in[t.par], t.nth_of_pair(16))
                        x = m.X[:, t.cols()]
                        nc.vector.scalar_tensor_tensor(x, y[:, t.par, 0:D], gate(t, 0), x, ALU.mult,
                                                       ALU.add).then_inc(added, 1)
                    if n == 10 and t.live:
                        dve.wait_ge(added, t.nth())
                        x = m.X[:, t.cols()]
                        nc.vector.scalar_tensor_tensor(x, y[:, t.par, D:2 * D], gate(t, 1), x, ALU.mult,
                                                       ALU.add).then_inc(joined.x_new, 1)
                    if n == 11 and t.live:
                        joined.dve(dve, t)
                    if n == 3 and nxt.live:
                        dve.wait_ge(joined.pool_step, nxt.nth(joined.steps))
                        if nxt.past(2):
                            dve.wait_ge(s["zT_ps"], nxt.before(2))
                        normed(m, z[:, nxt.par, :], nxt, m.RZ).then_inc(s["z"], 1)
                    if n == 4 and prev.live:
                        dve.wait_ge(s["y_ps"], prev.nth())
                        dve.wait_ge(s["xb"], prev.nth())
                        nc.vector.tensor_tensor(m.X[:, prev.cols()], ps[0][:, 2 * P:3 * P], xb[:, prev.par, :],
                                                ALU.add).then_inc(tail.x_new, 1)
                        tail.dve(dve, prev)
                    if n == 8 and nxt.live:
                        dve.wait_ge(s["q_ps"], nxt.nth())
                        if nxt.past(2):
                            dve.wait_ge(s["scores"], nxt.before(2, N))
                        nc.vector.tensor_tensor(
                            q_all[:, nxt.par],
                            ps[0][:, P:2 * P].rearrange("p (b i) -> p b i", i=LEN).unsqueeze(2).broadcast_to(
                                [P, B4, H4, LEN]),
                            c[:, C_M4G:C_M4G + H4].unsqueeze(1).unsqueeze(3).broadcast_to([P, B4, H4, LEN]),
                            ALU.mult).then_inc(s["q"], 1)
            over_tiles(dve, 4, steps)

        @block.gpsimd
        def _(pool):
            def steps(at):
                cur, nxt, prev = at(3), at(2), at(4)
                for n in range(N):
                    t, u = (cur, n + AHEAD - 1) if n + AHEAD - 1 < N else (nxt, n + AHEAD - 1 - N)
                    if t.live:
                        pool.wait_ge(s["recip"], t.unit(u))
                        p = prob[:, u // G % 2, u % G, :]
                        nc.gpsimd.tensor_tensor(p, p, recip[:, u:u + 1].broadcast_to([P, CTX]),
                                                ALU.mult).then_inc(s["normed"], 1)
                    if n == 2 and prev.live:
                        if prev.past(2):
                            pool.wait_ge(tail.x_new, prev.before(2))
                        nc.gpsimd.tensor_tensor(xb[:, prev.par, :], m.X[:, prev.cols()], m.bX[:, :], ALU.add).then_inc(s["xb"], 1)
                    if n == 5 and prev.live:
                        tail.pool(pool, prev)
                    if n == 12 and at(1).live:
                        joined.pool(pool, at(1))
            over_tiles(pool, 4, steps)


def lay_out_experts(f):
    def first(w):
        return w.transpose(1, 0, 2).reshape(D, E * F)

    def second(w):
        return w.reshape(E, FC, P, D).transpose(2, 0, 1, 3).reshape(P, E * FC * D)

    return {
        "Wg": f["L0_ffn_Wg"], "router_T": f["L1_ffn_router_w"].T,
        "w1_0": first(f["L0_ffn_fc1_w"]), "w2_0": second(f["L0_ffn_fc2_w"]),
        "w1_1": first(f["L1_ffn_w1"]), "w2_1": second(f["L1_ffn_w2"]),
        "ln_wT": f["L0_ffn_ln_w"].T, "ln_bT": f["L0_ffn_ln_b"].T, 
        "b1_T": f["L0_ffn_fc1_b"].reshape(E, FC, P).transpose(2, 0, 1).reshape(P, E * FC),
        "b2": np.tile(f["L0_ffn_fc2_b"].reshape(1, E * D), (P, 1)), "alpha": np.tile(f["L0_ffn_alpha"][None], (P, 1)),
    }


def route(m, name, layer):
    nc, ps, c = m.nc, m.ps, m.const
    s = {n: m.sem(name + "_" + n) for n in (
        "loaded", "z", "zT_ps", "zT", "logit_ps", "logits", "best", "which", "whichf", "hot", "both", "gap", "cum", "rank_ps",
        "ranked", "prod", "slotf", "slot", "dest", "pad", "x", "go", "count_ps", "step", "exp", "mapped", "gaps")}
    SETS = 4
    scattered = [m.sem(name + f"_scattered{n}") for n in range(SETS)]
    ident = c[:, C_ID:C_ID + P]
    tri, ones = c[:, C_TRI:C_TRI + P], c[:, C_ONES:C_ONES + P]
    iota, base = c[:, C_IOTA:C_IOTA + E], c[:, C_BASE:C_BASE + E]
    STAGES = 6
    scaled = layer == 0
    LOADS = 2 if scaled else 1
    with ExitStack() as own, nc.Block() as block:
        sb = lambda n, shape, dt=F32: own.enter_context(nc.sbuf_tensor(name + "_" + n, shape, dt))
        z, zT, x = sb("z", [P, 2, P]), sb("zT", [P, 2, P]), sb("x", [P, SETS, TOPK, WIDTH])
        wg = sb("wg", [P, E])
        logits, best, which = sb("logits", [P, 2, E]), sb("best", [P, 2, E]), sb("which", [P, 2, E], U32)
        whichf = sb("whichf", [P, 2, TOPK])
        hot = sb("hot", [P, TILES * TOPK * E])
        cum, both = sb("cum", [P, 2, E]), sb("both", [P, 2, E])
        rank, prod = sb("rank", [P, 2, E]), sb("prod", [P, 2, TOPK, E])
        slotf, slot = sb("slotf", [P, 2, TOPK]), sb("slot", [P, SETS, TOPK], I32)
        gap, ex, den = sb("gap", [P, TILES]), sb("ex", [P, TILES]), sb("den", [P, TILES])
        pad = sb("pad", [P, PADS, WIDTH])
        tiny = sb("tiny", [P, 1])
        count, jobs, first, end, q = (sb(n, [P, E]) for n in ("count", "jobs", "first", "end", "q"))
        count_i = sb("count_i", [P, E], I32)
        full, before = sb("full", [P, E, TILES]), sb("before", [P, E, E])
        owner, upper, value = (sb(n, [P, JOBS, E]) for n in ("owner", "upper", "value"))
        job = sb("job", [P, JOBS])
        picked, moved = sb("picked", [P, TILES * TOPK, E]), sb("moved", [P, TILES * TOPK])
        alpha, spare = sb("alpha", [P, E]), sb("spare", [P, 1])

        @block.sync
        def _(sp):
            sp.dma_start(wg[:, :], m.a["Wg" if scaled else "router_T"]).then_inc(s["loaded"], 16)
            if scaled:
                sp.dma_start(alpha[:, :], m.a["alpha"]).then_inc(s["loaded"], 16)
            sp.wait_ge(s["pad"], 3)
            for e in range(E):
                sp.dma_start(m.xs_dram[SPARE + e * P:SPARE + (e + 1) * P, :], pad[:, E + e, :]).then_inc(s["mapped"], 16)
            sp.wait_ge(s["gaps"], 1)
            for e in range(E):
                n = sp.value_load(count_i[0:1, e:e + 1], min_val=0, max_val=TOKENS)
                sp.dma_start(m.xs_dram[DS(n + e * REGION, P), :], pad[:, e, :]).then_inc(s["mapped"], 16)
            sp.wait_ge(s["mapped"], 16 * PADS)

        @block.tensor
        def _(pe):
            pe.wait_ge(s["loaded"], 16 * LOADS)

            def work(at):
                t = at(1)
                if t.live:
                    pe.wait_ge(s["z"], t.nth())
                    if t.past(2):
                        pe.wait_ge(s["zT"], t.before(2))
                    nc.tensor.transpose(ps[t.two][:, 0:P], z[:, t.two, :], ident).then_inc(s["zT_ps"], 1)
                t = at(4)
                if t.live:
                    pe.wait_ge(s["both"], t.nth())
                    pe.wait_ge(s["cum"], t.nth())
                    if t.past(2):
                        pe.wait_ge(s["ranked"], t.before(2))
                    out = ps[6 + t.two][:, 0:E]
                    nc.tensor.matmul(out, tri, both[:, t.two, :], start=True, stop=False)
                    last = nc.tensor.matmul(out, ones, cum[:, t.two, :], start=False, stop=True)
                    last.then_inc(s["rank_ps"], 1)
                t = at(2)
                if t.live:
                    pe.wait_ge(s["zT"], t.nth())
                    if t.past(2):
                        pe.wait_ge(s["logits"], t.before(2))
                    nc.tensor.matmul(ps[4 + t.two][:, 0:E], zT[:, t.two, :], wg[:, :],
                                     start=True, stop=True).then_inc(s["logit_ps"], 1)
            over_tiles(pe, STAGES, work, unroll=SETS)
            pe.wait_ge(s["cum"], TILES + 1)
            pe.wait_ge(s["logits"], TILES)
            last = nc.tensor.matmul(ps[4][:, 0:E], ones, cum[:, TILES % 2, :], start=True, stop=True)
            last.then_inc(s["count_ps"], 1)

        @block.scalar
        def _(act):
            def work(at):
                t = at(2)
                if t.live:
                    act.wait_ge(s["logit_ps"], t.nth())
                    if t.past(2):
                        act.wait_ge(s["which"], t.before(2))
                    nc.scalar.activation(logits[:, t.two, :], ps[4 + t.two][:, 0:E], ACT.Copy).then_inc(s["logits"], 1)
                t = at(1)
                if t.live:
                    act.wait_ge(s["zT_ps"], t.nth())
                    if t.past(2):
                        act.wait_ge(s["logit_ps"], t.before(2))
                    nc.scalar.activation(zT[:, t.two, :], ps[t.two][:, 0:P], ACT.Copy).then_inc(s["zT"], 1)
                t = at(5)
                if t.live:
                    act.wait_ge(s["slotf"], t.nth())
                    if t.past(SETS):
                        act.wait_ge(scattered[t.par], t.half * 16 * TOPK)
                    nc.scalar.activation(slot[:, t.par, :], slotf[:, t.two, :], ACT.Copy).then_inc(s["slot"], 1)
                    where = c[:, C_DEST:C_DEST + TOPK * TILES][:, t.cols(TOPK)]
                    nc.scalar.activation(x[:, t.par, :, D], where, ACT.Copy).then_inc(s["dest"], 1)
            over_tiles(act, STAGES, work, unroll=SETS)
            act.wait_ge(s["gap"], TILES)
            nc.scalar.activation(ex[:, :], gap[:, :], ACT.Exp).then_inc(s["exp"], 1)

        @block.vector
        def _(dve):
            nc.vector.memset(spare[:, :], float(SPARE - TOPK * TOKENS))
            nc.vector.memset(m.job_expert[:, :], 0).then_inc(s["pad"], 1)
            dve.wait_ge(s["pad"], 2)
            nc.vector.tensor_copy(pad[:, :, D], c[:, C_PAD:C_PAD + PADS]).then_inc(s["pad"], 1)
            nc.vector.memset(cum[:, 0, :], 0.0).then_inc(s["cum"], 1)

            def work(at):
                t = at(5)
                if t.live:
                    dve.wait_ge(s["rank_ps"], t.nth())
                    nc.vector.tensor_tensor(rank[:, t.two, :], ps[6 + t.two][:, 0:E], base, ALU.add).then_inc(s["ranked"], 1)
                    dve.wait_ge(s["ranked"], t.nth())
                    nc.vector.tensor_tensor(prod[:, t.two], hot[:, t.cols(TOPK * E)].rearrange("p (k e) -> p k e", e=E),
                                            rank[:, t.two, :].unsqueeze(1).broadcast_to([P, TOPK, E]),
                                            ALU.mult).then_inc(s["prod"], 1)
                t = at(3)
                if t.live:
                    dve.wait_ge(s["logits"], t.nth())
                    nc.vector.memset(m.gate[:, 0:1], 0.0)
                    nc.vector.max(best[:, t.two, :], logits[:, t.two, :]).then_inc(s["best"], 1)
                t = at(5)
                if t.live:
                    dve.wait_ge(s["prod"], t.nth())
                    if t.past(2):
                        dve.wait_ge(s["slot"], t.before(2))
                    nc.vector.tensor_reduce(slotf[:, t.two, :], prod[:, t.two], AX.X, ALU.add).then_inc(s["slotf"], 1)
                t = at(3)
                if t.live:
                    dve.wait_ge(s["best"], t.nth())
                    nc.vector.memset(m.gate[:, 1:2], 0.0)
                    nc.vector.max_index(which[:, t.two, :], best[:, t.two, :], logits[:, t.two, :]).then_inc(s["which"], 1)
                t = at(5)
                if t.live:
                    if t.past(SETS):
                        dve.wait_ge(scattered[t.par], t.half * 16 * TOPK)
                    f = m.RN if scaled else m.RZ
                    nc.vector.tensor_scalar(x[:, t.par, :, 0:D], m.X[:, t.cols()].unsqueeze(1).broadcast_to([P, TOPK, D]),
                                            m.MEAN[:, t.cols(1)], f[:, t.cols(1)], ALU.subtract,
                                            ALU.mult).then_inc(s["x"], 1)
                t = at(0)
                if t.live:
                    if t.past(2):
                        dve.wait_ge(s["zT_ps"], t.before(2))
                    normed(m, z[:, t.two, :], t, m.RZ).then_inc(s["z"], 1)
                t = at(3)
                if t.live:
                    dve.wait_ge(s["which"], t.nth())
                    nc.vector.memset(m.gate[:, 2:3], 0.0)
                    nc.vector.tensor_copy(whichf[:, t.two, :], which[:, t.two, 0:TOPK]).then_inc(s["whichf"], 1)
                    nc.vector.tensor_tensor(gap[:, t.cols(1)], best[:, t.two, 1:2], best[:, t.two, 0:1],
                                            ALU.subtract).then_inc(s["gap"], 1)
                    dve.wait_ge(s["whichf"], t.nth())
                    nc.vector.tensor_tensor(hot[:, t.cols(TOPK * E)].rearrange("p (k e) -> p k e", e=E),
                                            iota.unsqueeze(1).broadcast_to([P, TOPK, E]),
                                            whichf[:, t.two, :].unsqueeze(2).broadcast_to([P, TOPK, E]),
                                            ALU.is_equal).then_inc(s["hot"], 1)
                    dve.wait_ge(s["hot"], t.nth())
                    if t.past(2):
                        dve.wait_ge(s["rank_ps"], t.before(2))
                    h = hot[:, t.cols(TOPK * E)]
                    nc.vector.tensor_tensor(both[:, t.two, :], h[:, 0:E], h[:, E:2 * E], ALU.add).then_inc(s["both"], 1)
                    dve.wait_ge(s["both"], t.nth())
                    if t.past():
                        dve.wait_ge(s["rank_ps"], t.before())
                    nc.vector.tensor_tensor(cum[:, 1 - t.two, :], cum[:, t.two, :], both[:, t.two, :],
                                            ALU.add).then_inc(s["cum"], 1)
            over_tiles(dve, STAGES, work, unroll=SETS)

            dve.wait_ge(s["exp"], 1)
            nc.vector.tensor_scalar(den[:, :], ex[:, :], 1.0, None, ALU.add).then_inc(s["step"], 1)
            dve.wait_ge(s["step"], 1)
            nc.vector.reciprocal(m.gates[:, :, 0], den[:, :]).then_inc(s["step"], 1)
            dve.wait_ge(s["step"], 2)
            nc.vector.tensor_tensor(m.gates[:, :, 1], ex[:, :], m.gates[:, :, 0], ALU.mult).then_inc(s["step"], 1)

            dve.wait_ge(s["count_ps"], 1)
            by_job = lambda ap: ap.unsqueeze(1).broadcast_to([P, JOBS, E])
            by_expert = lambda ap: ap.unsqueeze(2).broadcast_to([P, E, E])
            row = c[:, C_JOB:C_JOB + JOBS].unsqueeze(2).broadcast_to([P, JOBS, E])
            hots = hot[:, :].rearrange("p (n e) -> p n e", e=E)
            tt, ts, red = nc.vector.tensor_tensor, nc.vector.tensor_scalar, nc.vector.tensor_reduce
            by_token = lambda ap: ap.unsqueeze(1).broadcast_to([P, TILES * TOPK, E])
            stages = [
                lambda: ts(count[:, :], ps[4][:, 0:E], 1.0, None, ALU.mult),
                lambda: ts(count_i[:, :], count[:, :], 1.0, None, ALU.mult),
                lambda: tt(full[:, :, :], count[:, :].unsqueeze(2).broadcast_to([P, E, TILES]),
                           c[:, C_JOB:C_JOB + TILES].unsqueeze(1).broadcast_to([P, E, TILES]), ALU.is_gt),
                lambda: red(jobs[:, :], full[:, :, :], AX.X, ALU.add),
                lambda: tt(before[:, :, :], by_expert(iota), iota.unsqueeze(1).broadcast_to([P, E, E]), ALU.is_gt),
                lambda: tt(before[:, :, :], before[:, :, :], jobs[:, :].unsqueeze(1).broadcast_to([P, E, E]), ALU.mult),
                lambda: red(first[:, :], before[:, :, :], AX.X, ALU.add),
                lambda: ts(first[:, :], first[:, :], float(P), None, ALU.mult),
                lambda: nc.vector.scalar_tensor_tensor(end[:, :], jobs[:, :], c[:, C_JOB + 1:C_JOB + 2], first[:, :],
                                                       ALU.mult, ALU.add),
                lambda: tt(q[:, :], base, first[:, :], ALU.subtract),
                lambda: tt(owner[:, :, :], row, by_job(first[:, :]), ALU.is_ge),
                lambda: tt(upper[:, :, :], row, by_job(end[:, :]), ALU.is_lt),
                lambda: tt(owner[:, :, :], owner[:, :, :], upper[:, :, :], ALU.mult),
                lambda: tt(upper[:, :, :], owner[:, :, :], by_job(iota), ALU.mult),
                lambda: red(job[:, :], upper[:, :, :], AX.X, ALU.add),
                lambda: ts(m.job_expert[:, AROUND:AROUND + JOBS], job[:, :], float(F), None, ALU.mult),
                lambda: ts(q[:, :], q[:, :], float(SPARE - TOPK * TOKENS), None, ALU.subtract),
                lambda: tt(value[:, :, :], owner[:, :, :], by_job(q[:, :]), ALU.mult),
                lambda: red(job[:, :], value[:, :, :], AX.X, ALU.add),
                lambda: nc.vector.scalar_tensor_tensor(m.job_row[:, :], job[:, :], spare[:, :], c[:, C_JOB:C_JOB + JOBS],
                                                       ALU.add, ALU.add),
            ]
            if scaled:
                gates = m.gates[:, :, :].rearrange("p t k -> p (t k)")
                stages += [
                    lambda: tt(picked[:, :, :], hots, by_token(alpha[:, :]), ALU.mult),
                    lambda: red(moved[:, :], picked[:, :, :], AX.X, ALU.add),
                    lambda: tt(gates, gates, moved[:, :], ALU.mult),
                ]
            for n, stage in enumerate(stages):
                dve.wait_ge(s["step"], 3 + n)
                stage().then_inc(s["step"], 1)
                if n == 1:
                    dve.wait_ge(s["step"], 5)
                    nc.vector.memset(m.gate[:, 3:4], 0.0).then_inc(s["gaps"], 1)

        @block.gpsimd
        def _(pool):
            nc.gpsimd.memset(pad[:, :, :], 0.0).then_inc(s["pad"], 1)

            def work(at):
                t = at(6)
                if t.live:
                    pool.wait_ge(s["slot"], t.nth())
                    pool.wait_ge(s["x"], t.nth())
                    pool.wait_ge(s["dest"], t.nth())
                    if t.past():
                        pool.wait_ge(s["go"], t.before())
                    nc.gpsimd.tensor_tensor(tiny[:, :], c[:, 0:1], c[:, 0:1], ALU.mult).then_inc(s["go"], 1)
                    for k in range(TOPK):
                        nc.gpsimd.indirect_dma_start(
                            m.xs_dram[:, :], bass.IndirectOffsetOnAxis(ap=slot[:, t.par, k:k + 1], axis=0),
                            x[:, t.par, k, :], None).then_inc(scattered[t.par], 16)
            over_tiles(pool, STAGES, work, unroll=SETS)
            for sem in scattered:
                pool.wait_ge(sem, TILES // SETS * 16 * TOPK)


def experts(m, name, layer):
    nc, ps = m.nc, m.ps
    s = {n: m.sem(name + "_" + n) for n in ("xT_ps", "xT", "w", "h_ps", "h", "aT", "y_ps", "y", "dest", "go")}
    SETS = 8
    FIRST, SECOND, STAGES = 1, 4, 6
    HALVES = JOBS // 2
    x_in = [m.sem(name + f"_x_in{n}") for n in range(SETS)]
    scattered = [m.sem(name + f"_scattered{n}") for n in range(SETS)]
    gelu = ACT.Gelu_apprx_tanh if layer == 0 else ACT.Gelu
    ident = m.const[:, C_ID:C_ID + P]
    biased = layer == 0
    with ExitStack() as own, nc.Block() as block:
        sb = lambda n, shape: own.enter_context(nc.sbuf_tensor(name + "_" + n, shape, F32))
        x, xT, y = sb("x", [P, SETS, WIDTH]), sb("xT", [P, 2, P]), sb("y", [P, SETS, D])
        dest = own.enter_context(nc.sbuf_tensor(name + "_dest", [P, SETS], I32))
        tiny = sb("tiny", [P, 1])
        w, h, aT = (sb(n, [P, 2, F]) for n in ("w", "h", "aT"))

        def experts_of(engine, half, first):
            n = SETS * half - SECOND + AROUND
            window = SETS + SECOND - first
            ap = m.job_expert[0:1, n:n + window] if isinstance(half, int) else m.job_expert[0:1, DS(n, window)]
            return nc.values_load_multi_w_load_instructions(
                ap, engines=[engine], min_val=0, max_val=(E - 1) * F, skip_runtime_bounds_check_because=
                "route() sums one expert's first column, or none, into each entry")[1]

        @block.sync
        def _(sp):
            def work(at):
                t = at(0)
                if t.live:
                    if t.past(SETS):
                        sp.wait_ge(s["xT_ps"], t.before(SETS))
                        sp.wait_ge(s["dest"], t.before(SETS))
                    row = sp.value_load(m.job_row[0:1, t.cols(1)], min_val=0, max_val=SPARE + (E - 1) * P)
                    sp.dma_start(x[:, t.par, :], m.xs_dram[DS(row, P), :]).then_inc(x_in[t.par], 16)
            over_tiles(sp, STAGES, work, HALVES, SETS)

        @block.gpsimd
        def _(pool):
            def work(at):
                t = at(6)
                if t.live:
                    pool.wait_ge(s["y"], t.nth())
                    pool.wait_ge(s["dest"], t.nth())
                    if t.past():
                        pool.wait_ge(s["go"], t.before())
                    nc.gpsimd.tensor_tensor(tiny[:, :], m.const[:, 0:1], m.const[:, 0:1], ALU.mult).then_inc(s["go"], 1)
                    nc.gpsimd.indirect_dma_start(
                        m.ys_dram[:, :], bass.IndirectOffsetOnAxis(ap=dest[:, t.par:t.par + 1], axis=0),
                        y[:, t.par, :], None).then_inc(scattered[t.par], 16)
            over_tiles(pool, STAGES, work, HALVES, SETS)
            for sem in scattered:
                pool.wait_ge(sem, 16 * JOBS // SETS)

        @block.tensor
        def _(pe):
            held = []

            def work(at):
                p = at(0).par
                if p == 0:
                    held[:] = experts_of(mybir.EngineType.PE, at(0).half, SECOND)
                t = at(SECOND)
                if t.live:
                    pe.wait_ge(s["aT"], t.nth())
                    if t.past(2):
                        pe.wait_ge(s["y"], t.before(2))
                    for f in range(FC):
                        last = nc.tensor.matmul(ps[6 + t.two][:, 0:D], aT[:, t.two, f * P:(f + 1) * P],
                                                m.w2[:, DS(held[p] + f * D, D)], start=(f == 0), stop=(f == FC - 1))
                    last.then_inc(s["y_ps"], 1)
                t = at(1)
                if t.live:
                    pe.wait_ge(x_in[t.par], t.nth_of_pair(16))
                    if t.past(2):
                        pe.wait_ge(s["xT"], t.before(2))
                    nc.tensor.transpose(ps[t.two][:, 0:P], x[:, t.par, 0:D], ident).then_inc(s["xT_ps"], 1)
                t = at(2)
                if t.live:
                    pe.wait_ge(s["xT"], t.nth())
                    pe.wait_ge(s["w"], t.nth())
                    if t.past(2):
                        pe.wait_ge(s["h" if biased else "aT"], t.before(2))
                    for f in range(FC):
                        last = nc.tensor.matmul(ps[2 + t.two][:, f * P:(f + 1) * P], w[:, t.two, f * P:(f + 1) * P],
                                                xT[:, t.two, :], start=True, stop=True)
                    last.then_inc(s["h_ps"], 1)
            over_tiles(pe, STAGES, work, HALVES, SETS)

        @block.scalar
        def _(act):
            def work(at):
                t = at(3)
                if t.live:
                    act.wait_ge(s["h" if biased else "h_ps"], t.nth())
                    if t.past(2):
                        act.wait_ge(s["y_ps"], t.before(2))
                    nc.scalar.activation(aT[:, t.two, :], h[:, t.two, :] if biased else ps[2 + t.two][:, :],
                                         gelu).then_inc(s["aT"], 1)
                t = at(1)
                if t.live:
                    act.wait_ge(s["xT_ps"], t.nth())
                    if t.past(2):
                        act.wait_ge(s["h_ps"], t.before(2))
                    nc.scalar.activation(xT[:, t.two, :], ps[t.two][:, 0:P], ACT.Copy).then_inc(s["xT"], 1)
                    act.wait_ge(x_in[t.par], t.nth_of_pair(16))
                    if t.past(SETS):
                        act.wait_ge(scattered[t.par], t.half * 16)
                    nc.scalar.activation(dest[:, t.par:t.par + 1], x[:, t.par, D:D + 1], ACT.Copy).then_inc(s["dest"], 1)
            over_tiles(act, STAGES, work, HALVES, SETS)

        @block.vector
        def _(dve):
            held = []

            def work(at):
                p = at(0).par
                if p == 0:
                    held[:] = experts_of(mybir.EngineType.DVE, at(0).half, FIRST)
                t = at(SECOND)
                if t.live:
                    dve.wait_ge(s["y_ps"], t.nth())
                    if t.past(SETS):
                        dve.wait_ge(scattered[t.par], t.half * 16)
                    if biased:
                        nc.vector.tensor_tensor(y[:, t.par, :], ps[6 + t.two][:, 0:D], m.bias[:, DS(held[p], D)],
                                                ALU.add).then_inc(s["y"], 1)
                    else:
                        nc.vector.tensor_scalar(y[:, t.par, :], ps[6 + t.two][:, 0:D], 1.0, None,
                                                ALU.mult).then_inc(s["y"], 1)
                t = at(FIRST)
                if t.live:
                    if t.past(2):
                        dve.wait_ge(s["h_ps"], t.before(2))
                    nc.vector.tensor_scalar(w[:, t.two, :], m.w1[:, DS(held[p + SECOND - FIRST], F)], 1.0, None,
                                            ALU.mult).then_inc(s["w"], 1)
                t = at(2)
                if t.live and biased:
                    dve.wait_ge(s["h_ps"], t.nth())
                    if t.past(2):
                        dve.wait_ge(s["aT"], t.before(2))
                    by_chunk = lambda ap: ap.rearrange("p (f n) -> p f n", f=FC)
                    nc.vector.tensor_tensor(by_chunk(h[:, t.two, :]), by_chunk(ps[2 + t.two][:, :]),
                                            m.bias[:, DS(held[p + SECOND - 2] + D, FC)].unsqueeze(2).broadcast_to(
                                                [P, FC, P]), ALU.add).then_inc(s["h"], 1)
            over_tiles(dve, STAGES, work, HALVES, SETS)


def combine(m, name):
    nc = m.nc
    GROUP = 4
    added = m.sem(name + "_added")
    y_in = [m.sem(name + f"_y_in{n}") for n in range(TILES // GROUP)]
    x_new, stored = m.sem(name + "_x_new"), m.sem(name + "_stored")
    with ExitStack() as own, nc.Block() as block:
        y = own.enter_context(nc.sbuf_tensor(name + "_y", [P, TILES, TOPK * D], F32))
        gates = m.gates[:, :, :].rearrange("p t k -> p (t k)")
        results = m.ys_dram[0:TOPK * TOKENS, :].rearrange("(t p k) d -> p t (k d)", p=P, k=TOPK)
        out = m.out_dram.rearrange("t p d -> p t d")

        @block.sync
        def _(sp):
            for n in range(TILES // GROUP):
                tiles = slice(n * GROUP, (n + 1) * GROUP)
                sp.dma_start(y[:, tiles, :], results[:, tiles, :]).then_inc(y_in[n], 16)

        @block.scalar
        def _(act):
            for n in range(TILES // GROUP):
                act.wait_ge(x_new, (n + 1) * GROUP)
                act.dma_start(out[:, n * GROUP:(n + 1) * GROUP, :], m.X[:, n * GROUP * D:(n + 1) * GROUP * D].rearrange(
                    "p (t d) -> p t d", d=D)).then_inc(stored, 16)
            act.wait_ge(stored, 16 * TILES // GROUP)

        @block.vector
        def _(dve):
            for n in range(TILES // GROUP):
                dve.wait_ge(y_in[n], 16)
                tiles = range(n * GROUP, (n + 1) * GROUP)
                for k, sem in ((0, added), (1, x_new)):
                    for t in tiles:
                        if k:
                            dve.wait_ge(added, t + 1)
                        x = m.X[:, t * D:(t + 1) * D]
                        g = t * TOPK + k
                        nc.vector.scalar_tensor_tensor(x, y[:, t, k * D:(k + 1) * D], gates[:, g:g + 1], x, ALU.mult,
                                                       ALU.add).then_inc(sem, 1)


def experts_one(m):
    route(m, "m0_route", 0)
    m.end_pass()
    experts(m, "m0_experts", 0)


def experts_two(m):
    route(m, "m1_route", 1)
    m.end_pass()
    experts(m, "m1_experts", 1)
    m.end_pass()
    combine(m, "m1_combine")


def build(nc, a, out, upto=99):
    m = Chip()
    m.nc = nc
    with ExitStack() as ctx:
        in_use = []

        def sem(name):
            in_use.append(nc.alloc_semaphore(name=name))
            return in_use[-1]

        def end_pass():
            nc.clear_and_free_semaphores(in_use)
            in_use.clear()
            nc.all_engine_barrier()

        m.sem, m.end_pass = sem, end_pass
        sb = lambda name, shape, dt=F32: ctx.enter_context(nc.sbuf_tensor("sb_" + name, shape, dt))
        m.ps = [ctx.enter_context(nc.psum_tensor(f"bank{n}", [P, 512], F32)) for n in range(8)]
        m.X = sb("X", [P, TILES * D])
        m.MEAN, m.RZ, m.RN = sb("MEAN", [P, TILES]), sb("RZ", [P, TILES]), sb("RN", [P, TILES])
        m.const = sb("const", [P, C_ALL])
        m.bnst, m.mv, m.rstd = sb("bnst", [P, 2, 6]), sb("mv", [P, 2, 2]), sb("rstd", [P, 4])
        m.mv_all, m.factor = sb("mv_all", [P, 2 * TILES]), sb("factor", [P, TILES])
        m.gate = sb("gate", [P, 4])
        m.M0, m.N0, m.c0 = sb("M0", [P, D]), sb("N0", [P, D]), sb("c0", [P, 1])
        m.b0, m.bA, m.bX = sb("b0", [P, D]), sb("bA", [P, D]), sb("bX", [P, D])
        m.ptab = sb("ptab", [P, H, 1 + LEN])
        m.QV = sb("QV", [P, TILES * P])
        m.gates = sb("gates", [P, TILES, TOPK])
        m.b1, m.ln_w, m.ln_b = sb("b1", [P, E * FC]), sb("ln_w", [P, E]), sb("ln_b", [P, E])
        m.job_row, m.job_expert = sb("job_row", [P, JOBS], I32), sb("job_expert", [P, AROUND + JOBS + AROUND], I32)
        m.w1, m.w2 = sb("w1", [P, E * F]), sb("w2", [P, E * F])
        m.bias = sb("bias", [P, E * F])
        m.a = a
        m.bqu = sb("bqu", [P, 2])
        m.cols, m.rows = sb("cols", [P, len(COLS)]), sb("rows", [1, 3 * D])
        m.colidx = {n: k for k, n in enumerate(COLS)}
        m.c_bq0 = m.colidx["bq0"]
        m.w = {n: sb("w_" + n, [P, w]) for n, w in WEIGHTS.items()}
        m.setup_loads = [(m.const[:, :], a["const"]), (m.cols[:, :], a["cols"]), (m.rows[:, :], a["rows"])]
        m.setup_loads += [(m.w[n][:, :], a[n]) for n in WEIGHTS]
        m.x_dram = a["x"].rearrange("(t b) i d -> t (b i) d", b=B4)
        m.ctxT_dram, m.ctxN_dram = a["ctxT"], a["ctxN"]
        m.bd_dram = nc.dram_tensor("bd_scores", [SEQS, LEN, H * LEN], F32).ap()
        m.xs_dram = nc.dram_tensor("expert_inputs", [SPARE + E * P, WIDTH], F32).ap()
        m.ys_dram = nc.dram_tensor("expert_outputs", [TOPK * TOKENS + PADS * P, D], F32).ap()
        m.out_dram = out.rearrange("(t b) i d -> t (b i) d", b=B4)
        passes = [setup_pass, cross_one_head, relative_scores, relative_attention,
                  experts_one, cross_many_heads, causal_attention, experts_two]
        for f in passes[:upto]:
            f(m)
            m.end_pass()


COLS = ("bq0", "bv0", "bv_a", "bq_a", "bk_a", "u", "v", "gamma", "beta", "norm_w")
WEIGHTS = {"Wq0": 128, "Wk0": 128, "Wv0": 128, "Wo0T": 128, "Wq_a": 128, "Wk_a": 128, "Wv_a": 128,
           "Wpos": 128, "Wf": 128, "WqT_x": 128, "WkT_x": 128, "WvT_x": 128, "WoT_x": 128,
           "w_q": 128, "w_k": 128, "w_v": 128, "w_o": 128}


def lay_out(i):
    f = {k: np.asarray(v) for k, v in i.items()}
    ctx = f["ctx_1024"]
    order = np.concatenate([np.arange(c, CTX, 3) for c in range(3)])
    padded = np.concatenate([ctx, np.zeros((SEQS, 1, D), np.float32)], 1)
    a = {
        "x": f["x"],
        "ctxT": ctx[:, order].transpose(2, 0, 1).reshape(D, SEQS * CTX),
        "ctxN": padded.reshape(TILES, B4, KC, 3, D).transpose(0, 2, 1, 3, 4).reshape(TILES, KC, B4 * 3 * D),
        "const": shape_constants(),
        "cols": np.stack([f["L0_xattn_bq"], f["L0_xattn_bv"], f["L0_attn_bv"], f["L0_attn_bq"], f["L0_attn_bk"],
                          f["L0_attn_u"].reshape(-1), f["L0_attn_v"].reshape(-1), f["L0_attn_gamma"],
                          f["L0_attn_beta"], f["L1_attn_norm_w"]], 1),
        "rows": np.concatenate([f["L0_xattn_bo"], f["L0_attn_bf"], f["L1_xattn_bo"]])[None],
        "Wq0": f["L0_xattn_Wq"], "Wk0": f["L0_xattn_Wk"], "Wv0": f["L0_xattn_Wv"], "Wo0T": f["L0_xattn_Wo"].T,
        "Wq_a": f["L0_attn_Wq"], "Wk_a": f["L0_attn_Wk"], "Wv_a": f["L0_attn_Wv"], "Wpos": f["L0_attn_Wpos"],
        "Wf": f["L0_attn_Wf"],
        "WqT_x": f["L1_xattn_Wq"].T, "WkT_x": f["L1_xattn_Wk"].T, "WvT_x": f["L1_xattn_Wv"].T,
        "WoT_x": f["L1_xattn_Wo"].T,
        "w_q": f["L1_attn_w_q"], "w_k": np.tile(f["L1_attn_w_k"], (1, G)),
        "w_v": np.tile(f["L1_attn_w_v"], (1, G)), "w_o": f["L1_attn_w_o"],
    }
    a.update(lay_out_experts(f))
    return {k: np.ascontiguousarray(v) for k, v in a.items()}


def kernel(**inputs):
    import concourse.bacc as bacc
    from concourse.bass_utils import run_bass_kernel_spmd

    arrays = lay_out(inputs)
    nc = bacc.Bacc("TRN2", target_bir_lowering=False, num_devices=1)
    views = {k: nc.dram_tensor(k, v.shape, mybir.dt.from_np(v.dtype), kind="ExternalInput").ap()
             for k, v in arrays.items()}
    out = nc.dram_tensor("latents_out", (SEQS, LEN, D), F32, kind="ExternalOutput").ap()
    build(nc, views, out)
    return run_bass_kernel_spmd(nc, [arrays], core_ids=[0]).results[0]["latents_out"]
```
